# Optimizing a Trainium2 kernel written in Bass

```python
import numpy as np
import jax
import jax.numpy as jnp

def _softmax(x, axis=-1):
    return jax.nn.softmax(x, axis=axis)

def _gelu(x):
    return jax.nn.gelu(x, approximate=True)

def _silu(x):
    return jax.nn.silu(x)

def _sigmoid(x):
    return jax.nn.sigmoid(x)

def _layernorm(x, axis=-1, eps=1e-05):
    m = jnp.mean(x, axis=axis, keepdims=True)
    v = jnp.var(x, axis=axis, keepdims=True)
    return (x - m) / jnp.sqrt(v + eps)

def _scatter_add(tgt, idx, src, axis=0):
    return tgt.at[idx].add(src)

def _segment_sum(src, seg, n):
    return jax.ops.segment_sum(src, seg, n)
kernel_name = 'mk_sandwich_d1_jaxref_r8_e15035'

def setup_inputs(seed: int=0):
    np.random.seed(seed)
    _w = jnp.asarray

    def _L0_attn_setup():
        import jax, jax.numpy as jnp
        import numpy as np
        B, T, D = (4, 256, 128)
        NUM_HEADS, HEAD_DIM = (16, 64)
        ROPE_THETA = 10000.0

        def precompute_freqs_cis(dim, max_seq_len, theta=10000.0):
            inv_freq = 1.0 / theta ** (jnp.arange(0, dim, 2, dtype=jnp.float32) / dim)
            freqs = jnp.outer(jnp.arange(max_seq_len, dtype=jnp.float32), inv_freq)
            return (jnp.cos(freqs), jnp.sin(freqs))

        def apply_rotary_emb(x, cos, sin):
            c = cos[None, None, :, :]
            s = sin[None, None, :, :]
            x1, x2 = jnp.split(x.astype(jnp.float32), 2, axis=-1)
            return jnp.concatenate([x1 * c - x2 * s, x1 * s + x2 * c], axis=-1).astype(x.dtype)
        key = jax.random.key(seed)
        ks = jax.random.split(key, 5)
        scale = 1.0 / np.sqrt(D)
        return {'x': jax.random.normal(ks[0], (B, T, D), dtype=jnp.float32), 'wq': jax.random.normal(ks[1], (NUM_HEADS * HEAD_DIM, D), dtype=jnp.float32) * scale, 'wk': jax.random.normal(ks[2], (NUM_HEADS * HEAD_DIM, D), dtype=jnp.float32) * scale, 'wv': jax.random.normal(ks[3], (NUM_HEADS * HEAD_DIM, D), dtype=jnp.float32) * scale, 'wo': jax.random.normal(ks[4], (D, NUM_HEADS * HEAD_DIM), dtype=jnp.float32) * scale}
    _L0_attn_in = _L0_attn_setup()

    def _L0_ffn_setup():
        import jax, jax.numpy as jnp
        import numpy as np
        B, S, D = (2, 256, 128)
        E, K, H = (8, 4, 128)
        SH = 2 * H

        def _silu(x):
            return x * jax.nn.sigmoid(x)

        def _swiglu(x, w1, b1, w2, b2):
            return _silu(x @ w1 + b1) * (x @ w2 + b2)

        def _moe(x, gate_w, exp_w1, exp_w3, exp_w2, sh_w1, sh_w3, sh_w2):
            b, s, d = x.shape
            t = b * s
            xt = x.reshape(t, d)
            scores = jax.nn.softmax(xt @ gate_w.T, axis=-1)
            topv, topi = jax.lax.top_k(scores, K)
            topv = topv / jnp.sum(topv, axis=-1, keepdims=True)
            combine = jnp.zeros((t, E), xt.dtype).at[jnp.arange(t)[:, None], topi].set(topv)
            g = _silu(jnp.einsum('td,edh->eth', xt, exp_w1))
            u = jnp.einsum('td,edh->eth', xt, exp_w3)
            yexp = jnp.einsum('eth,ehd->etd', g * u, exp_w2)
            routed = jnp.einsum('te,etd->td', combine, yexp)
            shared = _silu(xt @ sh_w1) * (xt @ sh_w3) @ sh_w2
            return (routed + shared).reshape(b, s, d)
        key = jax.random.key(seed)
        ks = jax.random.split(key, 24)
        f = lambda k, shape: jax.random.normal(k, shape, dtype=jnp.float32) * 0.02
        return {'x': jax.random.normal(ks[0], (B, S, D), dtype=jnp.float32), 'lin0_w': f(ks[1], (D, D)), 'lin0_b': f(ks[2], (D,)), 'swi1_w1': f(ks[3], (D, D)), 'swi1_b1': f(ks[4], (D,)), 'swi1_w2': f(ks[5], (D, D)), 'swi1_b2': f(ks[6], (D,)), 'gate_w': f(ks[7], (E, D)), 'exp_w1': f(ks[8], (E, D, H)), 'exp_w3': f(ks[9], (E, D, H)), 'exp_w2': f(ks[10], (E, H, D)), 'sh_w1': f(ks[11], (D, SH)), 'sh_w3': f(ks[12], (D, SH)), 'sh_w2': f(ks[13], (SH, D)), 'lin1_w': f(ks[14], (D, D)), 'lin1_b': f(ks[15], (D,)), 'swi2_w1': f(ks[16], (D, D)), 'swi2_b1': f(ks[17], (D,)), 'swi2_w2': f(ks[18], (D, D)), 'swi2_b2': f(ks[19], (D,))}
    _L0_ffn_in = _L0_ffn_setup()
    _d = {'L0_attn_x': _L0_attn_in['x'], 'L0_attn_wq': _L0_attn_in['wq'], 'L0_attn_wk': _L0_attn_in['wk'], 'L0_attn_wv': _L0_attn_in['wv'], 'L0_attn_wo': _L0_attn_in['wo'], 'L0_ffn_lin0_w': _L0_ffn_in['lin0_w'], 'L0_ffn_lin0_b': _L0_ffn_in['lin0_b'], 'L0_ffn_swi1_w1': _L0_ffn_in['swi1_w1'], 'L0_ffn_swi1_b1': _L0_ffn_in['swi1_b1'], 'L0_ffn_swi1_w2': _L0_ffn_in['swi1_w2'], 'L0_ffn_swi1_b2': _L0_ffn_in['swi1_b2'], 'L0_ffn_gate_w': _L0_ffn_in['gate_w'], 'L0_ffn_exp_w1': _L0_ffn_in['exp_w1'], 'L0_ffn_exp_w3': _L0_ffn_in['exp_w3'], 'L0_ffn_exp_w2': _L0_ffn_in['exp_w2'], 'L0_ffn_sh_w1': _L0_ffn_in['sh_w1'], 'L0_ffn_sh_w3': _L0_ffn_in['sh_w3'], 'L0_ffn_sh_w2': _L0_ffn_in['sh_w2'], 'L0_ffn_lin1_w': _L0_ffn_in['lin1_w'], 'L0_ffn_lin1_b': _L0_ffn_in['lin1_b'], 'L0_ffn_swi2_w1': _L0_ffn_in['swi2_w1'], 'L0_ffn_swi2_b1': _L0_ffn_in['swi2_b1'], 'L0_ffn_swi2_w2': _L0_ffn_in['swi2_w2'], 'L0_ffn_swi2_b2': _L0_ffn_in['swi2_b2']}
    _x0 = _d['L0_attn_x']
    _d['L0_attn_x'] = jax.random.normal(jax.random.fold_in(jax.random.key(seed), 1), (4, 1024, 128), dtype=_x0.dtype)
    del _x0
    return _d

def reference(L0_attn_x, L0_attn_wq, L0_attn_wk, L0_attn_wv, L0_attn_wo, L0_ffn_lin0_w, L0_ffn_lin0_b, L0_ffn_swi1_w1, L0_ffn_swi1_b1, L0_ffn_swi1_w2, L0_ffn_swi1_b2, L0_ffn_gate_w, L0_ffn_exp_w1, L0_ffn_exp_w3, L0_ffn_exp_w2, L0_ffn_sh_w1, L0_ffn_sh_w3, L0_ffn_sh_w2, L0_ffn_lin1_w, L0_ffn_lin1_b, L0_ffn_swi2_w1, L0_ffn_swi2_b1, L0_ffn_swi2_w2, L0_ffn_swi2_b2):

    def _L0_attn_ref(x, wq, wk, wv, wo):
        import jax, jax.numpy as jnp
        import numpy as np
        B, T, D = (4, 256, 128)
        NUM_HEADS, HEAD_DIM = (16, 64)
        ROPE_THETA = 10000.0

        def precompute_freqs_cis(dim, max_seq_len, theta=10000.0):
            inv_freq = 1.0 / theta ** (jnp.arange(0, dim, 2, dtype=jnp.float32) / dim)
            freqs = jnp.outer(jnp.arange(max_seq_len, dtype=jnp.float32), inv_freq)
            return (jnp.cos(freqs), jnp.sin(freqs))

        def apply_rotary_emb(x, cos, sin):
            c = cos[None, None, :, :]
            s = sin[None, None, :, :]
            x1, x2 = jnp.split(x.astype(jnp.float32), 2, axis=-1)
            return jnp.concatenate([x1 * c - x2 * s, x1 * s + x2 * c], axis=-1).astype(x.dtype)
        batch, seq_len, _ = x.shape
        q = jnp.einsum('btd,od->bto', x, wq, preferred_element_type=jnp.float32)
        k = jnp.einsum('btd,od->bto', x, wk, preferred_element_type=jnp.float32)
        v = jnp.einsum('btd,od->bto', x, wv, preferred_element_type=jnp.float32)
        q = q.reshape(batch, seq_len, NUM_HEADS, HEAD_DIM).transpose(0, 2, 1, 3)
        k = k.reshape(batch, seq_len, NUM_HEADS, HEAD_DIM).transpose(0, 2, 1, 3)
        v = v.reshape(batch, seq_len, NUM_HEADS, HEAD_DIM).transpose(0, 2, 1, 3)
        cos, sin = precompute_freqs_cis(HEAD_DIM, seq_len, ROPE_THETA)
        q = apply_rotary_emb(q, cos, sin)
        k = apply_rotary_emb(k, cos, sin)
        scale = jnp.asarray(HEAD_DIM ** (-0.5), dtype=jnp.float32)
        scores = jnp.einsum('bhid,bhjd->bhij', q, k, preferred_element_type=jnp.float32) * scale
        causal = jnp.tril(jnp.ones((seq_len, seq_len), dtype=bool))
        scores = jnp.where(causal, scores, -jnp.inf)
        probs = jax.nn.softmax(scores, axis=-1).astype(x.dtype)
        out = jnp.einsum('bhij,bhjd->bhid', probs, v, preferred_element_type=jnp.float32).astype(x.dtype)
        out = out.transpose(0, 2, 1, 3).reshape(batch, seq_len, NUM_HEADS * HEAD_DIM)
        out = jnp.einsum('btd,od->bto', out, wo, preferred_element_type=jnp.float32)
        return out

    def _L0_ffn_ref(x, lin0_w, lin0_b, swi1_w1, swi1_b1, swi1_w2, swi1_b2, gate_w, exp_w1, exp_w3, exp_w2, sh_w1, sh_w3, sh_w2, lin1_w, lin1_b, swi2_w1, swi2_b1, swi2_w2, swi2_b2):
        import jax, jax.numpy as jnp
        import numpy as np
        B, S, D = (2, 256, 128)
        E, K, H = (8, 4, 128)
        SH = 2 * H

        def _silu(x):
            return x * jax.nn.sigmoid(x)

        def _swiglu(x, w1, b1, w2, b2):
            return _silu(x @ w1 + b1) * (x @ w2 + b2)

        def _moe(x, gate_w, exp_w1, exp_w3, exp_w2, sh_w1, sh_w3, sh_w2):
            b, s, d = x.shape
            t = b * s
            xt = x.reshape(t, d)
            scores = jax.nn.softmax(xt @ gate_w.T, axis=-1)
            topv, topi = jax.lax.top_k(scores, K)
            topv = topv / jnp.sum(topv, axis=-1, keepdims=True)
            combine = jnp.zeros((t, E), xt.dtype).at[jnp.arange(t)[:, None], topi].set(topv)
            g = _silu(jnp.einsum('td,edh->eth', xt, exp_w1))
            u = jnp.einsum('td,edh->eth', xt, exp_w3)
            yexp = jnp.einsum('eth,ehd->etd', g * u, exp_w2)
            routed = jnp.einsum('te,etd->td', combine, yexp)
            shared = _silu(xt @ sh_w1) * (xt @ sh_w3) @ sh_w2
            return (routed + shared).reshape(b, s, d)
        h = x @ lin0_w + lin0_b
        h = _swiglu(h, swi1_w1, swi1_b1, swi1_w2, swi1_b2)
        h = _moe(h, gate_w, exp_w1, exp_w3, exp_w2, sh_w1, sh_w3, sh_w2)
        h = h @ lin1_w + lin1_b
        h = _swiglu(h, swi2_w1, swi2_b1, swi2_w2, swi2_b2)
        return h
    x = L0_attn_x
    x = x + _layernorm(_L0_attn_ref(_layernorm(x, axis=-1), L0_attn_wq, L0_attn_wk, L0_attn_wv, L0_attn_wo), axis=-1)
    x = x + _layernorm(_L0_ffn_ref(_layernorm(x, axis=-1), L0_ffn_lin0_w, L0_ffn_lin0_b, L0_ffn_swi1_w1, L0_ffn_swi1_b1, L0_ffn_swi1_w2, L0_ffn_swi1_b2, L0_ffn_gate_w, L0_ffn_exp_w1, L0_ffn_exp_w3, L0_ffn_exp_w2, L0_ffn_sh_w1, L0_ffn_sh_w3, L0_ffn_sh_w2, L0_ffn_lin1_w, L0_ffn_lin1_b, L0_ffn_swi2_w1, L0_ffn_swi2_b1, L0_ffn_swi2_w2, L0_ffn_swi2_b2), axis=-1)
    return x

_drawn_inputs = setup_inputs


def setup_inputs(seed=0):
    import zlib

    import numpy as np

    out = dict(_drawn_inputs(seed))
    spreads = {}
    factors = {'L0_ffn_lin0_w': 8.0,
     'L0_ffn_lin0_b': 8.0,
     'L0_ffn_swi1_w1': 8.0,
     'L0_ffn_swi1_b1': 8.0,
     'L0_ffn_swi1_w2': 8.0,
     'L0_ffn_swi1_b2': 8.0,
     'L0_ffn_gate_w': 8.0,
     'L0_ffn_exp_w1': 8.0,
     'L0_ffn_exp_w3': 8.0,
     'L0_ffn_exp_w2': 8.0,
     'L0_ffn_sh_w1': 8.0,
     'L0_ffn_sh_w3': 8.0,
     'L0_ffn_sh_w2': 8.0,
     'L0_ffn_lin1_w': 8.0,
     'L0_ffn_lin1_b': 3.895,
     'L0_ffn_swi2_w1': 5.809,
     'L0_ffn_swi2_w2': 5.51}
    for name, (base, spread) in spreads.items():
        noise = np.random.default_rng([zlib.crc32(name.encode()), seed]).standard_normal(out[name].shape)
        drawn = base * np.exp(spread * noise) if base else spread * noise
        out[name] = jnp.asarray(drawn.astype(out[name].dtype))
    for name, factor in factors.items():
        out[name] = (out[name] * factor).astype(out[name].dtype)
    return out
```

```python
from contextlib import ExitStack

import numpy as np

import concourse.bass as bass
from concourse import mybir

F32 = mybir.dt.float32
F16 = mybir.dt.float16
BF16 = mybir.dt.bfloat16
ALU = mybir.AluOpType
ACT = mybir.ActivationFunctionType
AX = mybir.AxisListType

P = 128
B, T, D = 4, 1024, 128
HEADS, HD = 16, 64
HALF = HD // 2
GH = P // HALF
GROUPS = HEADS // GH
TT = T // P
NT = B * TT
CH = GH * HD // P
BANK = 512
SCALE = float(HD) ** -0.5
EPS = 1e-5
NEG = -1.0e30
MSCALE = 64.0
VW = 2 * HD + 2
E, TOPK, H = 8, 4, 128
SH = 2 * H

UNITS = [(j, max(j * P, half * BANK), (half + 1) * BANK - max(j * P, half * BANK))
         for half in range(T // BANK) for j in range((half + 1) * BANK // P)]
NU = len(UNITS)
SU = NU * GH
PAIR_END = {max(i for i, (j, c, w) in enumerate(UNITS) if j == 2 * q + 1 and c <= (2 * q + 1) * P < c + w): q
            for q in range(TT // 2)}
MAXP = [(t, c, min(BANK, (t + 1) * P - c)) for t in range(TT) for c in range(0, (t + 1) * P, BANK)]
LO_LAG = 0
LAG = 3
NP_ = 5
ROPE_LAG = 3
NAUX = 3


def plan(slots, near, far):
    at = {}

    def put(slot, step, item):
        at.setdefault((slot, step), []).append((slot,) + item)

    for s in slots:
        w = s >= 0
        if s > 0:
            for k, item in enumerate([("tr", 1, 0), ("tr", 1, 1), ("wo", 0), ("wo", 1)]):
                put(s, 3 + k, item)
        if s in far:
            for r in range(4):
                for half in range(2):
                    put(s, w * (1 + 10 * r + half), ("qk", r // 2, r % 2, half))
        if s in near:
            for tp in range(TT // 2):
                put(s, w * (11 + 10 * tp), ("v", tp))
            for h in range(GH):
                for k in range(len(MAXP)):
                    put(s, w * (8 + (h * len(MAXP) + k) * 3 // 4), ("mx", h, k))
            put(s, w * 44, ("mt",))
        if s >= 0:
            put(s, 2 * NU + 5, ("tr", 0, 0))
            put(s, 2 * NU + 7, ("tr", 0, 1))
    if slots[-1] == GROUPS - 1:
        for item in [("tr", 1, 0), ("tr", 1, 1), ("wo", 0), ("wo", 1)]:
            put(GROUPS, 4, item)
    steps = []
    number = {}
    for s in slots:
        for u in range(SU if s >= 0 else 1):
            steps.append((s, u))
    if slots[-1] == GROUPS - 1:
        steps += [(GROUPS, u) for u in range(5)]
    for key in steps:
        for item in at.get(key, []):
            number[item] = len(number)
    assert sum(len(v) for v in at.values()) == len(number)
    return steps, at, number


def lo_on_pool(u):
    return u % 3 == 0


class Box:
    pass


class Counts:

    def __init__(self):
        self.pool, self.dve = [], []
        p = d = 0
        for k in range(SU * GROUPS):
            if lo_on_pool(k % SU):
                p += 1
            else:
                d += 1
            self.pool.append(p)
            self.dve.append(d)


COUNTS = Counts()


def attention_block(nc, M, S, b, slots, near, far):
    steps, at, number = plan(slots, near, far)
    first = slots[0]

    def loads(s):
        return sum(x in near for x in slots if x <= s)

    def ropes(s):
        return sum(x in far for x in slots if x < s)

    def bank(item):
        return number[item] % NAUX

    def taken(eng, item):
        eng.wait_ge(S.aux_free[bank(item)], number[item] // NAUX + 1)

    def ready(eng, item):
        eng.wait_ge(S.aux_ready, number[item] + 1)

    def free(item):
        return S.aux_free[bank(item)]

    def parts(U):
        return U // SU, (U % SU) // NU, U % NU

    def wait_lo(eng, U):
        if lo_on_pool(U % SU):
            eng.wait_ge(S.lo_pool, COUNTS.pool[U])
        else:
            eng.wait_ge(S.lo_dve, COUNTS.dve[U])

    last_unit = SU * len(slots) - 1 if slots[0] >= 0 else -1

    def pairs_at(s, u):
        U = SU * s + u - LAG
        if s >= 0 and 0 <= U <= last_unit and U % NU in PAIR_END:
            return [(U, 4 * (U // NU) + PAIR_END[U % NU])]
        return []

    with nc.Block() as blk:

        @blk.tensor
        def _(pe):
            def scores(U):
                s, h, u = parts(U)
                j, c, w = UNITS[u]
                p = s % 2
                if u == 0 and h == 0 and s > 0:
                    pe.wait_ge(S.row_max_in, 16 * s)
                    pe.wait_ge(S.far_in, 32 * s)
                if U >= 2:
                    pe.wait_ge(S.exp_done, U - 1)
                diagonal = c == j * P
                out = M.psS[:, U % 2, 0:w]
                nc.tensor.matmul(out, M.K1[:, p, h, j * P:(j + 1) * P], M.Q1[:, p, h, c:c + w],
                                 start=True, stop=False)
                mm = nc.tensor.matmul(out, M.K2[0:HD + 1, p, h, j * P:(j + 1) * P],
                                      M.Q2[0:HD + 1, p, h, c:c + w], start=False, stop=not diagonal)
                if diagonal:
                    mm = nc.tensor.matmul(out[:, 0:P], M.ident16[:], M.maskT[:], start=False, stop=True)
                mm.then_inc(S.scores_ready, 1)

            def weighted(U):
                s, h, u = parts(U)
                j, c, w = UNITS[u]
                wait_lo(pe, U)
                for k in range(w // P):
                    t = c // P + k
                    n = 4 * (U // NU) + t // 2
                    first = j == 0 and t % 2 == 0
                    if first and n >= 3:
                        pe.wait_ge(S.out_added, n - 2)
                    O = M.psO[:, n % 3, 256 * (t % 2):256 * (t % 2) + 2 * HD + 1]
                    nc.tensor.matmul(O, M.Phi[:, U % NP_, k * P:(k + 1) * P], M.V[:, s % 2, j, h, 0:2 * HD + 1],
                                     start=first, stop=False, skip_group_check=True)
                    mm = nc.tensor.matmul(O[:, HD:2 * HD + 1], M.Plo[:, U % NP_, k * P:(k + 1) * P],
                                          M.V[:, s % 2, j, h, HD:2 * HD + 1],
                                          start=False, stop=j == t, skip_group_check=True)
                mm.then_inc(S.weighted_done, 1)

            def side(item):
                s, kind, *a = item
                X = M.psX[:, bank(item), :]
                g = (s + (2 if kind == "qk" else 1)) % GROUPS
                p = (s + 1) % 2
                if number[item] >= NAUX:
                    pe.wait_ge(S.aux_free[bank(item)], number[item] // NAUX)
                if kind == "qk":
                    which, n, half = a
                    if s == GROUPS - 2 and which == 0 and n == 0 and half == 0:
                        pe.wait_ge(S.xq_in, 16)
                    cols = (2 * g + half) * P
                    w = M.wkq[:, which]
                    for k, (wi, xi) in enumerate([(0, 0), (0, 1), (1, 0)]):
                        mm = nc.tensor.matmul(X, w[:, wi, cols:cols + P], M.xq[:, xi, n * BANK:(n + 1) * BANK],
                                              start=k == 0, stop=k == 2)
                elif kind == "v":
                    if s == GROUPS - 1 and a[0] == 0:
                        pe.wait_ge(S.xv_in, 16)
                    for k in range(2):
                        t = 2 * a[0] + k
                        for i, (wi, xi) in enumerate([(0, 0), (1, 0), (0, 1)]):
                            mm = nc.tensor.matmul(X[:, k * 256:(k + 1) * 256], M.xv[:, xi, t * P:(t + 1) * P],
                                                  M.wv[:, wi, g * 256:(g + 1) * 256],
                                                  start=i == 0, stop=i == 2)
                elif kind == "mx":
                    h, k = a
                    t, c, w = MAXP[k]
                    if k == 0 and h % 2 == 0:
                        pe.wait_ge(S.near_in[h // 2], 48 * loads(s))
                    diagonal = c + w == (t + 1) * P
                    mm = nc.tensor.matmul(X[:, 0:w], M.Q1[:, p, h, t * P:(t + 1) * P], M.K1[:, p, h, c:c + w],
                                          start=True, stop=not diagonal)
                    if diagonal:
                        mm = nc.tensor.matmul(X[:, w - P:w], M.ident16[:], M.maskN[:], start=False, stop=True)
                elif kind == "mt":
                    pe.wait_ge(S.row_max, loads(s))
                    mm = nc.tensor.transpose(X[0:GH * TT, 0:P], M.rmax[:], M.ident[:])
                elif kind == "tr":
                    c, half = a
                    own = s - 1 if c == 1 else s
                    if half == 0:
                        pe.wait_ge(S.out_scaled, 4 * (GH * own + 2 * (c + 1)))
                    for k in range(4):
                        mm = nc.tensor.transpose(X[:, k * P:(k + 1) * P],
                                                 M.On[:, 4 * half + k, c * P:(c + 1) * P], M.ident[:])
                elif kind == "wo":
                    half = a[0]
                    og = s - 1
                    taken(pe, (og, "tr", 0, half))
                    taken(pe, (s, "tr", 1, half))
                    for k in range(4):
                        for c in range(CH):
                            t = 4 * half + k
                            mm = nc.tensor.matmul(X[:, k * P:(k + 1) * P], M.OT[:, c, t * P:(t + 1) * P],
                                                  M.wo[:, CH * og + c, :], start=c == 0, stop=c == CH - 1)
                mm.then_inc(S.aux_ready, 1)

            for s, u in steps:
                U = SU * s + u
                if 0 <= U <= last_unit:
                    scores(U)
                for item in at.get((s, u), []) if s < GROUPS else []:
                    side(item)
                if s >= 0 and 0 <= U - LAG <= last_unit:
                    weighted(U - LAG)
                for item in at.get((s, u), []) if s == GROUPS else []:
                    side(item)

        @blk.scalar
        def _(act):
            def exps(U):
                w = UNITS[U % NU][2]
                act.wait_ge(S.scores_ready, U + 1)
                if U >= NP_:
                    wait_lo(act, U - NP_)
                    act.wait_ge(S.weighted_done, U - NP_ + 1)
                nc.scalar.activation(M.P32[:, U % NP_, 0:w], M.psS[:, U % 2, 0:w], ACT.Exp, scale=SCALE)
                nc.scalar.activation(M.Phi[:, U % NP_, 0:w], M.psS[:, U % 2, 0:w], ACT.Exp,
                                     scale=SCALE).then_inc(S.exp_done, 1)

            def side(item):
                s, kind, *a = item
                X = M.psX[:, bank(item), :]
                p = (s + 1) % 2
                if kind == "qk" and a[2] == 1:
                    which, n, _ = a
                    r = 4 * ropes(s) + 2 * which + n
                    act.wait_ge(S.rope_sum, r + 1)
                    if ropes(s) > 0 and n == 0:
                        act.wait_ge(S.q_out if which else S.k_out, 16 * GH * ropes(s))
                    nc.scalar.copy(M.HL[:, which, 0:2, n * BANK:(n + 1) * BANK], M.R[:]).then_inc(S.rope_hi, 1)
                elif kind == "v":
                    ready(act, item)
                    if s > 0 and a[0] == 0:
                        act.wait_ge(S.weighted_done, SU * s)
                    nc.scalar.copy(M.V[:, p, 2 * a[0]:2 * a[0] + 2, :, HD:2 * HD],
                                   X.rearrange("p (t h d) -> p t h d", t=2, h=GH)).then_inc(S.v_hi, 1)
                elif kind == "mt":
                    ready(act, item)
                    if s > 0:
                        act.wait_ge(S.row_max_in, 16 * s)
                    nc.scalar.activation(M.mrow[:], X[0:GH * TT, 0:P], ACT.Copy, scale=1.0 / MSCALE).then_inc(free(item), 1)
                elif kind == "tr":
                    ready(act, item)
                    og = s - 1 if a[0] == 0 else s - 2
                    if og >= 0:
                        ready(act, (og + 1, "wo", 1))
                    nc.scalar.copy(M.OT[:, a[0], a[1] * BANK:(a[1] + 1) * BANK], X).then_inc(free(item), 1)

            def out_lo(Uw, n):
                O = M.psO[:, n % 3, :].rearrange("p (t c) -> p t c", t=2)
                act.wait_ge(S.weighted_done, Uw + 1)
                if n >= 2:
                    act.wait_ge(S.out_added, n - 1)
                nc.scalar.copy(M.Olo[:, n % 2], O[:, :, 0:HD]).then_inc(S.out_lo, 1)

            for s, u in steps:
                U = SU * s + u
                if 0 <= U <= last_unit:
                    exps(U)
                if s == GROUPS:
                    for Uw, n in pairs_at(s, u):
                        out_lo(Uw, n)
                for item in at.get((s, u), []):
                    if s < 0 or item[1] != "qk":
                        side(item)
                for item in at.get((s, u - ROPE_LAG), []):
                    if s >= 0 and item[1] == "qk":
                        side(item)
                if s < GROUPS:
                    for Uw, n in pairs_at(s, u):
                        out_lo(Uw, n)

        @blk.vector
        def _(dve):
            def low(U):
                w = UNITS[U % NU][2]
                dve.wait_ge(S.exp_done, U + 1)
                nc.vector.tensor_tensor(M.Plo[:, U % NP_, 0:w], M.P32[:, U % NP_, 0:w], M.Phi[:, U % NP_, 0:w],
                                        ALU.subtract).then_inc(S.lo_dve, 1)

            def side(item):
                s, kind, *a = item
                X = M.psX[:, bank(item), :]
                p = (s + 1) % 2
                if kind == "qk":
                    which, n, half = a
                    r = 4 * ropes(s) + 2 * which + n
                    cols = slice(n * BANK, (n + 1) * BANK)
                    ready(dve, item)
                    if half == 0:
                        if r > 0:
                            dve.wait_ge(S.rope_sum, r)
                        nc.vector.tensor_tensor(M.R4[:, 0, :], X, M.cos[:, cols], ALU.mult)
                        nc.vector.tensor_tensor(M.R4[:, 2, :], X, M.sin[:, cols], ALU.mult).then_inc(free(item), 1)
                    else:
                        nc.vector.tensor_tensor(M.R4[:, 1, :], X, M.sin[:, cols], ALU.mult)
                        nc.vector.tensor_tensor(M.R4[:, 3, :], X, M.cos[:, cols], ALU.mult).then_inc(free(item), 1)
                elif kind == "v":
                    dve.wait_ge(S.v_hi, 4 * (loads(s) - 1) + a[0] + 1)
                    nc.vector.tensor_tensor(M.V[:, p, 2 * a[0]:2 * a[0] + 2, :, 0:HD],
                                            X.rearrange("p (t h d) -> p t h d", t=2, h=GH),
                                            M.V[:, p, 2 * a[0]:2 * a[0] + 2, :, HD:2 * HD],
                                            ALU.subtract).then_inc(free(item), 1)
                elif kind == "mx":
                    h, k = a
                    t, c, w = MAXP[k]
                    ready(dve, item)
                    nc.vector.tensor_reduce(M.pmax[:, int(c > 0), h, t:t + 1], X[:, 0:w], AX.X, ALU.max,
                                            negate=True).then_inc(free(item), 1)
                    if h == GH - 1 and k == len(MAXP) - 1:
                        taken(dve, item)
                        if s > 0:
                            ready(dve, (s - 1, "mt"))
                        nc.vector.tensor_tensor(M.rmax[:], M.pmax[:, 0].rearrange("p h t -> p (h t)"),
                                                M.pmax[:, 1].rearrange("p h t -> p (h t)"),
                                                ALU.min).then_inc(S.row_max, 1)
                elif kind == "wo":
                    ready(dve, item)
                    y = M.y[:, bass.ds(b * TT + 4 * a[0], 4), :].rearrange("p t d -> p (t d)")
                    if s == 1:
                        nc.vector.tensor_copy(y, X).then_inc(free(item), 1)
                    else:
                        taken(dve, (s - 1, "wo", a[0]))
                        nc.vector.tensor_tensor(y, X, y, ALU.add).then_inc(free(item), 1)

            def out_add(Uw, n):
                O = M.psO[:, n % 3, :].rearrange("p (t c) -> p t c", t=2)
                dve.wait_ge(S.out_lo, n + 1)
                if n >= 2:
                    dve.wait_ge(S.out_scaled, n - 1)
                nc.vector.reciprocal(M.rsum[:, n % 2, :, :], O[:, :, 2 * HD:2 * HD + 1])
                nc.vector.tensor_tensor(M.Osum[:, n % 2], O[:, :, HD:2 * HD], M.Olo[:, n % 2],
                                        ALU.add).then_inc(S.out_added, 1)

            for s, u in steps:
                U = SU * s + u - LO_LAG
                for item in at.get((s, u), []) if s < GROUPS else []:
                    side(item)
                if s >= 0 and 0 <= U <= last_unit and not lo_on_pool(U % SU):
                    low(U)
                for Uw, n in pairs_at(s, u):
                    out_add(Uw, n)
                for item in at.get((s, u), []) if s == GROUPS else []:
                    side(item)

        @blk.gpsimd
        def _(pool):
            def low(U):
                w = UNITS[U % NU][2]
                pool.wait_ge(S.exp_done, U + 1)
                nc.gpsimd.tensor_tensor(M.Plo[:, U % NP_, 0:w], M.P32[:, U % NP_, 0:w], M.Phi[:, U % NP_, 0:w],
                                        ALU.subtract).then_inc(S.lo_pool, 1)

            def rotate(item, second):
                s, kind, *a = item
                if kind != "qk" or a[2] == 0:
                    return
                which, n, _ = a
                r = 4 * ropes(s) + 2 * which + n
                cols = slice(n * BANK, (n + 1) * BANK)
                if not second:
                    taken(pool, item)
                    if r > 0:
                        pool.wait_ge(S.rope_lo, r)
                    nc.gpsimd.tensor_tensor(M.R[:, 0, :], M.R4[:, 0, :], M.R4[:, 1, :], ALU.subtract)
                    nc.gpsimd.tensor_tensor(M.R[:, 1, :], M.R4[:, 2, :], M.R4[:, 3, :],
                                            ALU.add).then_inc(S.rope_sum, 1)
                    return
                pool.wait_ge(S.rope_hi, r + 1)
                nc.gpsimd.tensor_tensor(M.HL[:, which, 2:4, cols], M.R[:], M.HL[:, which, 0:2, cols],
                                        ALU.subtract).then_inc(S.rope_lo, 1)

            def out_scale(n):
                head = n // 4
                h, q = head % GH, n % 4
                pool.wait_ge(S.out_added, n + 1)
                own = head // GH
                if q == 0 and h % 2 == 0 and own > 0:
                    ready(pool, (own - 1, "tr", 0, 1) if h == 0 else (own, "tr", 1, 1))
                nc.gpsimd.tensor_tensor(M.On[:, 2 * q:2 * q + 2, h * HD:(h + 1) * HD], M.Osum[:, n % 2],
                                        M.rsum[:, n % 2].to_broadcast([P, 2, HD]),
                                        ALU.mult).then_inc(S.out_scaled, 1)

            for s, u in steps:
                U = SU * s + u - LO_LAG
                if s >= 0 and 0 <= U <= last_unit and lo_on_pool(U % SU):
                    low(U)
                for item in at.get((s, u), []):
                    rotate(item, False)
                    if s < 0:
                        rotate(item, True)
                for item in at.get((s, u - ROPE_LAG - 1), []):
                    if s >= 0:
                        rotate(item, True)
                for _, n in pairs_at(s, u):
                    out_scale(n)

        @blk.sync
        def _(sp):
            def load(s):
                p = (s + 1) % 2
                if s > 0:
                    sp.wait_ge(S.scores_ready, SU * s)
                krows = M.k_way.rearrange("k f h n -> (k f) h n")
                qrows = M.q_way.rearrange("k f h n -> (k f) h n")
                if s > first:
                    sp.wait_ge(S.k_out, 16 * GH * ropes(s))
                    sp.wait_ge(S.q_out, 16 * GH * ropes(s))
                for i in range(2):
                    h = slice(2 * i, 2 * i + 2)
                    sp.dma_start(M.K1[:, p, h], krows[:, h]).then_inc(S.near_in[i], 16)
                    sp.dma_start(M.Q1[0:HD, p, h], qrows[0:HD, h]).then_inc(S.near_in[i], 16)
                    sp.dma_start(M.Q1[HD:P, p, h], qrows[0:HD, h]).then_inc(S.near_in[i], 16)
                sp.dma_start(M.K2[0:HD, p], krows[0:HD]).then_inc(S.far_in, 16)
                sp.dma_start(M.Q2[0:HD, p], qrows[HD:P]).then_inc(S.far_in, 16)

            def send(s, which):
                way, sent = (M.q_way, S.q_out) if which else (M.k_way, S.k_out)
                sp.wait_ge(S.rope_lo, 4 * ropes(s) + 2 * which + 2)
                if which == 0 and loads(s) > 0:
                    for i in range(2):
                        sp.wait_ge(S.near_in[i], 48 * loads(s))
                    sp.wait_ge(S.far_in, 32 * loads(s))
                for h in range(GH):
                    sp.dma_start(way[:, :, h, :].rearrange("k f n -> f k n"),
                                 M.HL[h * HALF:(h + 1) * HALF, which, :, :]).then_inc(sent, 16)

            for s in slots:
                if s in near:
                    load(s)
                    if s == GROUPS - 1:
                        ready(sp, (s - 1, "v", TT // 2 - 1))
                        sp.dma_start(M.xv[:], M.x_way[:, :, bass.ds((b + 1) * T, T)]).then_inc(S.xv_in, 16)
                if s in far:
                    if s == GROUPS - 2:
                        ready(sp, (s - 1, "qk", 1, 1, 1))
                        sp.dma_start(M.xq[:], M.x_way[:, :, bass.ds((b + 1) * T, T)]).then_inc(S.xq_in, 16)
                    send(s, 0)
                    send(s, 1)
                if s in near:
                    taken(sp, (s, "mt"))
                    sp.dma_start(M.Q2[HD:HD + 1, (s + 1) % 2, :, :].rearrange("o h (t i) -> o (h t) i", i=P),
                                 M.mrow[:]).then_inc(S.row_max_in, 16)
            if far:
                sp.wait_ge(S.k_out, 16 * GH * len(far))
                sp.wait_ge(S.q_out, 16 * GH * len(far))
            sp.wait_ge(S.far_in, 32 * len(near))
            sp.wait_ge(S.row_max_in, 16 * len(near))


def block_end(nc, S):
    nc.sync.sem_clear(range(S.first, S.last + 1))
    nc.all_engine_barrier()


def load_block(nc, I, M, S, stack, sb, ps):
    xs = sb(stack, "xs", [P, NT, D], F32)
    xn = sb(stack, "xn", [P, NT, D], F32)
    xT = sb(stack, "xT", [P, 2, NT * P], F16)
    w32 = sb(stack, "w32", [P, 3, HEADS * HD], F32)
    bn = sb(stack, "bn", [P, NT, 6], F32)
    mv = sb(stack, "mv", [P, NT, 2], F32)
    std = sb(stack, "std", [P, NT], F32)
    rstd = sb(stack, "rstd", [P, NT], F32)
    psT = ps(stack, "psT", [P, 2, BANK], F32)
    NB = NT * P // BANK
    x_tiles = I["x"].rearrange("b (t p) d -> p (b t) d", p=P)
    with nc.Block() as blk:
        @blk.sync
        def _(sp):
            for b in range(B):
                sp.dma_start(xs[:, b * TT:(b + 1) * TT, :], x_tiles[:, b * TT:(b + 1) * TT, :]).then_inc(S.x_load[b], 16)
            for k, w in enumerate((I["wk"], I["wq"], I["wv"])):
                sp.dma_start(w32[:, k, :], w).then_inc(S.w_in, 16)
            sp.dma_start(M.wo[:], I["wo"]).then_inc(S.c_in, 16)
            sp.dma_start(M.cos[:], I["cos"]).then_inc(S.c_in, 16)
            sp.dma_start(M.sin[:], I["sin"]).then_inc(S.c_in, 16)
            for k in range(NB):
                sp.wait_ge(S.split_lo, k + 1)
                cols = slice(k * BANK, (k + 1) * BANK)
                sp.dma_start(M.x_way[:, :, cols], xT[:, :, cols]).then_inc(S.stored, 16)
            sp.wait_ge(S.stored, 16 * NB)
            sp.wait_ge(S.c_in, 48)

        @blk.gpsimd
        def _(pool):
            nc.gpsimd.memset(M.ident[:], 0.0)
            nc.gpsimd.memset(M.ident16[:], 0.0)
            nc.gpsimd.memset(M.maskT[:], 0.0)
            nc.gpsimd.memset(M.maskN[:], 0.0).then_inc(S.consts, 1)
            pool.wait_ge(S.consts, 1)
            for t in (M.ident, M.ident16):
                nc.gpsimd.affine_select(out=t[:], in_=t[:], compare_op=ALU.not_equal, fill=1.0, base=0,
                                        pattern=[[-1, P]], channel_multiplier=1)
            nc.gpsimd.affine_select(out=M.maskT[:], in_=M.maskT[:], compare_op=ALU.is_ge, fill=NEG, base=0,
                                    pattern=[[1, P]], channel_multiplier=-1)
            nc.gpsimd.affine_select(out=M.maskN[:], in_=M.maskN[:], compare_op=ALU.is_ge, fill=NEG, base=0,
                                    pattern=[[-1, P]], channel_multiplier=1).then_inc(S.consts, 1)

        @blk.vector
        def _(dve):
            for b in range(B):
                dve.wait_ge(S.x_load[b], 16)
                for t in range(b * TT, (b + 1) * TT):
                    last = nc.vector.bn_stats(bn[:, t, :], xs[:, t, :])
            last.then_inc(S.stats, 1)
            dve.wait_ge(S.stats, 1)
            for t in range(NT):
                last = nc.vector.bn_aggr(mv[:, t, :], bn[:, t, :])
            last.then_inc(S.stats, 1)
            dve.wait_ge(S.stats, 2)
            nc.vector.tensor_scalar(std[:], mv[:, :, 1], EPS, None, ALU.add).then_inc(S.var_ready, 1)
            dve.wait_ge(S.std_ready, 1)
            nc.vector.reciprocal(rstd[:], std[:]).then_inc(S.stats, 1)
            dve.wait_ge(S.stats, 3)
            for t in range(NT):
                nc.vector.tensor_scalar(xn[:, t, :], xs[:, t, :], mv[:, t, 0:1], rstd[:, t:t + 1],
                                        ALU.subtract, ALU.mult).then_inc(S.norm_ready, 1)
            for k in range(NB):
                dve.wait_ge(S.split_hi, k + 1)
                cols = slice(k * BANK, (k + 1) * BANK)
                nc.vector.tensor_tensor(xT[:, 1, cols], psT[:, k % 2, :], xT[:, 0, cols],
                                        ALU.subtract).then_inc(S.split_lo, 1)
            for k, dst in enumerate((M.wkq[:, 0], M.wkq[:, 1], M.wv)):
                dve.wait_ge(S.split_hi, NB + k + 1)
                last = nc.vector.tensor_tensor(dst[:, 1, :], w32[:, k, :], dst[:, 0, :], ALU.subtract)

        @blk.scalar
        def _(act):
            act.wait_ge(S.var_ready, 1)
            nc.scalar.activation(std[:], std[:], ACT.Sqrt).then_inc(S.std_ready, 1)
            for k in range(NB):
                act.wait_ge(S.turned, k + 1)
                nc.scalar.copy(xT[:, 0, k * BANK:(k + 1) * BANK], psT[:, k % 2, :]).then_inc(S.split_hi, 1)
            act.wait_ge(S.w_in, 48)
            for k, dst in enumerate((M.wkq[:, 0], M.wkq[:, 1], M.wv)):
                nc.scalar.copy(dst[:, 0, :], w32[:, k, :]).then_inc(S.split_hi, 1)

        @blk.tensor
        def _(pe):
            pe.wait_ge(S.consts, 2)
            for k in range(NB):
                pe.wait_ge(S.norm_ready, 4 * k + 4)
                if k >= 2:
                    pe.wait_ge(S.split_lo, k - 1)
                for i in range(4):
                    mm = nc.tensor.transpose(psT[:, k % 2, i * P:(i + 1) * P], xn[:, 4 * k + i, :], M.ident[:])
                mm.then_inc(S.turned, 1)
    block_end(nc, S)


def init_block(nc, M, S):
    with nc.Block() as blk:
        @blk.vector
        def _(dve):
            nc.vector.memset(M.K2[HD:HD + 1], MSCALE)
            nc.vector.memset(M.V[:, :, :, :, 2 * HD:2 * HD + 1].rearrange("p a t h o -> p (a t h) o"), 1.0)
            nc.vector.memset(M.pmax[:], 3.0e38)

        @blk.sync
        def _(sp):
            sp.dma_start(M.xq[:], M.x_way[:, :, 0:T]).then_inc(S.xq_in, 16)
            sp.dma_start(M.xv[:], M.x_way[:, :, 0:T]).then_inc(S.xv_in, 16)
            sp.wait_ge(S.xq_in, 16)
            sp.wait_ge(S.xv_in, 16)
    block_end(nc, S)


def phase_attention(nc, I, M, S, sb, ps):
    with ExitStack() as stack:
        M.wkq = sb(stack, "wkq", [P, 2, 2, HEADS * HD], F16)
        M.wv = sb(stack, "wv", [P, 2, HEADS * HD], F16)
        M.wo = sb(stack, "wo", [P, HEADS * HD // P, D], F32)
        M.cos = sb(stack, "cos", [P, T], F32)
        M.sin = sb(stack, "sin", [P, T], F32)
        M.ident16 = sb(stack, "ident16", [P, P], BF16)
        M.maskT = sb(stack, "maskT", [P, P], BF16)
        M.maskN = sb(stack, "maskN", [P, P], BF16)
        with ExitStack() as temps:
            load_block(nc, I, M, S, temps, sb, ps)
        M.K1 = sb(stack, "K1", [P, 2, GH, T], F16)
        M.Q1 = sb(stack, "Q1", [P, 2, GH, T], F16)
        M.K2 = sb(stack, "K2", [P, 2, GH, T], F16)
        M.Q2 = sb(stack, "Q2", [P, 2, GH, T], F16)
        M.V = sb(stack, "V", [P, 2, TT, GH, VW], F16)
        M.P32 = sb(stack, "P32", [P, NP_, BANK], F32)
        M.Phi = sb(stack, "Phi", [P, NP_, BANK], F16)
        M.Plo = sb(stack, "Plo", [P, NP_, BANK], F16)
        M.R4 = sb(stack, "R4", [P, 4, BANK], F32)
        M.R = sb(stack, "R", [P, 2, BANK], F32)
        M.HL = sb(stack, "HL", [P, 2, 4, T], F16)
        M.On = sb(stack, "On", [P, TT, GH * HD], F32)
        M.OT = sb(stack, "OT", [P, CH, T], F32)
        M.Olo = sb(stack, "Olo", [P, 2, 2, HD], F32)
        M.Osum = sb(stack, "Osum", [P, 2, 2, HD], F32)
        M.rsum = sb(stack, "rsum", [P, 2, 2, 1], F32)
        M.pmax = sb(stack, "pmax", [P, 2, GH, TT], F32)
        M.rmax = sb(stack, "rmax", [P, GH * TT], F32)
        M.mrow = sb(stack, "mrow", [GH * TT, P], F16)
        M.xq = sb(stack, "xq", [P, 2, T], F16)
        M.xv = sb(stack, "xv", [P, 2, T], F16)
        M.psS = ps(stack, "psS", [P, 2, BANK], F32)
        M.psO = ps(stack, "psO", [P, 3, BANK], F32)
        M.psX = ps(stack, "psX", [P, NAUX, BANK], F32)
        init_block(nc, M, S)
        attention_block(nc, M, S, 0, [-2, -1], [-1], [-2, -1])
        block_end(nc, S)
        slots = list(range(GROUPS))
        with nc.Fori(0, B - 1) as b:
            attention_block(nc, M, S, b, slots, slots, slots)
            block_end(nc, S)
        attention_block(nc, M, S, B - 1, slots, slots[:-1], slots[:-2])
        block_end(nc, S)


def norm_block(nc, I, M, S, stack, sb, ps):
    zn = sb(stack, "zn", [P, NT, D], F32)
    bn = sb(stack, "bn3", [P, 2, NT, 6], F32)
    mv = sb(stack, "mv3", [P, 2, NT, 2], F32)
    std = sb(stack, "std3", [P, 2, NT], F32)
    rstd = sb(stack, "rstd3", [P, 2, NT], F32)
    psT = ps(stack, "psT3", [P, 2, BANK], F32)
    x_tiles = I["x"].rearrange("b (t p) d -> p (b t) d", p=P)
    with nc.Block() as blk:
        @blk.sync
        def _(sp):
            sp.dma_start(M.x1[:], x_tiles).then_inc(S.x_load[0], 16)
            for k, w in enumerate((I["lin0_w"], I["swi1_w1"], I["swi1_w2"], I["lin1_w"], I["swi2_w1"], I["swi2_w2"])):
                sp.dma_start(M.wd[:, k, :], w).then_inc(S.w_in, 16)
            for k, w in enumerate((I["lin0_b"], I["swi1_b1"], I["swi1_b2"], I["lin1_b"], I["swi2_b1"], I["swi2_b2"])):
                sp.dma_start(M.bias[:, k:k + 1], w.rearrange("(d o) -> d o", o=1)).then_inc(S.w_in, 16)
            sp.dma_start(M.gate[:], I["gate_w"]).then_inc(S.w_in, 16)
            sp.dma_start(M.w1[:, 0:E], I["exp_w1"].rearrange("e d h -> d e h")).then_inc(S.w_in, 16)
            sp.dma_start(M.w3[:, 0:E], I["exp_w3"].rearrange("e d h -> d e h")).then_inc(S.w_in, 16)
            sp.dma_start(M.w2[:, 0:E], I["exp_w2"].rearrange("e h d -> h e d")).then_inc(S.w_in, 16)
            sp.dma_start(M.w1[:, E:E + SH // H], I["sh_w1"].rearrange("d (c h) -> d c h", h=H)).then_inc(S.w_in, 16)
            sp.dma_start(M.w3[:, E:E + SH // H], I["sh_w3"].rearrange("d (c h) -> d c h", h=H)).then_inc(S.w_in, 16)
            sp.dma_start(M.w2[:, E:E + SH // H], I["sh_w2"].rearrange("(c h) d -> h c d", h=H)).then_inc(S.w_in, 16)
            sp.wait_ge(S.w_in, 16 * 19)

        @blk.vector
        def _(dve):
            for i, src in enumerate((M.y, M.x1)):
                for t in range(NT):
                    if i == 1:
                        dve.wait_ge(S.norm_ready, t + 1)
                    last = nc.vector.bn_stats(bn[:, i, t, :], src[:, t, :])
                last.then_inc(S.stats, 1)
                dve.wait_ge(S.stats, 3 * i + 1)
                for t in range(NT):
                    last = nc.vector.bn_aggr(mv[:, i, t, :], bn[:, i, t, :])
                last.then_inc(S.stats, 1)
                dve.wait_ge(S.stats, 3 * i + 2)
                nc.vector.tensor_scalar(std[:, i], mv[:, i, :, 1], EPS, None, ALU.add).then_inc(S.var_ready, 1)
                dve.wait_ge(S.std_ready, i + 1)
                nc.vector.reciprocal(rstd[:, i], std[:, i]).then_inc(S.stats, 1)
                dve.wait_ge(S.stats, 3 * i + 3)
                for t in range(NT):
                    nc.vector.tensor_scalar(zn[:, t, :], src[:, t, :], mv[:, i, t, 0:1], rstd[:, i, t:t + 1],
                                            ALU.subtract, ALU.mult).then_inc(S.step_a, 1)
            nc.vector.memset(M.tri[:], 1.0)

        @blk.scalar
        def _(act):
            for i in range(2):
                act.wait_ge(S.var_ready, i + 1)
                nc.scalar.activation(std[:, i], std[:, i], ACT.Sqrt).then_inc(S.std_ready, 1)
            for k in range(NT // 4):
                act.wait_ge(S.turned, k + 1)
                nc.scalar.copy(M.zT[:, k * BANK:(k + 1) * BANK], psT[:, k % 2, :]).then_inc(S.turned_out, 1)

        @blk.gpsimd
        def _(pool):
            pool.wait_ge(S.x_load[0], 16)
            for t in range(NT):
                pool.wait_ge(S.step_a, t + 1)
                nc.gpsimd.tensor_tensor(M.x1[:, t, :], M.x1[:, t, :], zn[:, t, :], ALU.add).then_inc(S.norm_ready, 1)

        @blk.tensor
        def _(pe):
            for k in range(NT // 4):
                pe.wait_ge(S.step_a, NT + 4 * k + 4)
                if k >= 2:
                    pe.wait_ge(S.turned_out, k - 1)
                for i in range(4):
                    mm = nc.tensor.transpose(psT[:, k % 2, i * P:(i + 1) * P], zn[:, 4 * k + i, :], M.ident[:])
                mm.then_inc(S.turned, 1)
    block_end(nc, S)


def front_block(nc, M, S, stack, sb, ps):
    h0 = sb(stack, "h0", [P, 2, BANK], F32)
    sg = sb(stack, "sg", [P, 2, BANK], F32)
    psH = ps(stack, "psH", [P, 2, BANK], F32)
    psG = ps(stack, "psG", [P, 2, BANK], F32)
    psU = ps(stack, "psU", [P, 2, BANK], F32)
    psL = ps(stack, "psL", [P, NT, E], F32)
    logit = sb(stack, "logit", [P, NT, E], F32)
    score = sb(stack, "score", [P, NT, E], F32)
    small = sb(stack, "small", [P, 4, NT, 1], F32)
    more = sb(stack, "more", [P, NT, E, E], F32)
    same = sb(stack, "same", [P, NT, E, E], F32)
    rank = sb(stack, "rank", [P, NT, E], F32)
    NB = NT * P // BANK
    TB = BANK // P
    with nc.Block() as blk:
        @blk.tensor
        def _(pe):
            for k in range(NB + 2):
                if k < NB:
                    if k >= 2:
                        pe.wait_ge(S.step_a, k - 1)
                    nc.tensor.matmul(psH[:, k % 2, :], M.wd[:, 0, :], M.zT[:, k * BANK:(k + 1) * BANK],
                                     start=True, stop=True).then_inc(S.step_b, 1)
                if 1 <= k <= NB:
                    i = k - 1
                    pe.wait_ge(S.step_a, i + 1)
                    if i >= 2:
                        pe.wait_ge(S.step_d, i - 1)
                    nc.tensor.matmul(psG[:, i % 2, :], M.wd[:, 1, :], h0[:, i % 2, :],
                                     start=True, stop=True).then_inc(S.step_c, 1)
                    nc.tensor.matmul(psU[:, i % 2, :], M.wd[:, 2, :], h0[:, i % 2, :],
                                     start=True, stop=True).then_inc(S.step_c, 1)
                if k >= 2:
                    i = k - 2
                    pe.wait_ge(S.step_d, i + 1)
                    for t in range(TB * i, TB * i + TB):
                        mm = nc.tensor.matmul(psL[:, t, :], M.h1T[:, t * P:(t + 1) * P], M.gate[:],
                                              start=True, stop=True)
                    mm.then_inc(S.step_e, 1)

        @blk.scalar
        def _(act):
            for k in range(NB):
                act.wait_ge(S.step_b, k + 1)
                if k >= 2:
                    act.wait_ge(S.step_c, 2 * k - 2)
                nc.scalar.activation(h0[:, k % 2, :], psH[:, k % 2, :], ACT.Identity,
                                     bias=M.bias[:, 0:1]).then_inc(S.step_a, 1)
                act.wait_ge(S.step_c, 2 * k + 1)
                if k >= 2:
                    act.wait_ge(S.step_d, k - 1)
                nc.scalar.activation(sg[:, k % 2, :], psG[:, k % 2, :], ACT.Silu,
                                     bias=M.bias[:, 1:2]).then_inc(S.step_f, 1)
            act.wait_ge(S.step_g, 2)
            nc.scalar.activation(score[:], logit[:], ACT.Exp).then_inc(S.step_h, 1)

        @blk.gpsimd
        def _(pool):
            nc.gpsimd.affine_select(out=M.tri[:], in_=M.tri[:], compare_op=ALU.is_ge, fill=0.0, base=-1,
                                    pattern=[[1, E], [-1, E]], channel_multiplier=0).then_inc(S.consts, 1)

        @blk.vector
        def _(dve):
            for k in range(NB):
                dve.wait_ge(S.step_f, k + 1)
                dve.wait_ge(S.step_c, 2 * k + 2)
                nc.vector.scalar_tensor_tensor(out=M.h1T[:, k * BANK:(k + 1) * BANK], in0=psU[:, k % 2, :],
                                               scalar=M.bias[:, 2:3], in1=sg[:, k % 2, :],
                                               op0=ALU.add, op1=ALU.mult).then_inc(S.step_d, 1)
            done = [0]
            dve.wait_ge(S.step_e, NB)

            def then(ins):
                done[0] += 1
                ins.then_inc(S.step_g, 1)
                dve.wait_ge(S.step_g, done[0])

            def wide(ap):
                return ap.to_broadcast([P, NT, E])

            then(nc.vector.tensor_reduce(small[:, 0, :, 0], psL[:], AX.X, ALU.max))
            then(nc.vector.tensor_tensor(logit[:], psL[:], wide(small[:, 0]), ALU.subtract))
            dve.wait_ge(S.step_h, 1)
            then(nc.vector.tensor_reduce(small[:, 1, :, 0], score[:], AX.X, ALU.add))
            then(nc.vector.reciprocal(small[:, 2], small[:, 1]))
            then(nc.vector.tensor_tensor(score[:], score[:], wide(small[:, 2]), ALU.mult))
            own = score[:].unsqueeze(3).to_broadcast([P, NT, E, E])
            other = score[:].unsqueeze(2).to_broadcast([P, NT, E, E])
            dve.wait_ge(S.consts, 1)
            nc.vector.tensor_tensor(same[:], other, own, ALU.is_equal)
            then(nc.vector.tensor_tensor(more[:], other, own, ALU.is_gt))
            then(nc.vector.tensor_tensor(same[:], same[:], M.tri[:].unsqueeze(1).to_broadcast([P, NT, E, E]),
                                         ALU.mult))
            then(nc.vector.tensor_tensor(more[:], more[:], same[:], ALU.add))
            then(nc.vector.tensor_reduce(rank[:], more[:], AX.X, ALU.add))
            then(nc.vector.tensor_scalar(rank[:], rank[:], TOPK - 0.5, None, ALU.is_lt))
            then(nc.vector.tensor_tensor(rank[:], rank[:], score[:], ALU.mult))
            then(nc.vector.tensor_reduce(small[:, 3, :, 0], rank[:], AX.X, ALU.add))
            then(nc.vector.reciprocal(small[:, 0], small[:, 3]))
            then(nc.vector.tensor_tensor(M.comb[:], rank[:], wide(small[:, 0]), ALU.mult))
    block_end(nc, S)


def expert_block(nc, M, S, R, i):
    TB = BANK // P
    NC = SH // H
    work = [(k, c) for k in range(2) for c in [*range(E, E + NC), *range(E)]]
    W = len(work)
    with nc.Block() as blk:
        @blk.tensor
        def _(pe):
            def hidden(n):
                k, c = work[n]
                if n >= 2:
                    pe.wait_ge(S.step_b, n - 1)
                x = M.h1T[:, bass.ds((2 * i + k) * BANK, BANK)]
                nc.tensor.matmul(R.psG[:, n % 2, :], M.w1[:, c, :], x, start=True, stop=True).then_inc(S.step_a, 1)
                nc.tensor.matmul(R.psU[:, n % 2, :], M.w3[:, c, :], x, start=True, stop=True).then_inc(S.step_a, 1)

            def back(n):
                k, c = work[n]
                if c == E:
                    return
                chunks = range(n - NC + 1, n + 1) if c > E else [n]
                o = n - k * (NC - 1) - (NC - 1)
                pe.wait_ge(S.step_b, n + 1)
                if o >= 2:
                    pe.wait_ge(S.step_c, o - 1)
                for t in range(TB):
                    for m in chunks:
                        mm = nc.tensor.matmul(R.psY[:, o % 2, t * P:(t + 1) * P], R.hid[:, m % 4, t * P:(t + 1) * P],
                                              M.w2[:, work[m][1], :], start=m == chunks[0], stop=m == n)
                mm.then_inc(S.step_d, 1)

            for n in range(W + 1):
                if n < W:
                    hidden(n)
                if n >= 1:
                    back(n - 1)

        @blk.scalar
        def _(act):
            for n in range(W):
                act.wait_ge(S.step_a, 2 * n + 1)
                if n >= 2:
                    act.wait_ge(S.step_b, n - 1)
                nc.scalar.activation(R.sg[:, n % 2, :], R.psG[:, n % 2, :], ACT.Silu).then_inc(S.step_e, 1)

        @blk.vector
        def _(dve):
            def gated(n):
                dve.wait_ge(S.step_e, n + 1)
                dve.wait_ge(S.step_a, 2 * n + 2)
                o = n - 4 - (n - 4) // (E + NC) * (NC - 1) - (NC - 1)
                if n >= 4:
                    dve.wait_ge(S.step_d, max(o, 0) + 1)
                nc.vector.tensor_tensor(R.hid[:, n % 4, :], R.psU[:, n % 2, :], R.sg[:, n % 2, :],
                                        ALU.mult).then_inc(S.step_b, 1)

            def add(n):
                k, c = work[n]
                if c == E:
                    return
                o = n - k * (NC - 1) - (NC - 1)
                dve.wait_ge(S.step_d, o + 1)
                at = (2 * i + k) * TB
                if c > E:
                    nc.vector.tensor_copy(M.moe[:, bass.ds(at, TB), :].rearrange("p t d -> p (t d)"),
                                          R.psY[:, o % 2, :]).then_inc(S.step_c, 1)
                    return
                dve.wait_ge(S.step_c, o)
                for t in range(TB):
                    acc = M.moe[:, bass.ds(at + t, 1), :].rearrange("p t d -> p (t d)")
                    last = nc.vector.scalar_tensor_tensor(
                        out=acc, in0=R.psY[:, o % 2, t * P:(t + 1) * P],
                        scalar=R.comb[:, k * TB + t, c:c + 1], in1=acc, op0=ALU.mult, op1=ALU.add)
                last.then_inc(S.step_c, 1)

            nc.vector.tensor_copy(R.comb[:].rearrange("p t e -> p (t e)"),
                                  M.comb[:, bass.ds(2 * i * TB, 2 * TB), :].rearrange("p t e -> p (t e)"))
            for n in range(W + 1):
                if n < W:
                    gated(n)
                if n >= 1:
                    add(n - 1)
    block_end(nc, S)


def back_block(nc, M, S, stack, sb, ps, out):
    mT = sb(stack, "mT", [P, 2, BANK], F32)
    h3 = sb(stack, "h3", [P, 2, BANK], F32)
    sg = sb(stack, "sg5", [P, 2, BANK], F32)
    h4 = sb(stack, "h4", [P, 2, BANK], F32)
    hn = sb(stack, "hn", [P, NT, D], F32)
    bn = sb(stack, "bn5", [P, NT, 6], F32)
    mv = sb(stack, "mv5", [P, NT, 2], F32)
    std = sb(stack, "std5", [P, NT], F32)
    rstd = sb(stack, "rstd5", [P, NT], F32)
    psM = ps(stack, "psM", [P, 2, BANK], F32)
    psH = ps(stack, "psH5", [P, BANK], F32)
    psG = ps(stack, "psG5", [P, 2, BANK], F32)
    psU = ps(stack, "psU5", [P, 2, BANK], F32)
    psN = ps(stack, "psN", [P, BANK], F32)
    NB = NT * P // BANK
    TB = BANK // P
    out_tiles = out.rearrange("b (t p) d -> p (b t) d", p=P)
    with nc.Block() as blk:
        @blk.tensor
        def _(pe):
            for k in range(NB + 3):
                if k < NB:
                    if k >= 2:
                        pe.wait_ge(S.step_b, k - 1)
                    for t in range(TB):
                        mm = nc.tensor.transpose(psM[:, k % 2, t * P:(t + 1) * P], M.moe[:, TB * k + t, :], M.ident[:])
                    mm.then_inc(S.step_a, 1)
                if 1 <= k <= NB:
                    i = k - 1
                    pe.wait_ge(S.step_b, i + 1)
                    if i >= 1:
                        pe.wait_ge(S.step_d, i)
                    nc.tensor.matmul(psH[:], M.wd[:, 3, :], mT[:, i % 2, :], start=True, stop=True).then_inc(S.step_c, 1)
                if 2 <= k <= NB + 1:
                    i = k - 2
                    pe.wait_ge(S.step_d, i + 1)
                    if i >= 2:
                        pe.wait_ge(S.step_g, i - 1)
                    nc.tensor.matmul(psG[:, i % 2, :], M.wd[:, 4, :], h3[:, i % 2, :],
                                     start=True, stop=True).then_inc(S.step_e, 1)
                    nc.tensor.matmul(psU[:, i % 2, :], M.wd[:, 5, :], h3[:, i % 2, :],
                                     start=True, stop=True).then_inc(S.step_e, 1)
                if k >= 3:
                    i = k - 3
                    pe.wait_ge(S.step_g, i + 1)
                    if i >= 1:
                        pe.wait_ge(S.norm_ready, i)
                    for t in range(TB):
                        mm = nc.tensor.transpose(psN[:, t * P:(t + 1) * P], h4[:, i % 2, t * P:(t + 1) * P], M.ident[:])
                    mm.then_inc(S.step_h, 1)

        @blk.scalar
        def _(act):
            for k in range(NB + 2):
                if k < NB:
                    act.wait_ge(S.step_a, k + 1)
                    if k >= 2:
                        act.wait_ge(S.step_c, k - 1)
                    nc.scalar.copy(mT[:, k % 2, :], psM[:, k % 2, :]).then_inc(S.step_b, 1)
                if 1 <= k <= NB:
                    i = k - 1
                    act.wait_ge(S.step_c, i + 1)
                    if i >= 2:
                        act.wait_ge(S.step_e, 2 * i - 2)
                    nc.scalar.activation(h3[:, i % 2, :], psH[:], ACT.Identity,
                                         bias=M.bias[:, 3:4]).then_inc(S.step_d, 1)
                if k >= 2:
                    i = k - 2
                    act.wait_ge(S.step_e, 2 * i + 1)
                    if i >= 2:
                        act.wait_ge(S.step_g, i - 1)
                    nc.scalar.activation(sg[:, i % 2, :], psG[:, i % 2, :], ACT.Silu,
                                         bias=M.bias[:, 4:5]).then_inc(S.step_f, 1)
            act.wait_ge(S.var_ready, 1)
            nc.scalar.activation(std[:], std[:], ACT.Sqrt).then_inc(S.std_ready, 1)

        @blk.vector
        def _(dve):
            for k in range(NB + 1):
                if k < NB:
                    dve.wait_ge(S.step_f, k + 1)
                    dve.wait_ge(S.step_e, 2 * k + 2)
                    if k >= 2:
                        dve.wait_ge(S.step_h, k - 1)
                    nc.vector.scalar_tensor_tensor(out=h4[:, k % 2, :], in0=psU[:, k % 2, :],
                                                   scalar=M.bias[:, 5:6], in1=sg[:, k % 2, :],
                                                   op0=ALU.add, op1=ALU.mult).then_inc(S.step_g, 1)
                if k >= 1:
                    i = k - 1
                    dve.wait_ge(S.step_h, i + 1)
                    for t in range(TB):
                        nc.vector.bn_stats(bn[:, TB * i + t, :], psN[:, t * P:(t + 1) * P])
                    nc.vector.tensor_copy(hn[:, TB * i:TB * i + TB, :].rearrange("p t d -> p (t d)"),
                                          psN[:]).then_inc(S.norm_ready, 1)
            dve.wait_ge(S.norm_ready, NB)
            for t in range(NT):
                last = nc.vector.bn_aggr(mv[:, t, :], bn[:, t, :])
            last.then_inc(S.stats, 1)
            dve.wait_ge(S.stats, 1)
            nc.vector.tensor_scalar(std[:], mv[:, :, 1], EPS, None, ALU.add).then_inc(S.var_ready, 1)
            dve.wait_ge(S.std_ready, 1)
            nc.vector.reciprocal(rstd[:], std[:]).then_inc(S.stats, 1)
            dve.wait_ge(S.stats, 2)
            for t in range(NT):
                nc.vector.tensor_scalar(hn[:, t, :], hn[:, t, :], mv[:, t, 0:1], rstd[:, t:t + 1],
                                        ALU.subtract, ALU.mult).then_inc(S.split_hi, 1)

        @blk.gpsimd
        def _(pool):
            for t in range(NT):
                pool.wait_ge(S.split_hi, t + 1)
                nc.gpsimd.tensor_tensor(M.x1[:, t, :], M.x1[:, t, :], hn[:, t, :], ALU.add).then_inc(S.split_lo, 1)

        @blk.sync
        def _(sp):
            for k in range(NB):
                sp.wait_ge(S.split_lo, TB * (k + 1))
                sp.dma_start(out_tiles[:, TB * k:TB * k + TB, :], M.x1[:, TB * k:TB * k + TB, :]).then_inc(S.stored, 16)
            sp.wait_ge(S.stored, 16 * NB)


def phase_ffn(nc, I, M, S, sb, ps, out):
    with ExitStack() as stack:
        M.x1 = sb(stack, "x1", [P, NT, D], F32)
        M.wd = sb(stack, "wd", [P, 6, D], F32)
        M.bias = sb(stack, "bias", [P, 6], F32)
        M.gate = sb(stack, "gate", [P, E], F32)
        M.w1 = sb(stack, "w1", [P, E + SH // H, H], F32)
        M.w3 = sb(stack, "w3", [P, E + SH // H, H], F32)
        M.w2 = sb(stack, "w2", [P, E + SH // H, D], F32)
        M.zT = sb(stack, "zT", [P, NT * P], F32)
        M.h1T = sb(stack, "h1T", [P, NT * P], F32)
        M.comb = sb(stack, "comb", [P, NT, E], F32)
        M.moe = sb(stack, "moe", [P, NT, D], F32)
        M.tri = sb(stack, "tri", [P, E, E], F32)
        with ExitStack() as temps:
            norm_block(nc, I, M, S, temps, sb, ps)
        with ExitStack() as temps:
            front_block(nc, M, S, temps, sb, ps)
        with ExitStack() as temps:
            R = Box()
            R.sg = sb(temps, "sg4", [P, 2, BANK], F32)
            R.hid = sb(temps, "hid", [P, 4, BANK], F32)
            R.comb = sb(temps, "comb4", [P, 2 * BANK // P, E], F32)
            R.psG = ps(temps, "psG4", [P, 2, BANK], F32)
            R.psU = ps(temps, "psU4", [P, 2, BANK], F32)
            R.psY = ps(temps, "psY", [P, 2, BANK], F32)
            with nc.Fori(0, NT * P // (2 * BANK)) as i:
                expert_block(nc, M, S, R, i)
        with ExitStack() as temps:
            back_block(nc, M, S, temps, sb, ps, out)


def build(nc, I, out):
    with ExitStack() as top:
        numbers = []

        def sem(name):
            x = top.enter_context(nc.semaphore(name))
            numbers.append(x.num)
            return x

        def sb(stack, name, shape, dt):
            return stack.enter_context(nc.sbuf_tensor(name, shape, dt))

        def ps(stack, name, shape, dt):
            return stack.enter_context(nc.psum_tensor(name, shape, dt))

        S = Box()
        S.scores_ready = sem("scores_ready")
        S.exp_done = sem("exp_done")
        S.lo_dve = sem("lo_dve")
        S.lo_pool = sem("lo_pool")
        S.weighted_done = sem("weighted_done")
        S.out_lo = sem("out_lo")
        S.out_added = sem("out_added")
        S.out_scaled = sem("out_scaled")
        S.aux_ready = sem("aux_ready")
        S.aux_free = [sem(f"aux_free{k}") for k in range(NAUX)]
        S.rope_sum = sem("rope_sum")
        S.rope_hi = sem("rope_hi")
        S.rope_lo = sem("rope_lo")
        S.v_hi = sem("v_hi")
        S.row_max = sem("row_max")
        S.k_out = sem("k_out")
        S.q_out = sem("q_out")
        S.near_in = [sem(f"near_in{i}") for i in range(2)]
        S.far_in = sem("far_in")
        S.row_max_in = sem("row_max_in")
        S.xq_in = sem("xq_in")
        S.xv_in = sem("xv_in")
        S.x_load = [sem(f"x_load{b}") for b in range(B)]
        S.w_in = sem("w_in")
        S.c_in = sem("c_in")
        S.consts = sem("consts")
        S.stats = sem("stats")
        S.var_ready = sem("var_ready")
        S.std_ready = sem("std_ready")
        S.norm_ready = sem("norm_ready")
        S.turned = sem("turned")
        S.turned_out = sem("turned_out")
        S.split_hi = sem("split_hi")
        S.split_lo = sem("split_lo")
        S.step_a = sem("step_a")
        S.step_b = sem("step_b")
        S.step_c = sem("step_c")
        S.step_d = sem("step_d")
        S.step_e = sem("step_e")
        S.step_f = sem("step_f")
        S.step_g = sem("step_g")
        S.step_h = sem("step_h")
        S.stored = sem("stored")
        S.first, S.last = min(numbers), max(numbers)
        M = Box()
        M.ident = sb(top, "ident", [P, P], F32)
        M.y = sb(top, "y", [P, NT, D], F32)
        M.x_way = nc.dram_tensor("x_way", (P, 2, NT * P), F16, kind="Internal").ap()
        M.k_way = nc.dram_tensor("k_way", (4, HALF, GH, T), F16, kind="Internal").ap()
        M.q_way = nc.dram_tensor("q_way", (4, HALF, GH, T), F16, kind="Internal").ap()
        phase_attention(nc, I, M, S, sb, ps)
        phase_ffn(nc, I, M, S, sb, ps, out)


def rotary_table():
    inv = np.float32(1.0) / np.float32(10000.0) ** (np.arange(0, HD, 2, dtype=np.float32) / np.float32(HD))
    angle = np.outer(np.arange(T, dtype=np.float32), inv.astype(np.float32)).astype(np.float32)
    cos, sin = np.cos(angle).astype(np.float32), np.sin(angle).astype(np.float32)
    return (np.ascontiguousarray(np.tile(cos.T, (GH, 1))), np.ascontiguousarray(np.tile(sin.T, (GH, 1))))


def by_halves(w):
    w = w.reshape(GROUPS, GH, 2, HALF, D).transpose(4, 0, 2, 1, 3)
    return np.ascontiguousarray(w.reshape(D, HEADS * HD))


def kernel(**inputs):
    import concourse.bacc as bacc
    from concourse.bass_utils import run_bass_kernel_spmd

    a = {name.removeprefix("L0_ffn_").removeprefix("L0_attn_"): np.asarray(v) for name, v in inputs.items()
         if name != "L0_attn_x"}
    laid = {name: np.ascontiguousarray(v) for name, v in a.items() if name not in ("wq", "wk", "wv", "wo", "gate_w")}
    laid["x"] = np.ascontiguousarray(np.asarray(inputs["L0_attn_x"]))
    laid["wq"], laid["wk"] = by_halves(a["wq"]), by_halves(a["wk"])
    laid["wv"] = np.ascontiguousarray(a["wv"].T)
    laid["wo"] = np.ascontiguousarray(a["wo"].T.reshape(HEADS * HD // P, P, D).transpose(1, 0, 2))
    laid["gate_w"] = np.ascontiguousarray(a["gate_w"].T)
    laid["cos"], laid["sin"] = rotary_table()

    nc = bacc.Bacc("TRN2", target_bir_lowering=False, num_devices=1)
    I = {name: nc.dram_tensor(f"in_{name}", v.shape, mybir.dt.from_np(v.dtype), kind="ExternalInput").ap()
         for name, v in laid.items()}
    out = nc.dram_tensor("out", (B, T, D), F32, kind="ExternalOutput").ap()
    build(nc, I, out)
    r = run_bass_kernel_spmd(nc, [{f"in_{name}": v for name, v in laid.items()}], core_ids=[0])
    return r.results[0]["out"]
```

```python
from contextlib import ExitStack

import numpy as np

import concourse.bass as bass
from concourse import mybir

F32 = mybir.dt.float32
F16 = mybir.dt.float16
BF16 = mybir.dt.bfloat16
ALU = mybir.AluOpType
ACT = mybir.ActivationFunctionType
AX = mybir.AxisListType

P = 128
B, T, D = 4, 1024, 128
HEADS, HD = 16, 64
HALF = HD // 2
GH = P // HALF
GROUPS = HEADS // GH
TT = T // P
NT = B * TT
CH = GH * HD // P
BANK = 512
SCALE = float(HD) ** -0.5
EPS = 1e-5
NEG = -1.0e30
MSCALE = 64.0
VW = 2 * HD + 2
E, TOPK, H = 8, 4, 128
SH = 2 * H
NC = SH // H
KB = 4

UNITS = [(j, max(j * P, half * BANK), (half + 1) * BANK - max(j * P, half * BANK))
         for half in range(T // BANK) for j in range((half + 1) * BANK // P)]
NU = len(UNITS)
SU = NU * GH
PAIR_END = {max(i for i, (j, c, w) in enumerate(UNITS) if j == 2 * q + 1 and c <= (2 * q + 1) * P < c + w): q
            for q in range(TT // 2)}
MAXP = [(t, c, min(BANK, (t + 1) * P - c)) for t in range(TT) for c in range(0, (t + 1) * P, BANK)]
LO_LAG = 0
LAG = 3
NP_ = 4
ROPE_LAG = 6
SUM_LAG = 2
REST_LAG = 6
QK_STEPS = (0, 2, 9, 11, 18, 20, 27, 29)
V_STEPS = (5, 20, 27, 43)
MX_FIRST, MX_LAST, MT_STEP = 8, 43, 45
TR1_STEPS, WO_STEPS, TR0_STEPS = (11, 15), (17, 19), (36, 37)
LO_POOL = (1,)
LO_OF = 2
SCALE_FIRST = False
PE_SIDE_FIRST = True
ACT_OUT_FIRST = True
ACT_LAG = 1
DVE_ORDER = 'slo'
SCALE_LAG = 2
OUT_LAG = 1
NO = 4
NAUX = 3


def plan(slots, near, far):
    at = {}

    def put(slot, step, item):
        at.setdefault((slot, step), []).append((slot,) + item)

    for s in slots:
        w = s >= 0
        if s > 0:
            for half in range(2):
                put(s, TR1_STEPS[half], ("tr", 1, half))
                put(s, WO_STEPS[half], ("wo", half))
        if s in far:
            for r in range(8):
                put(s, w * QK_STEPS[r], ("qk", r // 4, r // 2 % 2, r % 2))
        if s in near:
            for tp in range(TT // 2):
                put(s, w * V_STEPS[tp], ("v", tp))
            for h in range(GH):
                for k in range(len(MAXP)):
                    at_step = MX_FIRST + (h * len(MAXP) + k) * (MX_LAST - MX_FIRST) // (GH * len(MAXP) - 1)
                    put(s, w * at_step, ("mx", h, k))
            put(s, w * MT_STEP, ("mt",))
        if s >= 0:
            for half in range(2):
                put(s, TR0_STEPS[half], ("tr", 0, half))
    if slots[-1] == GROUPS - 1:
        for item in [("tr", 1, 0), ("tr", 1, 1), ("wo", 0), ("wo", 1)]:
            put(GROUPS, LAG + max(OUT_LAG, SCALE_LAG), item)
    steps = []
    number = {}
    for s in slots:
        for u in range(SU if s >= 0 else 1):
            steps.append((s, u))
    if slots[-1] == GROUPS - 1:
        steps += [(GROUPS, u) for u in range(LAG + max(OUT_LAG, SCALE_LAG) + 1)]
    for key in steps:
        for item in at.get(key, []):
            number[item] = len(number)
    assert sum(len(v) for v in at.values()) == len(number)
    return steps, at, number


def lo_on_pool(u):
    return u % LO_OF in LO_POOL


class Box:
    pass


class Counts:

    def __init__(self):
        self.pool, self.dve = [], []
        p = d = 0
        for k in range(SU * GROUPS):
            if lo_on_pool(k % SU):
                p += 1
            else:
                d += 1
            self.pool.append(p)
            self.dve.append(d)


COUNTS = Counts()


def attention_block(nc, M, S, b, slots, near, far):
    steps, at, number = plan(slots, near, far)
    first = slots[0]

    def loads(s):
        return sum(x in near for x in slots if x <= s)

    def ropes(s):
        return sum(x in far for x in slots if x < s)

    def bank(item):
        return number[item] % NAUX

    def taken(eng, item):
        eng.wait_ge(S.aux_free[bank(item)], number[item] // NAUX + 1)

    def ready(eng, item):
        eng.wait_ge(S.aux_ready, number[item] + 1)

    def free(item):
        return S.aux_free[bank(item)]

    def parts(U):
        return U // SU, (U % SU) // NU, U % NU

    def wait_lo(eng, U):
        if lo_on_pool(U % SU):
            eng.wait_ge(S.lo_pool, COUNTS.pool[U])
        else:
            eng.wait_ge(S.lo_dve, COUNTS.dve[U])

    last_unit = SU * len(slots) - 1 if slots[0] >= 0 else -1

    def pairs_at(s, u, lag=0):
        U = SU * s + u - LAG - lag
        if s >= 0 and 0 <= U <= last_unit and U % NU in PAIR_END:
            return [(U, 4 * (U // NU) + PAIR_END[U % NU])]
        return []

    with nc.Block() as blk:

        @blk.tensor
        def _(pe):
            def scores(U):
                s, h, u = parts(U)
                j, c, w = UNITS[u]
                p = s % 2
                if u == 0 and h == 0 and s > 0:
                    pe.wait_ge(S.row_max_in, 16 * s)
                    pe.wait_ge(S.far_in, 32 * s)
                if U >= 2:
                    pe.wait_ge(S.exp_done, U - 1)
                diagonal = c == j * P
                out = M.psS[:, U % 2, 0:w]
                nc.tensor.matmul(out, M.K1[:, p, h, j * P:(j + 1) * P], M.Q1[:, p, h, c:c + w],
                                 start=True, stop=False)
                mm = nc.tensor.matmul(out, M.K2[0:HD + 1, p, h, j * P:(j + 1) * P],
                                      M.Q2[0:HD + 1, p, h, c:c + w], start=False, stop=not diagonal)
                if diagonal:
                    mm = nc.tensor.matmul(out[:, 0:P], M.ident16[:], M.maskT[:], start=False, stop=True)
                mm.then_inc(S.scores_ready, 1)

            def weighted(U):
                s, h, u = parts(U)
                j, c, w = UNITS[u]
                wait_lo(pe, U)
                for k in range(w // P):
                    t = c // P + k
                    n = 4 * (U // NU) + t // 2
                    first = j == 0 and t % 2 == 0
                    if first and n >= 3:
                        pe.wait_ge(S.out_added, n - 2)
                    O = M.psO[:, n % 3, 256 * (t % 2):256 * (t % 2) + 2 * HD + 1]
                    nc.tensor.matmul(O, M.Phi[:, U % NP_, k * P:(k + 1) * P], M.V[:, s % 2, j, h, 0:2 * HD + 1],
                                     start=first, stop=False, skip_group_check=True)
                    mm = nc.tensor.matmul(O[:, HD:2 * HD + 1], M.Plo[:, U % NP_, k * P:(k + 1) * P],
                                          M.V[:, s % 2, j, h, HD:2 * HD + 1],
                                          start=False, stop=j == t, skip_group_check=True)
                mm.then_inc(S.weighted_done, 1)

            def side(item):
                s, kind, *a = item
                X = M.psX[:, bank(item), :]
                g = (s + (2 if kind == "qk" else 1)) % GROUPS
                p = (s + 1) % 2
                if number[item] >= NAUX:
                    pe.wait_ge(S.aux_free[bank(item)], number[item] // NAUX)
                if kind == "qk":
                    which, n, half = a
                    if s == GROUPS - 2 and which == 0 and n == 0 and half == 0:
                        pe.wait_ge(S.xq_in, 16)
                    cols = (2 * g + half) * P
                    w = M.wkq[:, which]
                    for k, (wi, xi) in enumerate([(0, 0), (0, 1), (1, 0)]):
                        mm = nc.tensor.matmul(X, w[:, wi, cols:cols + P], M.xq[:, xi, n * BANK:(n + 1) * BANK],
                                              start=k == 0, stop=k == 2)
                elif kind == "v":
                    if s == GROUPS - 1 and a[0] == 0:
                        pe.wait_ge(S.xv_in, 16)
                    for k in range(2):
                        t = 2 * a[0] + k
                        for i, (wi, xi) in enumerate([(0, 0), (1, 0), (0, 1)]):
                            mm = nc.tensor.matmul(X[:, k * 256:(k + 1) * 256], M.xv[:, xi, t * P:(t + 1) * P],
                                                  M.wv[:, wi, g * 256:(g + 1) * 256],
                                                  start=i == 0, stop=i == 2)
                elif kind == "mx":
                    h, k = a
                    t, c, w = MAXP[k]
                    if k == 0 and h % 2 == 0:
                        pe.wait_ge(S.near_in[h // 2], 48 * loads(s))
                    diagonal = c + w == (t + 1) * P
                    mm = nc.tensor.matmul(X[:, 0:w], M.Q1[:, p, h, t * P:(t + 1) * P], M.K1[:, p, h, c:c + w],
                                          start=True, stop=not diagonal)
                    if diagonal:
                        mm = nc.tensor.matmul(X[:, w - P:w], M.ident16[:], M.maskN[:], start=False, stop=True)
                elif kind == "mt":
                    pe.wait_ge(S.row_max, loads(s))
                    mm = nc.tensor.transpose(X[0:GH * TT, 0:P], M.rmax[:], M.ident[:])
                elif kind == "tr":
                    c, half = a
                    own = s - 1 if c == 1 else s
                    if half == 0:
                        pe.wait_ge(S.out_scaled, 4 * (GH * own + 2 * (c + 1)))
                    for k in range(4):
                        mm = nc.tensor.transpose(X[:, k * P:(k + 1) * P],
                                                 M.On[:, 4 * half + k, c * P:(c + 1) * P], M.ident[:])
                elif kind == "wo":
                    half = a[0]
                    og = s - 1
                    taken(pe, (og, "tr", 0, half))
                    taken(pe, (s, "tr", 1, half))
                    for k in range(4):
                        for c in range(CH):
                            t = 4 * half + k
                            mm = nc.tensor.matmul(X[:, k * P:(k + 1) * P], M.OT[:, c, t * P:(t + 1) * P],
                                                  M.wo[:, CH * og + c, :], start=c == 0, stop=c == CH - 1)
                mm.then_inc(S.aux_ready, 1)

            for s, u in steps:
                U = SU * s + u
                if 0 <= U <= last_unit:
                    scores(U)
                if PE_SIDE_FIRST or s < 0:
                    for item in at.get((s, u), []) if s < GROUPS else []:
                        side(item)
                if s >= 0 and 0 <= U - LAG <= last_unit:
                    weighted(U - LAG)
                if not PE_SIDE_FIRST and s >= 0:
                    for item in at.get((s, u), []) if s < GROUPS else []:
                        side(item)
                for item in at.get((s, u), []) if s == GROUPS else []:
                    side(item)

        @blk.scalar
        def _(act):
            def exps(U):
                w = UNITS[U % NU][2]
                act.wait_ge(S.scores_ready, U + 1)
                if U >= NP_:
                    wait_lo(act, U - NP_)
                    act.wait_ge(S.weighted_done, U - NP_ + 1)
                nc.scalar.activation(M.P32[:, U % NP_, 0:w], M.psS[:, U % 2, 0:w], ACT.Exp, scale=SCALE)
                nc.scalar.activation(M.Phi[:, U % NP_, 0:w], M.psS[:, U % 2, 0:w], ACT.Exp,
                                     scale=SCALE).then_inc(S.exp_done, 1)

            def side(item):
                s, kind, *a = item
                X = M.psX[:, bank(item), :]
                p = (s + 1) % 2
                if kind == "qk" and a[2] == 1:
                    which, n, _ = a
                    r = 4 * ropes(s) + 2 * which + n
                    act.wait_ge(S.rope_sum, r + 1)
                    if ropes(s) > 0 and n == 0:
                        act.wait_ge(S.q_out if which else S.k_out, 16 * GH * ropes(s))
                    nc.scalar.copy(M.HL[:, which, 0:2, n * BANK:(n + 1) * BANK], M.R[:]).then_inc(S.rope_hi, 1)
                elif kind == "v":
                    ready(act, item)
                    if s > 0 and a[0] == 0:
                        act.wait_ge(S.weighted_done, SU * s)
                    nc.scalar.copy(M.V[:, p, 2 * a[0]:2 * a[0] + 2, :, HD:2 * HD],
                                   X.rearrange("p (t h d) -> p t h d", t=2, h=GH)).then_inc(S.v_hi, 1)
                elif kind == "mt":
                    ready(act, item)
                    if s > 0:
                        act.wait_ge(S.row_max_in, 16 * s)
                    nc.scalar.activation(M.mrow[:], X[0:GH * TT, 0:P], ACT.Copy, scale=1.0 / MSCALE).then_inc(free(item), 1)
                elif kind == "tr":
                    ready(act, item)
                    og = s - 1 if a[0] == 0 else s - 2
                    if og >= 0:
                        ready(act, (og + 1, "wo", 1))
                    nc.scalar.copy(M.OT[:, a[0], a[1] * BANK:(a[1] + 1) * BANK], X).then_inc(free(item), 1)

            def out_lo(Uw, n):
                O = M.psO[:, n % 3, :].rearrange("p (t c) -> p t c", t=2)
                act.wait_ge(S.weighted_done, Uw + 1)
                if n >= NO:
                    act.wait_ge(S.out_added, n - NO + 1)
                nc.scalar.copy(M.Olo[:, n % NO], O[:, :, 0:HD]).then_inc(S.out_lo, 1)

            for s, u in steps:
                U = SU * s + u
                if 0 <= U <= last_unit:
                    exps(U)
                if s == GROUPS:
                    for Uw, n in pairs_at(s, u, ACT_LAG):
                        out_lo(Uw, n)
                if s < GROUPS and ACT_OUT_FIRST:
                    for Uw, n in pairs_at(s, u, ACT_LAG):
                        out_lo(Uw, n)
                for item in at.get((s, u), []):
                    if s < 0 or item[1] != "qk":
                        side(item)
                for item in at.get((s, u - ROPE_LAG), []):
                    if s >= 0 and item[1] == "qk":
                        side(item)
                if s < GROUPS and not ACT_OUT_FIRST:
                    for Uw, n in pairs_at(s, u, ACT_LAG):
                        out_lo(Uw, n)

        @blk.vector
        def _(dve):
            def low(U):
                w = UNITS[U % NU][2]
                dve.wait_ge(S.exp_done, U + 1)
                nc.vector.tensor_tensor(M.Plo[:, U % NP_, 0:w], M.P32[:, U % NP_, 0:w], M.Phi[:, U % NP_, 0:w],
                                        ALU.subtract).then_inc(S.lo_dve, 1)

            def side(item):
                s, kind, *a = item
                X = M.psX[:, bank(item), :]
                p = (s + 1) % 2
                if kind == "qk":
                    which, n, half = a
                    r = 4 * ropes(s) + 2 * which + n
                    cols = slice(n * BANK, (n + 1) * BANK)
                    ready(dve, item)
                    if half == 0:
                        if r > 0:
                            dve.wait_ge(S.rope_sum, r)
                        nc.vector.tensor_tensor(M.R4[:, 0, :], X, M.cos[:, cols], ALU.mult)
                        nc.vector.tensor_tensor(M.R4[:, 2, :], X, M.sin[:, cols], ALU.mult).then_inc(free(item), 1)
                    else:
                        nc.vector.tensor_tensor(M.R4[:, 1, :], X, M.sin[:, cols], ALU.mult)
                        nc.vector.tensor_tensor(M.R4[:, 3, :], X, M.cos[:, cols], ALU.mult).then_inc(free(item), 1)
                elif kind == "v":
                    dve.wait_ge(S.v_hi, 4 * (loads(s) - 1) + a[0] + 1)
                    nc.vector.tensor_tensor(M.V[:, p, 2 * a[0]:2 * a[0] + 2, :, 0:HD],
                                            X.rearrange("p (t h d) -> p t h d", t=2, h=GH),
                                            M.V[:, p, 2 * a[0]:2 * a[0] + 2, :, HD:2 * HD],
                                            ALU.subtract).then_inc(free(item), 1)
                elif kind == "mx":
                    h, k = a
                    t, c, w = MAXP[k]
                    ready(dve, item)
                    nc.vector.tensor_reduce(M.pmax[:, int(c > 0), h, t:t + 1], X[:, 0:w], AX.X, ALU.max,
                                            negate=True).then_inc(free(item), 1)
                    if h == GH - 1 and k == len(MAXP) - 1:
                        taken(dve, item)
                        if s > 0:
                            ready(dve, (s - 1, "mt"))
                        nc.vector.tensor_tensor(M.rmax[:], M.pmax[:, 0].rearrange("p h t -> p (h t)"),
                                                M.pmax[:, 1].rearrange("p h t -> p (h t)"),
                                                ALU.min).then_inc(S.row_max, 1)
                elif kind == "wo":
                    ready(dve, item)
                    y = M.y[:, bass.ds(b * TT + 4 * a[0], 4), :].rearrange("p t d -> p (t d)")
                    if s == 1:
                        nc.vector.tensor_copy(y, X).then_inc(free(item), 1)
                    else:
                        taken(dve, (s - 1, "wo", a[0]))
                        nc.vector.tensor_tensor(y, X, y, ALU.add).then_inc(free(item), 1)

            def out_add(Uw, n):
                O = M.psO[:, n % 3, :].rearrange("p (t c) -> p t c", t=2)
                dve.wait_ge(S.out_lo, n + 1)
                if n >= NO:
                    dve.wait_ge(S.out_scaled, n - NO + 1)
                nc.vector.reciprocal(M.rsum[:, n % NO, :, :], O[:, :, 2 * HD:2 * HD + 1])
                nc.vector.tensor_tensor(M.Osum[:, n % NO], O[:, :, HD:2 * HD], M.Olo[:, n % NO],
                                        ALU.add).then_inc(S.out_added, 1)

            for s, u in steps:
                U = SU * s + u - LO_LAG
                for what in DVE_ORDER:
                    if what == "s":
                        for item in at.get((s, u), []) if s < GROUPS else []:
                            side(item)
                    if what == "l":
                        if s >= 0 and 0 <= U <= last_unit and not lo_on_pool(U % SU):
                            low(U)
                    if what == "o":
                        for Uw, n in pairs_at(s, u, OUT_LAG):
                            out_add(Uw, n)
                for item in at.get((s, u), []) if s == GROUPS else []:
                    side(item)

        @blk.gpsimd
        def _(pool):
            def low(U):
                w = UNITS[U % NU][2]
                pool.wait_ge(S.exp_done, U + 1)
                nc.gpsimd.tensor_tensor(M.Plo[:, U % NP_, 0:w], M.P32[:, U % NP_, 0:w], M.Phi[:, U % NP_, 0:w],
                                        ALU.subtract).then_inc(S.lo_pool, 1)

            def rotate(item, second):
                s, kind, *a = item
                if kind != "qk" or a[2] == 0:
                    return
                which, n, _ = a
                r = 4 * ropes(s) + 2 * which + n
                cols = slice(n * BANK, (n + 1) * BANK)
                if not second:
                    taken(pool, item)
                    if r > 0:
                        pool.wait_ge(S.rope_lo, r)
                    nc.gpsimd.tensor_tensor(M.R[:, 0, :], M.R4[:, 0, :], M.R4[:, 1, :], ALU.subtract)
                    nc.gpsimd.tensor_tensor(M.R[:, 1, :], M.R4[:, 2, :], M.R4[:, 3, :],
                                            ALU.add).then_inc(S.rope_sum, 1)
                    return
                pool.wait_ge(S.rope_hi, r + 1)
                nc.gpsimd.tensor_tensor(M.HL[:, which, 2:4, cols], M.R[:], M.HL[:, which, 0:2, cols],
                                        ALU.subtract).then_inc(S.rope_lo, 1)

            def out_scale(n):
                head = n // 4
                h, q = head % GH, n % 4
                pool.wait_ge(S.out_added, n + 1)
                own = head // GH
                if q == 0 and h % 2 == 0 and own > 0:
                    ready(pool, (own - 1, "tr", 0, 1) if h == 0 else (own, "tr", 1, 1))
                nc.gpsimd.tensor_tensor(M.On[:, 2 * q:2 * q + 2, h * HD:(h + 1) * HD], M.Osum[:, n % NO],
                                        M.rsum[:, n % NO].to_broadcast([P, 2, HD]),
                                        ALU.mult).then_inc(S.out_scaled, 1)

            for s, u in steps:
                U = SU * s + u - LO_LAG
                if s >= 0 and 0 <= U <= last_unit and lo_on_pool(U % SU):
                    low(U)
                if SCALE_FIRST:
                    for _, n in pairs_at(s, u, SCALE_LAG):
                        out_scale(n)
                for item in at.get((s, u), []) if s < 0 else []:
                    rotate(item, False)
                    rotate(item, True)
                if s >= 0:
                    for item in at.get((s, u - SUM_LAG), []):
                        rotate(item, False)
                    for item in at.get((s, u - REST_LAG), []):
                        rotate(item, True)
                if not SCALE_FIRST:
                    for _, n in pairs_at(s, u, SCALE_LAG):
                        out_scale(n)

        @blk.sync
        def _(sp):
            def load(s):
                p = (s + 1) % 2
                if s > 0:
                    sp.wait_ge(S.scores_ready, SU * s)
                krows = M.k_way.rearrange("k f h n -> (k f) h n")
                qrows = M.q_way.rearrange("k f h n -> (k f) h n")
                if s > first:
                    sp.wait_ge(S.k_out, 16 * GH * ropes(s))
                    sp.wait_ge(S.q_out, 16 * GH * ropes(s))
                for i in range(2):
                    h = slice(2 * i, 2 * i + 2)
                    sp.dma_start(M.K1[:, p, h], krows[:, h]).then_inc(S.near_in[i], 16)
                    sp.dma_start(M.Q1[0:HD, p, h], qrows[0:HD, h]).then_inc(S.near_in[i], 16)
                    sp.dma_start(M.Q1[HD:P, p, h], qrows[0:HD, h]).then_inc(S.near_in[i], 16)
                sp.dma_start(M.K2[0:HD, p], krows[0:HD]).then_inc(S.far_in, 16)
                sp.dma_start(M.Q2[0:HD, p], qrows[HD:P]).then_inc(S.far_in, 16)

            def send(s, which):
                way, sent = (M.q_way, S.q_out) if which else (M.k_way, S.k_out)
                sp.wait_ge(S.rope_lo, 4 * ropes(s) + 2 * which + 2)
                if which == 0 and loads(s) > 0:
                    for i in range(2):
                        sp.wait_ge(S.near_in[i], 48 * loads(s))
                    sp.wait_ge(S.far_in, 32 * loads(s))
                for h in range(GH):
                    sp.dma_start(way[:, :, h, :].rearrange("k f n -> f k n"),
                                 M.HL[h * HALF:(h + 1) * HALF, which, :, :]).then_inc(sent, 16)

            for s in slots:
                if s in near:
                    load(s)
                if s in far:
                    send(s, 0)
                    send(s, 1)
                    if s == GROUPS - 3 and s + 1 in far:
                        ready(sp, (s, "qk", 1, 1, 1))
                        sp.dma_start(M.xq[:], M.x_way[:, :, bass.ds((b + 1) * T, T)]).then_inc(S.xq_in, 16)
                if s in near:
                    taken(sp, (s, "mt"))
                    sp.dma_start(M.Q2[HD:HD + 1, (s + 1) % 2, :, :].rearrange("o h (t i) -> o (h t) i", i=P),
                                 M.mrow[:]).then_inc(S.row_max_in, 16)
                    if s == GROUPS - 2 and s + 1 in near:
                        ready(sp, (s, "v", TT // 2 - 1))
                        sp.dma_start(M.xv[:], M.x_way[:, :, bass.ds((b + 1) * T, T)]).then_inc(S.xv_in, 16)
            if far:
                sp.wait_ge(S.k_out, 16 * GH * len(far))
                sp.wait_ge(S.q_out, 16 * GH * len(far))
            sp.wait_ge(S.far_in, 32 * len(near))
            sp.wait_ge(S.row_max_in, 16 * len(near))


def block_end(nc, S):
    nc.sync.sem_clear(range(S.first, S.last + 1))
    nc.all_engine_barrier()


def load_block(nc, I, M, S, stack, sb, ps):
    xs = sb(stack, "xs", [P, NT, D], F32)
    xn = sb(stack, "xn", [P, NT, D], F32)
    xT = sb(stack, "xT", [P, 2, NT * P], F16)
    w32 = sb(stack, "w32", [P, 3, HEADS * HD], F32)
    bn = sb(stack, "bn", [P, NT, 6], F32)
    mv = sb(stack, "mv", [P, NT, 2], F32)
    std = sb(stack, "std", [P, NT], F32)
    rstd = sb(stack, "rstd", [P, NT], F32)
    psT = ps(stack, "psT", [P, 2, BANK], F32)
    NB = NT * P // BANK
    x_tiles = I["x"].rearrange("b (t p) d -> p (b t) d", p=P)
    with nc.Block() as blk:
        @blk.sync
        def _(sp):
            for b in range(B):
                sp.dma_start(xs[:, b * TT:(b + 1) * TT, :], x_tiles[:, b * TT:(b + 1) * TT, :]).then_inc(S.x_load[b], 16)
            for k, w in enumerate((I["wk"], I["wq"], I["wv"])):
                sp.dma_start(w32[:, k, :], w).then_inc(S.w_in, 16)
            sp.dma_start(M.wo[:], I["wo"]).then_inc(S.c_in, 16)
            sp.dma_start(M.cos[:], I["cos"]).then_inc(S.c_in, 16)
            sp.dma_start(M.sin[:], I["sin"]).then_inc(S.c_in, 16)
            for k in range(NB):
                sp.wait_ge(S.split_lo, k + 1)
                cols = slice(k * BANK, (k + 1) * BANK)
                sp.dma_start(M.x_way[:, :, cols], xT[:, :, cols]).then_inc(S.stored, 16)
            sp.wait_ge(S.stored, 16 * NB)
            sp.wait_ge(S.c_in, 48)

        @blk.gpsimd
        def _(pool):
            nc.gpsimd.memset(M.ident[:], 0.0)
            nc.gpsimd.memset(M.ident16[:], 0.0)
            nc.gpsimd.memset(M.maskT[:], 0.0)
            nc.gpsimd.memset(M.maskN[:], 0.0).then_inc(S.consts, 1)
            pool.wait_ge(S.consts, 1)
            for t in (M.ident, M.ident16):
                nc.gpsimd.affine_select(out=t[:], in_=t[:], compare_op=ALU.not_equal, fill=1.0, base=0,
                                        pattern=[[-1, P]], channel_multiplier=1)
            nc.gpsimd.affine_select(out=M.maskT[:], in_=M.maskT[:], compare_op=ALU.is_ge, fill=NEG, base=0,
                                    pattern=[[1, P]], channel_multiplier=-1)
            nc.gpsimd.affine_select(out=M.maskN[:], in_=M.maskN[:], compare_op=ALU.is_ge, fill=NEG, base=0,
                                    pattern=[[-1, P]], channel_multiplier=1).then_inc(S.consts, 1)

        @blk.vector
        def _(dve):
            for b in range(B):
                dve.wait_ge(S.x_load[b], 16)
                for t in range(b * TT, (b + 1) * TT):
                    last = nc.vector.bn_stats(bn[:, t, :], xs[:, t, :])
            last.then_inc(S.stats, 1)
            dve.wait_ge(S.stats, 1)
            for t in range(NT):
                last = nc.vector.bn_aggr(mv[:, t, :], bn[:, t, :])
            last.then_inc(S.stats, 1)
            dve.wait_ge(S.stats, 2)
            nc.vector.tensor_scalar(std[:], mv[:, :, 1], EPS, None, ALU.add).then_inc(S.var_ready[0], 1)
            dve.wait_ge(S.std_ready[0], 1)
            nc.vector.reciprocal(rstd[:], std[:]).then_inc(S.stats, 1)
            dve.wait_ge(S.stats, 3)
            for t in range(NT):
                nc.vector.tensor_scalar(xn[:, t, :], xs[:, t, :], mv[:, t, 0:1], rstd[:, t:t + 1],
                                        ALU.subtract, ALU.mult).then_inc(S.norm_ready, 1)
            for k in range(NB):
                dve.wait_ge(S.split_hi, k + 1)
                cols = slice(k * BANK, (k + 1) * BANK)
                nc.vector.tensor_tensor(xT[:, 1, cols], psT[:, k % 2, :], xT[:, 0, cols],
                                        ALU.subtract).then_inc(S.split_lo, 1)
            for k, dst in enumerate((M.wkq[:, 0], M.wkq[:, 1], M.wv)):
                dve.wait_ge(S.split_hi, NB + k + 1)
                last = nc.vector.tensor_tensor(dst[:, 1, :], w32[:, k, :], dst[:, 0, :], ALU.subtract)

        @blk.scalar
        def _(act):
            act.wait_ge(S.var_ready[0], 1)
            nc.scalar.activation(std[:], std[:], ACT.Sqrt).then_inc(S.std_ready[0], 1)
            for k in range(NB):
                act.wait_ge(S.turned, k + 1)
                nc.scalar.copy(xT[:, 0, k * BANK:(k + 1) * BANK], psT[:, k % 2, :]).then_inc(S.split_hi, 1)
            act.wait_ge(S.w_in, 48)
            for k, dst in enumerate((M.wkq[:, 0], M.wkq[:, 1], M.wv)):
                nc.scalar.copy(dst[:, 0, :], w32[:, k, :]).then_inc(S.split_hi, 1)

        @blk.tensor
        def _(pe):
            pe.wait_ge(S.consts, 2)
            for k in range(NB):
                pe.wait_ge(S.norm_ready, 4 * k + 4)
                if k >= 2:
                    pe.wait_ge(S.split_lo, k - 1)
                for i in range(4):
                    mm = nc.tensor.transpose(psT[:, k % 2, i * P:(i + 1) * P], xn[:, 4 * k + i, :], M.ident[:])
                mm.then_inc(S.turned, 1)
    block_end(nc, S)


def init_block(nc, M, S):
    with nc.Block() as blk:
        @blk.vector
        def _(dve):
            nc.vector.memset(M.K2[HD:HD + 1], MSCALE)
            nc.vector.memset(M.V[:, :, :, :, 2 * HD:2 * HD + 1].rearrange("p a t h o -> p (a t h) o"), 1.0)
            nc.vector.memset(M.pmax[:], 3.0e38)

        @blk.sync
        def _(sp):
            sp.dma_start(M.xq[:], M.x_way[:, :, 0:T]).then_inc(S.xq_in, 16)
            sp.dma_start(M.xv[:], M.x_way[:, :, 0:T]).then_inc(S.xv_in, 16)
            sp.wait_ge(S.xq_in, 16)
            sp.wait_ge(S.xv_in, 16)
    block_end(nc, S)


def phase_attention(nc, I, M, S, sb, ps):
    with ExitStack() as stack:
        M.wkq = sb(stack, "wkq", [P, 2, 2, HEADS * HD], F16)
        M.wv = sb(stack, "wv", [P, 2, HEADS * HD], F16)
        M.wo = sb(stack, "wo", [P, HEADS * HD // P, D], F32)
        M.cos = sb(stack, "cos", [P, T], F32)
        M.sin = sb(stack, "sin", [P, T], F32)
        M.ident16 = sb(stack, "ident16", [P, P], BF16)
        M.maskT = sb(stack, "maskT", [P, P], BF16)
        M.maskN = sb(stack, "maskN", [P, P], BF16)
        with ExitStack() as temps:
            load_block(nc, I, M, S, temps, sb, ps)
        M.K1 = sb(stack, "K1", [P, 2, GH, T], F16)
        M.Q1 = sb(stack, "Q1", [P, 2, GH, T], F16)
        M.K2 = sb(stack, "K2", [P, 2, GH, T], F16)
        M.Q2 = sb(stack, "Q2", [P, 2, GH, T], F16)
        M.V = sb(stack, "V", [P, 2, TT, GH, VW], F16)
        M.P32 = sb(stack, "P32", [P, NP_, BANK], F32)
        M.Phi = sb(stack, "Phi", [P, NP_, BANK], F16)
        M.Plo = sb(stack, "Plo", [P, NP_, BANK], F16)
        M.R4 = sb(stack, "R4", [P, 4, BANK], F32)
        M.R = sb(stack, "R", [P, 2, BANK], F32)
        M.HL = sb(stack, "HL", [P, 2, 4, T], F16)
        M.On = sb(stack, "On", [P, TT, GH * HD], F32)
        M.OT = sb(stack, "OT", [P, CH, T], F32)
        M.Olo = sb(stack, "Olo", [P, NO, 2, HD], F32)
        M.Osum = sb(stack, "Osum", [P, NO, 2, HD], F32)
        M.rsum = sb(stack, "rsum", [P, NO, 2, 1], F32)
        M.pmax = sb(stack, "pmax", [P, 2, GH, TT], F32)
        M.rmax = sb(stack, "rmax", [P, GH * TT], F32)
        M.mrow = sb(stack, "mrow", [GH * TT, P], F16)
        M.xq = sb(stack, "xq", [P, 2, T], F16)
        M.xv = sb(stack, "xv", [P, 2, T], F16)
        M.psS = ps(stack, "psS", [P, 2, BANK], F32)
        M.psO = ps(stack, "psO", [P, 3, BANK], F32)
        M.psX = ps(stack, "psX", [P, NAUX, BANK], F32)
        init_block(nc, M, S)
        attention_block(nc, M, S, 0, [-2, -1], [-1], [-2, -1])
        block_end(nc, S)
        slots = list(range(GROUPS))
        with nc.Fori(0, B - 1) as b:
            attention_block(nc, M, S, b, slots, slots, slots)
            block_end(nc, S)
        attention_block(nc, M, S, B - 1, slots, slots[:-1], slots[:-2])
        block_end(nc, S)


def norm_block(nc, I, M, S, stack, sb, ps):
    zn = sb(stack, "zn", [P, 2, NT, D], F32)
    bn = sb(stack, "bn3", [P, 2, NT, 6], F32)
    mv = sb(stack, "mv3", [P, 2, NT, 2], F32)
    std = sb(stack, "std3", [P, 2, NT], F32)
    rstd = sb(stack, "rstd3", [P, 2, NT], F32)
    shift = sb(stack, "shift3", [P, NT], F32)
    zT = sb(stack, "zT", [P, 2, BANK], F32)
    psT = ps(stack, "psT3", [P, 2, BANK], F32)
    psH = ps(stack, "psH3", [P, 2, BANK], F32)
    x_tiles = I["x"].rearrange("b (t p) d -> p (b t) d", p=P)
    TB = BANK // P
    NB = NT // TB
    CT = 2 * TB
    NCH = NT // CT
    with nc.Block() as blk:
        @blk.sync
        def _(sp):
            for c in range(NCH):
                tiles = slice(c * CT, (c + 1) * CT)
                sp.dma_start(M.x1[:, tiles], x_tiles[:, tiles]).then_inc(S.x_load[c], 16)
            sp.dma_start(M.wd[:, 0, :], I["lin0_w"]).then_inc(S.lin0_in, 16)
            sp.dma_start(M.bias[:, 0:1], I["lin0_b"].rearrange("(d o) -> d o", o=1)).then_inc(S.lin0_in, 16)
            for k, w in enumerate((I["swi1_w1"], I["swi1_w2"], I["lin1_w"], I["swi2_w1"], I["swi2_w2"])):
                sp.dma_start(M.wd[:, k + 1, :], w).then_inc(S.w_in, 16)
            for k, w in enumerate((I["swi1_b1"], I["swi1_b2"], I["lin1_b"], I["swi2_b1"], I["swi2_b2"])):
                sp.dma_start(M.bias[:, k + 1:k + 2], w.rearrange("(d o) -> d o", o=1)).then_inc(S.w_in, 16)
            sp.dma_start(M.gate[:], I["gate_w"]).then_inc(S.w_in, 16)
            sp.dma_start(M.we[:, 0, 0:E], I["exp_w1"].rearrange("e d h -> d e h")).then_inc(S.w_in, 16)
            sp.dma_start(M.we[:, 1, 0:E], I["exp_w3"].rearrange("e d h -> d e h")).then_inc(S.w_in, 16)
            sp.dma_start(M.we[:, 2, 0:E], I["exp_w2"].rearrange("e h d -> h e d")).then_inc(S.w_in, 16)
            sp.dma_start(M.we[:, 0, E:E + NC], I["sh_w1"].rearrange("d (c h) -> d c h", h=H)).then_inc(S.w_in, 16)
            sp.dma_start(M.we[:, 1, E:E + NC], I["sh_w3"].rearrange("d (c h) -> d c h", h=H)).then_inc(S.w_in, 16)
            sp.dma_start(M.we[:, 2, E:E + NC], I["sh_w2"].rearrange("(c h) d -> h c d", h=H)).then_inc(S.w_in, 16)
            sp.wait_ge(S.w_in, 16 * 17)

        @blk.vector
        def _(dve):
            done = [0]

            def then(ins):
                done[0] += 1
                ins.then_inc(S.stats, 1)
                dve.wait_ge(S.stats, done[0])

            def variance(i, c):
                if i == 1:
                    dve.wait_ge(S.x1_ready, CT * (c + 1))
                tiles = range(c * CT, (c + 1) * CT)
                src = (M.y, M.x1)[i]
                for t in tiles:
                    last = nc.vector.bn_stats(bn[:, i, t, :], src[:, t, :])
                then(last)
                for t in tiles:
                    last = nc.vector.bn_aggr(mv[:, i, t, :], bn[:, i, t, :])
                then(last)
                tiles = slice(c * CT, (c + 1) * CT)
                nc.vector.tensor_scalar(std[:, i, tiles], mv[:, i, tiles, 1], EPS, None,
                                        ALU.add).then_inc(S.var_ready[i], 1)

            def inverse(i, c):
                tiles = slice(c * CT, (c + 1) * CT)
                dve.wait_ge(S.std_ready[i], c + 1)
                then(nc.vector.reciprocal(rstd[:, i, tiles], std[:, i, tiles]))
                if i == 1:
                    for t in range(c * CT, (c + 1) * CT):
                        nc.vector.tensor_scalar(zn[:, 1, t, :], M.x1[:, t, :], mv[:, 1, t, 0:1], rstd[:, 1, t:t + 1],
                                                ALU.subtract, ALU.mult).then_inc(S.normal_ready[1], 1)
                    return
                nc.vector.scalar_tensor_tensor(out=shift[:, tiles], in0=mv[:, i, tiles, 0], scalar=-1.0,
                                               in1=rstd[:, i, tiles], op0=ALU.mult,
                                               op1=ALU.mult).then_inc(S.rstd_ready[0], 1)

            for k in range(NCH + 3):
                if k < NCH:
                    variance(0, k)
                if 1 <= k <= NCH:
                    inverse(0, k - 1)
                if 2 <= k <= NCH + 1:
                    variance(1, k - 2)
                if k >= 3:
                    inverse(1, k - 3)
            nc.vector.memset(M.tri[:], 1.0)

        @blk.scalar
        def _(act):
            def root(i, c):
                tiles = slice(c * CT, (c + 1) * CT)
                act.wait_ge(S.var_ready[i], c + 1)
                nc.scalar.activation(std[:, i, tiles], std[:, i, tiles], ACT.Sqrt).then_inc(S.std_ready[i], 1)

            def normal(c):
                act.wait_ge(S.rstd_ready[0], c + 1)
                for t in range(c * CT, (c + 1) * CT):
                    nc.scalar.activation(zn[:, 0, t, :], M.y[:, t, :], ACT.Identity, scale=rstd[:, 0, t:t + 1],
                                         bias=shift[:, t:t + 1]).then_inc(S.normal_ready[0], 1)

            def turned_out(k):
                act.wait_ge(S.turned, k + 1)
                if k >= 2:
                    act.wait_ge(S.lin0_mm, k - 1)
                nc.scalar.copy(zT[:, k % 2, :], psT[:, k % 2, :]).then_inc(S.turned_out, 1)

            def lin0_out(k):
                act.wait_ge(S.lin0_mm, k + 1)
                nc.scalar.activation(M.h0T[:, k * BANK:(k + 1) * BANK], psH[:, k % 2, :], ACT.Identity,
                                     bias=M.bias[:, 0:1]).then_inc(S.lin0_out, 1)

            for k in range(NCH + 3):
                if k < NCH:
                    root(0, k)
                if 1 <= k <= NCH:
                    normal(k - 1)
                if 2 <= k <= NCH + 1:
                    root(1, k - 2)
                if k >= 3:
                    if k == 3:
                        act.wait_ge(S.lin0_in, 32)
                    for n in range(2 * (k - 3), 2 * (k - 3) + 2):
                        turned_out(n)
                        if n >= 1:
                            lin0_out(n - 1)
            lin0_out(NB - 1)

        @blk.gpsimd
        def _(pool):
            for t in range(NT):
                if t % CT == 0:
                    pool.wait_ge(S.x_load[t // CT], 16)
                pool.wait_ge(S.normal_ready[0], t + 1)
                nc.gpsimd.tensor_tensor(M.x1[:, t, :], M.x1[:, t, :], zn[:, 0, t, :], ALU.add).then_inc(S.x1_ready, 1)

        @blk.tensor
        def _(pe):
            pe.wait_ge(S.lin0_in, 32)
            for k in range(NB + 1):
                if k < NB:
                    pe.wait_ge(S.normal_ready[1], TB * k + TB)
                    if k >= 2:
                        pe.wait_ge(S.turned_out, k - 1)
                    for i in range(TB):
                        mm = nc.tensor.transpose(psT[:, k % 2, i * P:(i + 1) * P], zn[:, 1, TB * k + i, :], M.ident[:])
                    mm.then_inc(S.turned, 1)
                if k >= 1:
                    i = k - 1
                    pe.wait_ge(S.turned_out, i + 1)
                    if i >= 2:
                        pe.wait_ge(S.lin0_out, i - 1)
                    nc.tensor.matmul(psH[:, i % 2, :], M.wd[:, 0, :], zT[:, i % 2, :],
                                     start=True, stop=True).then_inc(S.lin0_mm, 1)
    block_end(nc, S)


def front_block(nc, M, S, stack, sb, ps):
    sg = sb(stack, "sg", [P, 2, BANK], F32)
    psG = ps(stack, "psG", [P, 2, BANK], F32)
    psU = ps(stack, "psU", [P, 2, BANK], F32)
    psL = ps(stack, "psL", [P, NT, E], F32)
    NB = NT * P // BANK
    TB = BANK // P
    with nc.Block() as blk:
        @blk.tensor
        def _(pe):
            for k in range(NB + 2):
                if k < NB:
                    if k >= 2:
                        pe.wait_ge(S.h1_ready, k - 1)
                    x = M.h0T[:, k * BANK:(k + 1) * BANK]
                    nc.tensor.matmul(psG[:, k % 2, :], M.wd[:, 1, :], x, start=True, stop=True).then_inc(S.swi_mm, 1)
                    nc.tensor.matmul(psU[:, k % 2, :], M.wd[:, 2, :], x, start=True, stop=True).then_inc(S.swi_mm, 1)
                if k >= 2:
                    i = k - 2
                    pe.wait_ge(S.h1_ready, i + 1)
                    for t in range(TB * i, TB * i + TB):
                        mm = nc.tensor.matmul(psL[:, t, :], M.h1T[:, t * P:(t + 1) * P], M.gate[:],
                                              start=True, stop=True)
                    mm.then_inc(S.logits_mm, 1)

        @blk.scalar
        def _(act):
            for k in range(NB + 1):
                if k < NB:
                    act.wait_ge(S.swi_mm, 2 * k + 1)
                    if k >= 2:
                        act.wait_ge(S.h1_ready, k - 1)
                    nc.scalar.activation(sg[:, k % 2, :], psG[:, k % 2, :], ACT.Silu,
                                         bias=M.bias[:, 1:2]).then_inc(S.silu_done, 1)
                if k < 3:
                    nc.scalar.copy(M.ws[:, 0, k], M.we[:, k]).then_inc(S.split_hi, 1)
                if k >= 1:
                    i = k - 1
                    act.wait_ge(S.h1_ready, i + 1)
                    cols = slice(i * BANK, (i + 1) * BANK)
                    nc.scalar.copy(M.h1s[:, 0, cols], M.h1T[:, cols]).then_inc(S.h1_hi, 1)

        @blk.gpsimd
        def _(pool):
            nc.gpsimd.affine_select(out=M.tri[:], in_=M.tri[:], compare_op=ALU.is_ge, fill=0.0, base=-1,
                                    pattern=[[1, E], [-1, E]], channel_multiplier=0)
            for k in range(NB):
                pool.wait_ge(S.h1_hi, k + 1)
                cols = slice(k * BANK, (k + 1) * BANK)
                nc.gpsimd.tensor_tensor(M.h1s[:, 1, cols], M.h1T[:, cols], M.h1s[:, 0, cols], ALU.subtract)
                if k < 3:
                    pool.wait_ge(S.split_hi, k + 1)
                    nc.gpsimd.tensor_tensor(M.ws[:, 1, k], M.we[:, k], M.ws[:, 0, k], ALU.subtract)

        @blk.vector
        def _(dve):
            for k in range(NB):
                dve.wait_ge(S.silu_done, k + 1)
                dve.wait_ge(S.swi_mm, 2 * k + 2)
                nc.vector.scalar_tensor_tensor(out=M.h1T[:, k * BANK:(k + 1) * BANK], in0=psU[:, k % 2, :],
                                               scalar=M.bias[:, 2:3], in1=sg[:, k % 2, :],
                                               op0=ALU.add, op1=ALU.mult).then_inc(S.h1_ready, 1)
            dve.wait_ge(S.logits_mm, NB)
            nc.vector.tensor_copy(M.logit[:], psL[:])
    block_end(nc, S)


def routing_steps(nc, M, S, R, dve):
    logit, score, small, more, same, rank = M.logit, R.score, R.small, R.more, R.same, R.rank

    def wide(ap):
        return ap.to_broadcast([P, NT, E])

    done = 0

    def then(ins):
        nonlocal done
        done += 1
        ins.then_inc(S.route_step, 1)
        dve.wait_ge(S.route_step, done)

    then(nc.vector.tensor_reduce(small[:, 0, :, 0], logit[:], AX.X, ALU.max))
    nc.vector.tensor_tensor(logit[:], logit[:], wide(small[:, 0]), ALU.subtract).then_inc(S.route_shifted, 1)
    yield
    dve.wait_ge(S.route_exp, 1)
    then(nc.vector.tensor_reduce(small[:, 1, :, 0], score[:], AX.X, ALU.add))
    then(nc.vector.reciprocal(small[:, 2], small[:, 1]))
    then(nc.vector.tensor_tensor(score[:], score[:], wide(small[:, 2]), ALU.mult))
    yield
    own = score[:].unsqueeze(3).to_broadcast([P, NT, E, E])
    other = score[:].unsqueeze(2).to_broadcast([P, NT, E, E])
    tri = M.tri[:].unsqueeze(1).to_broadcast([P, NT, E, E])
    for h in (slice(0, NT // 2), slice(NT // 2, NT)):
        then(nc.vector.tensor_tensor(same[:, h], other[:, h], own[:, h], ALU.is_equal))
        yield
        then(nc.vector.tensor_tensor(same[:, h], same[:, h], tri[:, h], ALU.mult))
        yield
        then(nc.vector.tensor_tensor(more[:, h], other[:, h], own[:, h], ALU.is_gt))
        yield
        then(nc.vector.tensor_tensor(more[:, h], more[:, h], same[:, h], ALU.add))
        yield
        then(nc.vector.tensor_reduce(rank[:, h], more[:, h], AX.X, ALU.add))
        yield
    then(nc.vector.tensor_scalar(rank[:], rank[:], TOPK - 0.5, None, ALU.is_lt))
    then(nc.vector.tensor_tensor(rank[:], rank[:], score[:], ALU.mult))
    yield
    then(nc.vector.tensor_reduce(small[:, 3, :, 0], rank[:], AX.X, ALU.add))
    then(nc.vector.reciprocal(small[:, 0], small[:, 3]))
    then(nc.vector.tensor_tensor(M.comb[:], rank[:], wide(small[:, 0]), ALU.mult))
    yield


def expert_block(nc, M, S, R, base, work, per, routing):
    TB = BANK // P
    W = len(work)
    BACK = 2
    with nc.Block() as blk:
        @blk.tensor
        def _(pe):
            def hidden(n):
                k, c = work[n]
                if n >= 2:
                    pe.wait_ge(S.gated, n - 1)
                for j, bank in enumerate((R.psG, R.psU)):
                    for q, (wi, xi) in enumerate([(0, 0), (0, 1), (1, 0)]):
                        mm = nc.tensor.matmul(bank[:, n % 2, :], M.ws[:, wi, j, c, :],
                                              M.h1s[:, xi, bass.ds((base + k) * BANK, BANK)],
                                              start=q == 0, stop=q == 2)
                    mm.then_inc(S.hidden_mm, 1)

            def back(n):
                if n % per != per - 1:
                    return
                o = n // per
                chunks = range(n - per + 1, n + 1)
                pe.wait_ge(S.hid_lo, n + 1)
                if o >= 2:
                    pe.wait_ge(S.expert_added, o - 1)
                for t in range(TB):
                    for m in chunks:
                        for q, (hi, wi) in enumerate([(0, 0), (0, 1), (1, 0)]):
                            mm = nc.tensor.matmul(R.psY[:, o % 2, t * P:(t + 1) * P],
                                                  R.hid[:, m % 4, hi, t * P:(t + 1) * P], M.ws[:, wi, 2, work[m][1], :],
                                                  start=m == chunks[0] and q == 0, stop=m == n and q == 2)
                mm.then_inc(S.expert_out, 1)

            for n in range(W + BACK):
                if n < W:
                    hidden(n)
                if n >= BACK:
                    back(n - BACK)

        @blk.scalar
        def _(act):
            for n in range(W + 1):
                if n < W:
                    act.wait_ge(S.hidden_mm, 2 * n + 1)
                    if n >= 2:
                        act.wait_ge(S.gated, n - 1)
                    nc.scalar.activation(R.sg[:, n % 2, :], R.psG[:, n % 2, :], ACT.Silu).then_inc(S.silu_done, 1)
                if routing and n == 2:
                    act.wait_ge(S.route_shifted, 1)
                    nc.scalar.activation(R.score[:], M.logit[:], ACT.Exp).then_inc(S.route_exp, 1)
                if n >= 1:
                    m = n - 1
                    act.wait_ge(S.gated, m + 1)
                    if m >= 4:
                        act.wait_ge(S.expert_out, (m - 4) // per + 1)
                    nc.scalar.copy(R.hid[:, m % 4, 0, :], R.hid32[:, m % 3, :]).then_inc(S.hid_hi, 1)

        @blk.gpsimd
        def _(pool):
            for n in range(W):
                pool.wait_ge(S.hid_hi, n + 1)
                nc.gpsimd.tensor_tensor(R.hid[:, n % 4, 1, :], R.hid32[:, n % 3, :], R.hid[:, n % 4, 0, :],
                                        ALU.subtract).then_inc(S.hid_lo, 1)

        @blk.vector
        def _(dve):
            def gated(n):
                dve.wait_ge(S.silu_done, n + 1)
                dve.wait_ge(S.hidden_mm, 2 * n + 2)
                if n >= 3:
                    dve.wait_ge(S.hid_lo, n - 2)
                nc.vector.tensor_tensor(R.hid32[:, n % 3, :], R.psU[:, n % 2, :], R.sg[:, n % 2, :],
                                        ALU.mult).then_inc(S.gated, 1)

            def add(n):
                if n % per != per - 1:
                    return
                k, c = work[n]
                o = n // per
                dve.wait_ge(S.expert_out, o + 1)
                at = (base + k) * TB
                if routing:
                    nc.vector.tensor_copy(M.moe[:, at:at + TB, :].rearrange("p t d -> p (t d)"),
                                          R.psY[:, o % 2, :]).then_inc(S.expert_added, 1)
                    return
                if o >= 1:
                    dve.wait_ge(S.expert_added, o)
                for t in range(TB):
                    acc = M.moe[:, bass.ds(at + t, 1), :].rearrange("p t d -> p (t d)")
                    last = nc.vector.scalar_tensor_tensor(
                        out=acc, in0=R.psY[:, o % 2, t * P:(t + 1) * P],
                        scalar=R.comb[:, k * TB + t, c:c + 1], in1=acc, op0=ALU.mult, op1=ALU.add)
                last.then_inc(S.expert_added, 1)

            steps = routing_steps(nc, M, S, R, dve) if routing else iter(())
            if not routing:
                nc.vector.tensor_copy(R.comb[:].rearrange("p t e -> p (t e)"),
                                      M.comb[:, bass.ds(base * TB, KB * TB), :].rearrange("p t e -> p (t e)")
                                      ).then_inc(S.comb_here, 1)
            for n in range(W + BACK):
                if n < W:
                    gated(n)
                next(steps, None)
                if not routing and n == BACK:
                    dve.wait_ge(S.comb_here, 1)
                if n >= BACK:
                    add(n - BACK)
    block_end(nc, S)


def back_block(nc, M, S, stack, sb, ps, out):
    mT = sb(stack, "mT", [P, 2, BANK], F32)
    h3 = sb(stack, "h3", [P, 2, BANK], F32)
    sg = sb(stack, "sg5", [P, 2, BANK], F32)
    h4 = sb(stack, "h4", [P, 2, BANK], F32)
    hn = sb(stack, "hn", [P, NT, D], F32)
    bn = sb(stack, "bn5", [P, NT, 6], F32)
    mv = sb(stack, "mv5", [P, NT, 2], F32)
    std = sb(stack, "std5", [P, NT], F32)
    rstd = sb(stack, "rstd5", [P, NT], F32)
    psM = ps(stack, "psM", [P, 2, BANK], F32)
    psH = ps(stack, "psH5", [P, BANK], F32)
    psG = ps(stack, "psG5", [P, 2, BANK], F32)
    psU = ps(stack, "psU5", [P, 2, BANK], F32)
    psN = ps(stack, "psN", [P, BANK], F32)
    NB = NT * P // BANK
    TB = BANK // P
    CUTS = (0, NB // 2, NB - 1, NB)
    out_tiles = out.rearrange("b (t p) d -> p (b t) d", p=P)
    with nc.Block() as blk:
        @blk.tensor
        def _(pe):
            for k in range(NB + 3):
                if k < NB:
                    if k >= 2:
                        pe.wait_ge(S.step_b, k - 1)
                    for t in range(TB):
                        mm = nc.tensor.transpose(psM[:, k % 2, t * P:(t + 1) * P], M.moe[:, TB * k + t, :], M.ident[:])
                    mm.then_inc(S.step_a, 1)
                if 1 <= k <= NB:
                    i = k - 1
                    pe.wait_ge(S.step_b, i + 1)
                    if i >= 1:
                        pe.wait_ge(S.step_d, i)
                    nc.tensor.matmul(psH[:], M.wd[:, 3, :], mT[:, i % 2, :], start=True, stop=True).then_inc(S.step_c, 1)
                if 2 <= k <= NB + 1:
                    i = k - 2
                    pe.wait_ge(S.step_d, i + 1)
                    if i >= 2:
                        pe.wait_ge(S.step_g, i - 1)
                    nc.tensor.matmul(psG[:, i % 2, :], M.wd[:, 4, :], h3[:, i % 2, :],
                                     start=True, stop=True).then_inc(S.step_e, 1)
                    nc.tensor.matmul(psU[:, i % 2, :], M.wd[:, 5, :], h3[:, i % 2, :],
                                     start=True, stop=True).then_inc(S.step_e, 1)
                if k >= 3:
                    i = k - 3
                    pe.wait_ge(S.step_g, i + 1)
                    if i >= 1:
                        pe.wait_ge(S.norm_ready, i)
                    for t in range(TB):
                        mm = nc.tensor.transpose(psN[:, t * P:(t + 1) * P], h4[:, i % 2, t * P:(t + 1) * P], M.ident[:])
                    mm.then_inc(S.step_h, 1)

        @blk.scalar
        def _(act):
            def root(j):
                tiles = slice(TB * CUTS[j], TB * CUTS[j + 1])
                act.wait_ge(S.var_ready[0], j + 1)
                nc.scalar.activation(std[:, tiles], std[:, tiles], ACT.Sqrt).then_inc(S.std_ready[0], 1)

            for k in range(NB + 2):
                if k < NB:
                    act.wait_ge(S.step_a, k + 1)
                    if k >= 2:
                        act.wait_ge(S.step_c, k - 1)
                    nc.scalar.copy(mT[:, k % 2, :], psM[:, k % 2, :]).then_inc(S.step_b, 1)
                if 1 <= k <= NB:
                    i = k - 1
                    act.wait_ge(S.step_c, i + 1)
                    if i >= 2:
                        act.wait_ge(S.step_e, 2 * i - 2)
                    nc.scalar.activation(h3[:, i % 2, :], psH[:], ACT.Identity,
                                         bias=M.bias[:, 3:4]).then_inc(S.step_d, 1)
                if k >= 2:
                    i = k - 2
                    act.wait_ge(S.step_e, 2 * i + 1)
                    if i >= 2:
                        act.wait_ge(S.step_g, i - 1)
                    nc.scalar.activation(sg[:, i % 2, :], psG[:, i % 2, :], ACT.Silu,
                                         bias=M.bias[:, 4:5]).then_inc(S.step_f, 1)
                if k - 3 in CUTS[1:]:
                    root(CUTS.index(k - 3) - 1)
            for j, cut in enumerate(CUTS[1:]):
                if cut + 3 >= NB + 2:
                    root(j)

        @blk.vector
        def _(dve):
            def variance(j):
                for t in range(TB * CUTS[j], TB * CUTS[j + 1]):
                    last = nc.vector.bn_aggr(mv[:, t, :], bn[:, t, :])
                last.then_inc(S.stats, 1)
                dve.wait_ge(S.stats, j + 1)
                tiles = slice(TB * CUTS[j], TB * CUTS[j + 1])
                nc.vector.tensor_scalar(std[:, tiles], mv[:, tiles, 1], EPS, None, ALU.add).then_inc(S.var_ready[0], 1)

            def normal(j):
                tiles = slice(TB * CUTS[j], TB * CUTS[j + 1])
                dve.wait_ge(S.std_ready[0], j + 1)
                nc.vector.reciprocal(rstd[:, tiles], std[:, tiles]).then_inc(S.rstd_ready[0], 1)
                dve.wait_ge(S.rstd_ready[0], j + 1)
                for t in range(TB * CUTS[j], TB * CUTS[j + 1]):
                    nc.vector.tensor_scalar(hn[:, t, :], hn[:, t, :], mv[:, t, 0:1], rstd[:, t:t + 1],
                                            ALU.subtract, ALU.mult).then_inc(S.split_hi, 1)

            for k in range(NB + 1):
                if k < NB:
                    dve.wait_ge(S.step_f, k + 1)
                    dve.wait_ge(S.step_e, 2 * k + 2)
                    if k >= 2:
                        dve.wait_ge(S.step_h, k - 1)
                    nc.vector.scalar_tensor_tensor(out=h4[:, k % 2, :], in0=psU[:, k % 2, :],
                                                   scalar=M.bias[:, 5:6], in1=sg[:, k % 2, :],
                                                   op0=ALU.add, op1=ALU.mult).then_inc(S.step_g, 1)
                if k >= 1:
                    i = k - 1
                    dve.wait_ge(S.step_h, i + 1)
                    for t in range(TB):
                        nc.vector.bn_stats(bn[:, TB * i + t, :], psN[:, t * P:(t + 1) * P])
                    nc.vector.tensor_copy(hn[:, TB * i:TB * i + TB, :].rearrange("p t d -> p (t d)"),
                                          psN[:]).then_inc(S.norm_ready, 1)
                if k in CUTS[1:]:
                    dve.wait_ge(S.norm_ready, k)
                    variance(CUTS.index(k) - 1)
                if k - 2 in CUTS[1:]:
                    normal(CUTS.index(k - 2) - 1)
            for j, cut in enumerate(CUTS[1:]):
                if cut + 2 > NB:
                    normal(j)

        @blk.gpsimd
        def _(pool):
            for t in range(NT):
                pool.wait_ge(S.split_hi, t + 1)
                nc.gpsimd.tensor_tensor(M.x1[:, t, :], M.x1[:, t, :], hn[:, t, :], ALU.add).then_inc(S.split_lo, 1)

        @blk.sync
        def _(sp):
            for k in range(NB):
                sp.wait_ge(S.split_lo, TB * (k + 1))
                sp.dma_start(out_tiles[:, TB * k:TB * k + TB, :], M.x1[:, TB * k:TB * k + TB, :]).then_inc(S.stored, 16)
            sp.wait_ge(S.stored, 16 * NB)


def phase_ffn(nc, I, M, S, sb, ps, out):
    with ExitStack() as stack:
        M.x1 = sb(stack, "x1", [P, NT, D], F32)
        M.wd = sb(stack, "wd", [P, 6, D], F32)
        M.bias = sb(stack, "bias", [P, 6], F32)
        M.gate = sb(stack, "gate", [P, E], F32)
        M.ws = sb(stack, "ws", [P, 2, 3, E + NC, H], F16)
        M.h1s = sb(stack, "h1s", [P, 2, NT * P], F16)
        M.logit = sb(stack, "logit", [P, NT, E], F32)
        M.comb = sb(stack, "comb", [P, NT, E], F32)
        M.tri = sb(stack, "tri", [P, E, E], F32)
        with ExitStack() as early:
            M.h0T = sb(early, "h0T", [P, NT * P], F32)
            M.h1T = sb(early, "h1T", [P, NT * P], F32)
            M.we = sb(early, "we", [P, 3, E + NC, H], F32)
            with ExitStack() as temps:
                norm_block(nc, I, M, S, temps, sb, ps)
            with ExitStack() as temps:
                front_block(nc, M, S, temps, sb, ps)
        M.moe = sb(stack, "moe", [P, NT, D], F32)
        with ExitStack() as temps:
            R = Box()
            R.sg = sb(temps, "sg4", [P, 2, BANK], F32)
            R.hid32 = sb(temps, "hid32", [P, 3, BANK], F32)
            R.hid = sb(temps, "hid", [P, 4, 2, BANK], F16)
            R.comb = sb(temps, "comb4", [P, KB * BANK // P, E], F32)
            R.score = sb(temps, "score", [P, NT, E], F32)
            R.small = sb(temps, "small", [P, 4, NT, 1], F32)
            R.more = sb(temps, "more", [P, NT, E, E], F32)
            R.same = sb(temps, "same", [P, NT, E, E], F32)
            R.rank = sb(temps, "rank", [P, NT, E], F32)
            R.psG = ps(temps, "psG4", [P, 2, BANK], F32)
            R.psU = ps(temps, "psU4", [P, 2, BANK], F32)
            R.psY = ps(temps, "psY", [P, 2, BANK], F32)
            blocks = NT * P // BANK
            expert_block(nc, M, S, R, 0, [(k, E + c) for k in range(blocks) for c in range(NC)], NC, True)
            with nc.Fori(0, blocks // KB) as i:
                expert_block(nc, M, S, R, i * KB, [(k, c) for k in range(KB) for c in range(E)], 1, False)
        with ExitStack() as temps:
            back_block(nc, M, S, temps, sb, ps, out)


def build(nc, I, out):
    with ExitStack() as top:
        numbers = []

        def sem(name):
            x = top.enter_context(nc.semaphore(name))
            numbers.append(x.num)
            return x

        def sb(stack, name, shape, dt):
            return stack.enter_context(nc.sbuf_tensor(name, shape, dt))

        def ps(stack, name, shape, dt):
            return stack.enter_context(nc.psum_tensor(name, shape, dt))

        S = Box()
        S.scores_ready = sem("scores_ready")
        S.exp_done = sem("exp_done")
        S.lo_dve = sem("lo_dve")
        S.lo_pool = sem("lo_pool")
        S.weighted_done = sem("weighted_done")
        S.out_lo = sem("out_lo")
        S.out_added = sem("out_added")
        S.out_scaled = sem("out_scaled")
        S.aux_ready = sem("aux_ready")
        S.aux_free = [sem(f"aux_free{k}") for k in range(NAUX)]
        S.rope_sum = sem("rope_sum")
        S.rope_hi = sem("rope_hi")
        S.rope_lo = sem("rope_lo")
        S.v_hi = sem("v_hi")
        S.row_max = sem("row_max")
        S.k_out = sem("k_out")
        S.q_out = sem("q_out")
        S.near_in = [sem(f"near_in{i}") for i in range(2)]
        S.far_in = sem("far_in")
        S.row_max_in = sem("row_max_in")
        S.xq_in = sem("xq_in")
        S.xv_in = sem("xv_in")
        S.x_load = [sem(f"x_load{b}") for b in range(B)]
        S.w_in = sem("w_in")
        S.c_in = sem("c_in")
        S.consts = sem("consts")
        S.stats = sem("stats")
        S.var_ready = [sem(f"var_ready{i}") for i in range(2)]
        S.std_ready = [sem(f"std_ready{i}") for i in range(2)]
        S.rstd_ready = [sem(f"rstd_ready{i}") for i in range(2)]
        S.normal_ready = [sem(f"normal_ready{i}") for i in range(2)]
        S.x1_ready = sem("x1_ready")
        S.lin0_in = sem("lin0_in")
        S.lin0_mm = sem("lin0_mm")
        S.lin0_out = sem("lin0_out")
        S.swi_mm = sem("swi_mm")
        S.silu_done = sem("silu_done")
        S.h1_ready = sem("h1_ready")
        S.h1_hi = sem("h1_hi")
        S.logits_mm = sem("logits_mm")
        S.hidden_mm = sem("hidden_mm")
        S.gated = sem("gated")
        S.hid_hi = sem("hid_hi")
        S.hid_lo = sem("hid_lo")
        S.expert_out = sem("expert_out")
        S.expert_added = sem("expert_added")
        S.comb_here = sem("comb_here")
        S.route_step = sem("route_step")
        S.route_shifted = sem("route_shifted")
        S.route_exp = sem("route_exp")
        S.norm_ready = sem("norm_ready")
        S.turned = sem("turned")
        S.turned_out = sem("turned_out")
        S.split_hi = sem("split_hi")
        S.split_lo = sem("split_lo")
        S.step_a = sem("step_a")
        S.step_b = sem("step_b")
        S.step_c = sem("step_c")
        S.step_d = sem("step_d")
        S.step_e = sem("step_e")
        S.step_f = sem("step_f")
        S.step_g = sem("step_g")
        S.step_h = sem("step_h")
        S.stored = sem("stored")
        S.first, S.last = min(numbers), max(numbers)
        M = Box()
        M.ident = sb(top, "ident", [P, P], F32)
        M.y = sb(top, "y", [P, NT, D], F32)
        M.x_way = nc.dram_tensor("x_way", (P, 2, NT * P), F16, kind="Internal").ap()
        M.k_way = nc.dram_tensor("k_way", (4, HALF, GH, T), F16, kind="Internal").ap()
        M.q_way = nc.dram_tensor("q_way", (4, HALF, GH, T), F16, kind="Internal").ap()
        phase_attention(nc, I, M, S, sb, ps)
        phase_ffn(nc, I, M, S, sb, ps, out)


def rotary_table():
    inv = np.float32(1.0) / np.float32(10000.0) ** (np.arange(0, HD, 2, dtype=np.float32) / np.float32(HD))
    angle = np.outer(np.arange(T, dtype=np.float32), inv.astype(np.float32)).astype(np.float32)
    cos, sin = np.cos(angle).astype(np.float32), np.sin(angle).astype(np.float32)
    return (np.ascontiguousarray(np.tile(cos.T, (GH, 1))), np.ascontiguousarray(np.tile(sin.T, (GH, 1))))


def by_halves(w):
    w = w.reshape(GROUPS, GH, 2, HALF, D).transpose(4, 0, 2, 1, 3)
    return np.ascontiguousarray(w.reshape(D, HEADS * HD))


def kernel(**inputs):
    import concourse.bacc as bacc
    from concourse.bass_utils import run_bass_kernel_spmd

    a = {name.removeprefix("L0_ffn_").removeprefix("L0_attn_"): np.asarray(v) for name, v in inputs.items()
         if name != "L0_attn_x"}
    laid = {name: np.ascontiguousarray(v) for name, v in a.items() if name not in ("wq", "wk", "wv", "wo", "gate_w")}
    laid["x"] = np.ascontiguousarray(np.asarray(inputs["L0_attn_x"]))
    laid["wq"], laid["wk"] = by_halves(a["wq"]), by_halves(a["wk"])
    laid["wv"] = np.ascontiguousarray(a["wv"].T)
    laid["wo"] = np.ascontiguousarray(a["wo"].T.reshape(HEADS * HD // P, P, D).transpose(1, 0, 2))
    laid["gate_w"] = np.ascontiguousarray(a["gate_w"].T)
    laid["cos"], laid["sin"] = rotary_table()

    nc = bacc.Bacc("TRN2", target_bir_lowering=False, num_devices=1)
    I = {name: nc.dram_tensor(f"in_{name}", v.shape, mybir.dt.from_np(v.dtype), kind="ExternalInput").ap()
         for name, v in laid.items()}
    out = nc.dram_tensor("out", (B, T, D), F32, kind="ExternalOutput").ap()
    build(nc, I, out)
    r = run_bass_kernel_spmd(nc, [{f"in_{name}": v for name, v in laid.items()}], core_ids=[0])
    return r.results[0]["out"]
```

```python
from contextlib import ExitStack

import numpy as np

import concourse.bass as bass
from concourse import mybir

F32 = mybir.dt.float32
F16 = mybir.dt.float16
BF16 = mybir.dt.bfloat16
ALU = mybir.AluOpType
ACT = mybir.ActivationFunctionType
AX = mybir.AxisListType

P = 128
B, T, D = 4, 1024, 128
HEADS, HD = 16, 64
HALF = HD // 2
GH = P // HALF
GROUPS = HEADS // GH
TT = T // P
NT = B * TT
CH = GH * HD // P
BANK = 512
SCALE = float(HD) ** -0.5
EPS = 1e-5
NEG = -1.0e30
LOWEST = -3.0e38
MSCALE = 64.0
VW = 2 * HD + 2
E, TOPK, H = 8, 4, 128
SH = 2 * H
NC = SH // H
KB = 4

UNITS = [(j, max(j * P, half * BANK), (half + 1) * BANK - max(j * P, half * BANK))
         for half in range(T // BANK) for j in range((half + 1) * BANK // P)]
NU = len(UNITS)
SU = NU * GH
PAIR_END = {max(i for i, (j, c, w) in enumerate(UNITS) if j == 2 * q + 1 and c <= (2 * q + 1) * P < c + w): q
            for q in range(TT // 2)}
MAXP = [(t, c, min(BANK, (t + 1) * P - c)) for t in range(TT) for c in range(0, (t + 1) * P, BANK)]
LO_LAG = 0
LAG = 5
NP_ = 6
ROPE_LAG = 6
SUM_LAG = 2
REST_LAG = 6
LN_STEPS = (3, 12, 21, 30, 31)
STAT_FIRST, STAT_STEPS = 4, (30, 34, 38)
QK_STEPS = (0, 2, 8, 11, 18, 18, 26, 28)
V_STEPS = (4, 20, 26, 46)
MX_FIRST, MX_LAST, MT_STEP = 8, 43, 44
TR1_STEPS, WO_STEPS, TR0_STEPS = (11, 15), (19, 21), (32, 36)
LO_OF = 12
LO_POOL = (0, 1, 2, 3, 5, 7, 9)
ACT_LAG = 1
OUT_LAG = 1
SCALE_LAG = 1
NO = 3
NAUX = 3


def plan(slots, near, far, flush):
    at = {}

    def put(slot, step, item):
        at.setdefault((slot, step), []).append((slot,) + item)

    for s in slots:
        if s >= 0:
            for half in range(2):
                put(s, TR1_STEPS[half], ("tr", 1, half))
                put(s, WO_STEPS[half], ("wo", half))
        if s in far:
            for r in range(8):
                put(s, QK_STEPS[r], ("qk", r // 4, r // 2 % 2, r % 2))
        if s in near:
            for tp in range(TT // 2):
                put(s, V_STEPS[tp], ("v", tp))
            for h in range(GH):
                for k in range(len(MAXP)):
                    at_step = MX_FIRST + (h * len(MAXP) + k) * (MX_LAST - MX_FIRST) // (GH * len(MAXP) - 1)
                    put(s, at_step, ("mx", h, k))
            put(s, MT_STEP, ("mt",))
        if s >= 0:
            for half in range(2):
                put(s, TR0_STEPS[half], ("tr", 0, half))
    if flush:
        for item in [("tr", 1, 0), ("tr", 1, 1), ("wo", 0), ("wo", 1)]:
            put(GROUPS, LAG + max(OUT_LAG, SCALE_LAG), item)
    steps = []
    number = {}
    for s in slots:
        for u in range(SU):
            steps.append((s, u))
    if slots[-1] == GROUPS - 1:
        steps += [(GROUPS, u) for u in range(LAG + max(OUT_LAG, SCALE_LAG) + 1)]
    for key in steps:
        for item in at.get(key, []):
            number[item] = len(number)
    assert sum(len(v) for v in at.values()) == len(number)
    return steps, at, number


def lo_on_pool(u):
    return u % LO_OF in LO_POOL


class Box:
    pass


class Counts:

    def __init__(self):
        self.pool, self.dve = [], []
        p = d = 0
        for k in range(SU * GROUPS):
            if lo_on_pool(k % SU):
                p += 1
            else:
                d += 1
            self.pool.append(p)
            self.dve.append(d)


COUNTS = Counts()


def attention_block(nc, M, S, b, slots, near, far, flush=False):
    steps, at, number = plan(slots, near, far, flush)
    first = slots[0]

    def loads(s):
        return sum(x in near for x in slots if x <= s)

    def ropes(s):
        return sum(x in far for x in slots if x < s)

    def bank(item):
        return number[item] % NAUX

    def taken(eng, item):
        eng.wait_ge(S.aux_free[bank(item)], number[item] // NAUX + 1)

    def ready(eng, item):
        eng.wait_ge(S.aux_ready, number[item] + 1)

    def free(item):
        return S.aux_free[bank(item)]

    def parts(U):
        return U // SU, (U % SU) // NU, U % NU

    def wait_lo(eng, U):
        if lo_on_pool(U % SU):
            eng.wait_ge(S.lo_pool, COUNTS.pool[U])
        else:
            eng.wait_ge(S.lo_dve, COUNTS.dve[U])

    def ln_stage(s, u):
        return LN_STEPS.index(u) if first < 0 and s == first and u in LN_STEPS else None

    def staged(batch):
        halves = (M.Phi, M.Plo)[1 - batch % 2][:].rearrange("p a n -> p (a n)")[:, 0:2 * T]
        return M.y[:, batch * TT:(batch + 1) * TT, :], halves.rearrange("p (h n) -> p h n", h=2)

    last_unit = SU * len(slots) - 1 if slots[0] >= 0 else -1

    def pairs_at(s, u, lag=0):
        U = SU * s + u - LAG - lag
        if s >= 0 and 0 <= U <= last_unit and U % NU in PAIR_END:
            return [(U, 4 * (U // NU) + PAIR_END[U % NU])]
        return []

    with nc.Block() as blk:

        @blk.tensor
        def _(pe):
            def scores(U):
                s, h, u = parts(U)
                j, c, w = UNITS[u]
                p = s % 2
                if u == 0 and h == 0 and s > 0:
                    pe.wait_ge(S.row_max_in, 16 * s)
                    pe.wait_ge(S.far_in, 32 * s)
                if U >= 2:
                    pe.wait_ge(S.exp_done, U - 1)
                diagonal = c == j * P
                out = M.psS[:, U % 2, 0:w]
                nc.tensor.matmul(out, M.K1[:, p, h, j * P:(j + 1) * P], M.Q1[:, p, h, c:c + w],
                                 start=True, stop=False)
                mm = nc.tensor.matmul(out, M.K2[0:HD + 1, p, h, j * P:(j + 1) * P],
                                      M.Q2[0:HD + 1, p, h, c:c + w], start=False, stop=not diagonal)
                if diagonal:
                    mm = nc.tensor.matmul(out[:, 0:P], M.ident16[:], M.maskT[:], start=False, stop=True)
                mm.then_inc(S.scores_ready, 1)

            def weighted(U):
                s, h, u = parts(U)
                j, c, w = UNITS[u]
                wait_lo(pe, U)
                for k in range(w // P):
                    t = c // P + k
                    n = 4 * (U // NU) + t // 2
                    first = j == 0 and t % 2 == 0
                    if first and n >= 3:
                        pe.wait_ge(S.out_added, n - 2)
                    O = M.psO[:, n % 3, 256 * (t % 2):256 * (t % 2) + 2 * HD + 1]
                    nc.tensor.matmul(O, M.Phi[:, U % NP_, k * P:(k + 1) * P], M.V[:, s % 2, j, h, 0:2 * HD + 1],
                                     start=first, stop=False, skip_group_check=True)
                    mm = nc.tensor.matmul(O[:, HD:2 * HD + 1], M.Plo[:, U % NP_, k * P:(k + 1) * P],
                                          M.V[:, s % 2, j, h, HD:2 * HD + 1],
                                          start=False, stop=j == t, skip_group_check=True)
                mm.then_inc(S.weighted_done, 1)

            def side(item):
                s, kind, *a = item
                X = M.psX[:, bank(item), :]
                g = (s + (2 if kind == "qk" else 1)) % GROUPS
                p = (s + 1) % 2
                if number[item] >= NAUX:
                    pe.wait_ge(S.aux_free[bank(item)], number[item] // NAUX)
                if kind == "qk":
                    which, n, half = a
                    if s == GROUPS - 2 and which == 0 and n == 0 and half == 0:
                        pe.wait_ge(S.xq_in, 16)
                    cols = (2 * g + half) * P
                    w = M.wkq[:, which]
                    for k, (wi, xi) in enumerate([(0, 0), (0, 1), (1, 0)]):
                        mm = nc.tensor.matmul(X, w[:, wi, cols:cols + P], M.xq[:, xi, n * BANK:(n + 1) * BANK],
                                              start=k == 0, stop=k == 2)
                elif kind == "v":
                    if s == GROUPS - 1 and a[0] == 0:
                        pe.wait_ge(S.xv_in, 16)
                    for k in range(2):
                        t = 2 * a[0] + k
                        for i, (wi, xi) in enumerate([(0, 0), (1, 0), (0, 1)]):
                            mm = nc.tensor.matmul(X[:, k * 256:(k + 1) * 256], M.xv[:, xi, t * P:(t + 1) * P],
                                                  M.wv[:, wi, g * 256:(g + 1) * 256],
                                                  start=i == 0, stop=i == 2)
                elif kind == "mx":
                    h, k = a
                    t, c, w = MAXP[k]
                    if k == 0 and h % 2 == 0:
                        pe.wait_ge(S.near_in[h // 2], 48 * loads(s))
                    mm = nc.tensor.matmul(X[:, 0:w], M.Q1[:, p, h, t * P:(t + 1) * P], M.K1[:, p, h, c:c + w],
                                          start=True, stop=True)
                elif kind == "mt":
                    pe.wait_ge(S.row_max, loads(s))
                    mm = nc.tensor.transpose(X[0:GH * TT, 0:P], M.rmax[:], M.ident[:])
                elif kind == "tr":
                    c, half = a
                    own = s - 1 if c == 1 else s
                    if half == 0 and own >= 0:
                        pe.wait_ge(S.out_scaled, 4 * (GH * own + 2 * (c + 1)))
                    for k in range(4):
                        mm = nc.tensor.transpose(X[:, k * P:(k + 1) * P],
                                                 M.On[:, 4 * half + k, c * P:(c + 1) * P], M.ident[:])
                elif kind == "wo":
                    half = a[0]
                    og = (s - 1) % GROUPS
                    if s > 0:
                        taken(pe, (s - 1, "tr", 0, half))
                    taken(pe, (s, "tr", 1, half))
                    for k in range(4):
                        for c in range(CH):
                            t = 4 * half + k
                            mm = nc.tensor.matmul(X[:, k * P:(k + 1) * P], M.OT[:, c, t * P:(t + 1) * P],
                                                  M.wo[:, CH * og + c, :], start=c == 0, stop=c == CH - 1)
                mm.then_inc(S.aux_ready, 1)

            for s, u in steps:
                U = SU * s + u
                if 0 <= U <= last_unit:
                    scores(U)
                stage = ln_stage(s, u)
                if stage is not None and 1 <= stage < B:
                    x, _ = staged(stage)
                    pe.wait_ge(S.norm_ready, stage)
                    if stage > 1:
                        pe.wait_ge(S.split_lo, stage - 1)
                    for t in range(TT):
                        mm = nc.tensor.transpose(M.psS[:, t // 4, t % 4 * P:(t % 4 + 1) * P], x[:, t, :], M.ident[:])
                    mm.then_inc(S.turned, 1)
                for item in at.get((s, u), []) if s < GROUPS else []:
                    side(item)
                if s >= 0 and 0 <= U - LAG <= last_unit:
                    weighted(U - LAG)
                for item in at.get((s, u), []) if s == GROUPS else []:
                    side(item)

        @blk.scalar
        def _(act):
            def exps(U):
                w = UNITS[U % NU][2]
                act.wait_ge(S.scores_ready, U + 1)
                if U >= NP_:
                    wait_lo(act, U - NP_)
                    act.wait_ge(S.weighted_done, U - NP_ + 1)
                nc.scalar.activation(M.P32[:, U % NP_, 0:w], M.psS[:, U % 2, 0:w], ACT.Exp, scale=SCALE)
                nc.scalar.activation(M.Phi[:, U % NP_, 0:w], M.psS[:, U % 2, 0:w], ACT.Exp,
                                     scale=SCALE).then_inc(S.exp_done, 1)

            def side(item):
                s, kind, *a = item
                X = M.psX[:, bank(item), :]
                p = (s + 1) % 2
                if kind == "qk" and a[2] == 1:
                    which, n, _ = a
                    r = 4 * ropes(s) + 2 * which + n
                    act.wait_ge(S.rope_sum, r + 1)
                    if ropes(s) > 0 and n == 0:
                        act.wait_ge(S.q_out if which else S.k_out, 16 * GH * ropes(s))
                    nc.scalar.copy(M.HL[:, which, 0:2, n * BANK:(n + 1) * BANK], M.R[:]).then_inc(S.rope_hi, 1)
                elif kind == "v":
                    ready(act, item)
                    if s > 0 and a[0] == 0:
                        act.wait_ge(S.weighted_done, SU * s)
                    nc.scalar.copy(M.V[:, p, 2 * a[0]:2 * a[0] + 2, :, HD:2 * HD],
                                   X.rearrange("p (t h d) -> p t h d", t=2, h=GH)).then_inc(S.v_hi, 1)
                elif kind == "mt":
                    ready(act, item)
                    if s > 0:
                        act.wait_ge(S.row_max_in, 16 * s)
                    nc.scalar.activation(M.mrow[:], X[0:GH * TT, 0:P], ACT.Copy,
                                         scale=-1.0 / MSCALE).then_inc(free(item), 1)
                elif kind == "tr":
                    ready(act, item)
                    last = (s if a[0] == 0 else s - 1, "wo", 1)
                    if last in number:
                        ready(act, last)
                    nc.scalar.copy(M.OT[:, a[0], a[1] * BANK:(a[1] + 1) * BANK], X).then_inc(free(item), 1)

            def out_lo(Uw, n):
                O = M.psO[:, n % 3, :].rearrange("p (t c) -> p t c", t=2)
                act.wait_ge(S.weighted_done, Uw + 1)
                if n >= NO:
                    act.wait_ge(S.out_added, n - NO + 1)
                nc.scalar.copy(M.Olo[:, n % NO], O[:, :, 0:HD]).then_inc(S.out_lo, 1)

            for s, u in steps:
                U = SU * s + u
                if 0 <= U <= last_unit:
                    exps(U)
                stage = ln_stage(s, u)
                if stage is not None and stage < B - 1:
                    tiles = slice((stage + 1) * TT, (stage + 2) * TT)
                    act.wait_ge(S.var_ready[0], stage + 1)
                    nc.scalar.activation(M.std[:, tiles], M.std[:, tiles], ACT.Sqrt).then_inc(S.std_ready[0], 1)
                if stage is not None and 1 <= stage < B:
                    _, halves = staged(stage)
                    act.wait_ge(S.turned, stage)
                    if stage > 2:
                        act.wait_ge(S.x_stored[stage % 2], 16)
                    nc.scalar.copy(halves[:, 0], M.psS[:].rearrange("p a n -> p (a n)")).then_inc(S.split_hi, 1)
                for Uw, n in pairs_at(s, u, ACT_LAG):
                    out_lo(Uw, n)
                for item in at.get((s, u), []):
                    if item[1] != "qk":
                        side(item)
                for item in at.get((s, u - ROPE_LAG), []):
                    if item[1] == "qk":
                        side(item)

        @blk.vector
        def _(dve):
            def low(U):
                w = UNITS[U % NU][2]
                dve.wait_ge(S.exp_done, U + 1)
                nc.vector.tensor_tensor(M.Plo[:, U % NP_, 0:w], M.P32[:, U % NP_, 0:w], M.Phi[:, U % NP_, 0:w],
                                        ALU.subtract).then_inc(S.lo_dve, 1)

            def side(item):
                s, kind, *a = item
                X = M.psX[:, bank(item), :]
                p = (s + 1) % 2
                if kind == "qk":
                    which, n, half = a
                    r = 4 * ropes(s) + 2 * which + n
                    cols = slice(n * BANK, (n + 1) * BANK)
                    ready(dve, item)
                    if half == 0:
                        if r > 0:
                            dve.wait_ge(S.rope_sum, r)
                        nc.vector.tensor_tensor(M.R4[:, 0, :], X, M.cos[:, cols], ALU.mult)
                        nc.vector.tensor_tensor(M.R4[:, 2, :], X, M.sin[:, cols], ALU.mult).then_inc(free(item), 1)
                    else:
                        nc.vector.tensor_tensor(M.R4[:, 1, :], X, M.sin[:, cols], ALU.mult)
                        nc.vector.tensor_tensor(M.R4[:, 3, :], X, M.cos[:, cols], ALU.mult).then_inc(free(item), 1)
                elif kind == "v":
                    dve.wait_ge(S.v_hi, 4 * (loads(s) - 1) + a[0] + 1)
                    nc.vector.tensor_tensor(M.V[:, p, 2 * a[0]:2 * a[0] + 2, :, 0:HD],
                                            X.rearrange("p (t h d) -> p t h d", t=2, h=GH),
                                            M.V[:, p, 2 * a[0]:2 * a[0] + 2, :, HD:2 * HD],
                                            ALU.subtract).then_inc(free(item), 1)
                elif kind == "mx":
                    h, k = a
                    t, c, w = MAXP[k]
                    ready(dve, item)
                    top = M.pmax[:, int(c > 0), h, t:t + 1]
                    if c + w == (t + 1) * P:
                        nc.vector.tensor_tensor_reduce(out=X[:, 0:w], in0=X[:, 0:w], in1=M.maskN[:, BANK - w:BANK],
                                                       scale=1.0, scalar=LOWEST, op0=ALU.add, op1=ALU.max,
                                                       accum_out=top).then_inc(free(item), 1)
                    else:
                        nc.vector.tensor_reduce(top, X[:, 0:w], AX.X, ALU.max).then_inc(free(item), 1)
                    if h == GH - 1 and k == len(MAXP) - 1:
                        taken(dve, item)
                        if s > 0:
                            ready(dve, (s - 1, "mt"))
                        nc.vector.tensor_tensor(M.rmax[:], M.pmax[:, 0].rearrange("p h t -> p (h t)"),
                                                M.pmax[:, 1].rearrange("p h t -> p (h t)"),
                                                ALU.max).then_inc(S.row_max, 1)
                elif kind == "wo":
                    ready(dve, item)
                    y = M.y[:, bass.ds((b + int(s > 0)) * TT + 4 * a[0], 4), :].rearrange("p t d -> p (t d)")
                    if s == 1:
                        nc.vector.tensor_copy(y, X).then_inc(free(item), 1)
                    else:
                        if s > 0:
                            taken(dve, (s - 1, "wo", a[0]))
                        nc.vector.tensor_tensor(y, X, y, ALU.add).then_inc(free(item), 1)

            def y_statistics(batch):
                dve.wait_ge(S.stats, NT - TT)
                for n in range(batch * TT, (batch + 1) * TT):
                    last = nc.vector.bn_aggr(M.mv[:, n, :], M.bn[:, n, :])
                last.then_inc(S.stats, 1)
                dve.wait_ge(S.stats, NT - TT + batch + 1)
                tiles = slice(batch * TT, (batch + 1) * TT)
                nc.vector.tensor_scalar(M.std[:, tiles], M.mv[:, tiles, 1], EPS, None, ALU.add)

            def ln_step(stage):
                if stage is None:
                    return
                if 2 <= stage <= B:
                    _, halves = staged(stage - 1)
                    dve.wait_ge(S.split_hi, stage - 1)
                    nc.vector.tensor_tensor(halves[:, 1], M.psS[:].rearrange("p a n -> p (a n)"), halves[:, 0],
                                            ALU.subtract).then_inc(S.split_lo, 1)
                if 1 <= stage < B:
                    x, _ = staged(stage)
                    tiles = slice(stage * TT, (stage + 1) * TT)
                    dve.wait_ge(S.std_ready[0], stage)
                    nc.vector.reciprocal(M.rstd[:, tiles], M.std[:, tiles]).then_inc(S.stats, 1)
                    dve.wait_ge(S.stats, 3 * stage)
                    for t in range(TT):
                        n = stage * TT + t
                        last = nc.vector.tensor_scalar(x[:, t, :], x[:, t, :], M.mv[:, n, 0:1], M.rstd[:, n:n + 1],
                                                       ALU.subtract, ALU.mult)
                    last.then_inc(S.norm_ready, 1)
                if stage < B - 1:
                    batch = stage + 1
                    x, _ = staged(batch)
                    dve.wait_ge(S.x_load[batch], 16)
                    for t in range(TT):
                        last = nc.vector.bn_stats(M.bn[:, batch * TT + t, :], x[:, t, :])
                    last.then_inc(S.stats, 1)
                    dve.wait_ge(S.stats, 3 * stage + 1)
                    for n in range(batch * TT, (batch + 1) * TT):
                        last = nc.vector.bn_aggr(M.mv[:, n, :], M.bn[:, n, :])
                    last.then_inc(S.stats, 1)
                    dve.wait_ge(S.stats, 3 * stage + 2)
                    tiles = slice(batch * TT, (batch + 1) * TT)
                    nc.vector.tensor_scalar(M.std[:, tiles], M.mv[:, tiles, 1], EPS, None,
                                            ALU.add).then_inc(S.var_ready[0], 1)

            def out_add(Uw, n):
                O = M.psO[:, n % 3, :].rearrange("p (t c) -> p t c", t=2)
                dve.wait_ge(S.out_lo, n + 1)
                if n >= NO:
                    dve.wait_ge(S.out_scaled, n - NO + 1)
                nc.vector.reciprocal(M.rsum[:, n % NO, :, :], O[:, :, 2 * HD:2 * HD + 1])
                nc.vector.tensor_tensor(M.Osum[:, n % NO], O[:, :, HD:2 * HD], M.Olo[:, n % NO],
                                        ALU.add).then_inc(S.out_added, 1)

            for s, u in steps:
                U = SU * s + u - LO_LAG
                ln_step(ln_stage(s, u))
                if flush and s == GROUPS - 1 and 0 <= u - STAT_FIRST < NT - TT:
                    n = u - STAT_FIRST
                    nc.vector.bn_stats(M.bn[:, n, :], M.y[:, TT + n, :]).then_inc(S.stats, 1)
                if flush and s == GROUPS - 1 and u in STAT_STEPS:
                    y_statistics(STAT_STEPS.index(u))
                for item in at.get((s, u), []) if s < GROUPS else []:
                    side(item)
                if s >= 0 and 0 <= U <= last_unit and not lo_on_pool(U % SU):
                    low(U)
                for Uw, n in pairs_at(s, u, OUT_LAG):
                    out_add(Uw, n)
                for item in at.get((s, u), []) if s == GROUPS else []:
                    side(item)

        @blk.gpsimd
        def _(pool):
            def low(U):
                w = UNITS[U % NU][2]
                pool.wait_ge(S.exp_done, U + 1)
                nc.gpsimd.tensor_tensor(M.Plo[:, U % NP_, 0:w], M.P32[:, U % NP_, 0:w], M.Phi[:, U % NP_, 0:w],
                                        ALU.subtract).then_inc(S.lo_pool, 1)

            def rotate(item, second):
                s, kind, *a = item
                if kind != "qk" or a[2] == 0:
                    return
                which, n, _ = a
                r = 4 * ropes(s) + 2 * which + n
                cols = slice(n * BANK, (n + 1) * BANK)
                if not second:
                    taken(pool, item)
                    if r > 0:
                        pool.wait_ge(S.rope_lo, r)
                    nc.gpsimd.tensor_tensor(M.R[:, 0, :], M.R4[:, 0, :], M.R4[:, 1, :], ALU.subtract)
                    nc.gpsimd.tensor_tensor(M.R[:, 1, :], M.R4[:, 2, :], M.R4[:, 3, :],
                                            ALU.add).then_inc(S.rope_sum, 1)
                    return
                pool.wait_ge(S.rope_hi, r + 1)
                nc.gpsimd.tensor_tensor(M.HL[:, which, 2:4, cols], M.R[:], M.HL[:, which, 0:2, cols],
                                        ALU.subtract).then_inc(S.rope_lo, 1)

            def out_scale(n):
                head = n // 4
                h, q = head % GH, n % 4
                pool.wait_ge(S.out_added, n + 1)
                own = head // GH
                if q == 0 and h % 2 == 0:
                    turned = (own - 1, "tr", 0, 1) if h == 0 else (own, "tr", 1, 1)
                    if turned in number:
                        ready(pool, turned)
                nc.gpsimd.tensor_tensor(M.On[:, 2 * q:2 * q + 2, h * HD:(h + 1) * HD], M.Osum[:, n % NO],
                                        M.rsum[:, n % NO].to_broadcast([P, 2, HD]),
                                        ALU.mult).then_inc(S.out_scaled, 1)

            for s, u in steps:
                U = SU * s + u - LO_LAG
                if s >= 0 and 0 <= U <= last_unit and lo_on_pool(U % SU):
                    low(U)
                for item in at.get((s, u - SUM_LAG), []):
                    rotate(item, False)
                for item in at.get((s, u - REST_LAG), []):
                    rotate(item, True)
                for _, n in pairs_at(s, u, SCALE_LAG):
                    out_scale(n)

        @blk.sync
        def _(sp):
            def load(s):
                p = (s + 1) % 2
                if s > 0:
                    sp.wait_ge(S.scores_ready, SU * s)
                krows = M.k_way.rearrange("k f h n -> (k f) h n")
                qrows = M.q_way.rearrange("k f h n -> (k f) h n")
                if s > first:
                    sp.wait_ge(S.k_out, 16 * GH * ropes(s))
                    sp.wait_ge(S.q_out, 16 * GH * ropes(s))
                for i in range(2):
                    h = slice(2 * i, 2 * i + 2)
                    sp.dma_start(M.K1[:, p, h], krows[:, h]).then_inc(S.near_in[i], 16)
                    sp.dma_start(M.Q1[0:HD, p, h], qrows[0:HD, h]).then_inc(S.near_in[i], 16)
                    sp.dma_start(M.Q1[HD:P, p, h], qrows[0:HD, h]).then_inc(S.near_in[i], 16)
                sp.dma_start(M.K2[0:HD, p], krows[0:HD]).then_inc(S.far_in, 16)
                sp.dma_start(M.Q2[0:HD, p], qrows[HD:P]).then_inc(S.far_in, 16)

            def send(s, which):
                way, sent = (M.q_way, S.q_out) if which else (M.k_way, S.k_out)
                sp.wait_ge(S.rope_lo, 4 * ropes(s) + 2 * which + 2)
                if which == 0 and loads(s) > 0:
                    for i in range(2):
                        sp.wait_ge(S.near_in[i], 48 * loads(s))
                    sp.wait_ge(S.far_in, 32 * loads(s))
                for h in range(GH):
                    sp.dma_start(way[:, :, h, :].rearrange("k f n -> f k n"),
                                 M.HL[h * HALF:(h + 1) * HALF, which, :, :]).then_inc(sent, 16)

            def store(batch):
                _, halves = staged(batch)
                sp.wait_ge(S.split_lo, batch)
                sp.dma_start(M.x_way[:, :, batch * T:(batch + 1) * T], halves).then_inc(S.x_stored[batch % 2], 16)

            if first < 0:
                for batch in range(1, B):
                    x, _ = staged(batch)
                    sp.dma_start(x, M.x_tiles[:, batch * TT:(batch + 1) * TT, :]).then_inc(S.x_load[batch], 16)
            for s in slots:
                if s in near:
                    load(s)
                if s in far:
                    send(s, 0)
                    if first < 0 and s == first:
                        store(1)
                    send(s, 1)
                    if first < 0 and s == first:
                        for batch in range(2, B):
                            store(batch)
                    if s == GROUPS - 3 and s + 1 in far:
                        ready(sp, (s, "qk", 1, 1, 1))
                        sp.dma_start(M.xq[:], M.x_way[:, :, bass.ds((b + 1) * T, T)]).then_inc(S.xq_in, 16)
                if s in near:
                    taken(sp, (s, "mt"))
                    sp.dma_start(M.Q2[HD:HD + 1, (s + 1) % 2, :, :].rearrange("o h (t i) -> o (h t) i", i=P),
                                 M.mrow[:]).then_inc(S.row_max_in, 16)
                    if s == GROUPS - 2 and s + 1 in near:
                        ready(sp, (s, "v", TT // 2 - 1))
                        sp.dma_start(M.xv[:], M.x_way[:, :, bass.ds((b + 1) * T, T)]).then_inc(S.xv_in, 16)
            if first < 0:
                for i in range(2):
                    sp.wait_ge(S.x_stored[i], 16 * len(range(2 - i, B, 2)))
            if far:
                sp.wait_ge(S.k_out, 16 * GH * len(far))
                sp.wait_ge(S.q_out, 16 * GH * len(far))
            sp.wait_ge(S.far_in, 32 * len(near))
            sp.wait_ge(S.row_max_in, 16 * len(near))


def block_end(nc, S):
    nc.sync.sem_clear(range(S.first, S.last + 1))
    nc.all_engine_barrier()


def load_block(nc, I, M, S, stack, sb, ps):
    xs = sb(stack, "xs", [P, TT, D], F32)
    xn = sb(stack, "xn", [P, TT, D], F32)
    xT = sb(stack, "xT", [P, 2, T], F16)
    w32 = sb(stack, "w32", [P, 3, HEADS * HD], F32)
    bn = sb(stack, "bn", [P, TT, 6], F32)
    mv = sb(stack, "mv", [P, TT, 2], F32)
    std = sb(stack, "std", [P, TT], F32)
    rstd = sb(stack, "rstd", [P, TT], F32)
    psT = ps(stack, "psT", [P, 2, BANK], F32)
    NB = T // BANK
    TB = BANK // P
    HT = TT // 2
    weights = (M.wkq[:, 0], M.wkq[:, 1], M.wv)
    with nc.Block() as blk:
        @blk.sync
        def _(sp):
            for b in range(2):
                tiles = slice(b * HT, (b + 1) * HT)
                sp.dma_start(xs[:, tiles, :], M.x_tiles[:, tiles, :]).then_inc(S.x_load[b], 16)
            for k, w in enumerate((I["wk"], I["wq"], I["wv"])):
                sp.dma_start(w32[:, k, :], w).then_inc(S.w_load[k], 16)
            sp.dma_start(M.wo[:], I["wo"]).then_inc(S.c_in, 16)
            sp.dma_start(M.cos[:], I["cos"]).then_inc(S.c_in, 16)
            sp.dma_start(M.sin[:], I["sin"]).then_inc(S.c_in, 16)
            sp.wait_ge(S.split_lo, NB)
            sp.dma_start(M.xq[:], xT[:]).then_inc(S.xq_in, 16)
            sp.dma_start(M.xv[:], xT[:]).then_inc(S.xv_in, 16)
            sp.wait_ge(S.c_in, 48)
            sp.wait_ge(S.xq_in, 16)
            sp.wait_ge(S.xv_in, 16)

        @blk.gpsimd
        def _(pool):
            nc.gpsimd.memset(M.ident[:], 0.0)
            nc.gpsimd.memset(M.ident16[:], 0.0)
            nc.gpsimd.memset(M.maskT[:], 0.0)
            nc.gpsimd.memset(M.maskN[:], 0.0).then_inc(S.consts, 1)
            pool.wait_ge(S.consts, 1)
            for t in (M.ident, M.ident16):
                nc.gpsimd.affine_select(out=t[:], in_=t[:], compare_op=ALU.not_equal, fill=1.0, base=0,
                                        pattern=[[-1, P]], channel_multiplier=1)
            nc.gpsimd.affine_select(out=M.maskT[:], in_=M.maskT[:], compare_op=ALU.is_ge, fill=NEG, base=0,
                                    pattern=[[1, P]], channel_multiplier=-1)
            nc.gpsimd.affine_select(out=M.maskN[:, BANK - P:], in_=M.maskN[:, BANK - P:], compare_op=ALU.is_ge,
                                    fill=NEG, base=0, pattern=[[-1, P]], channel_multiplier=1).then_inc(S.consts, 1)
            nc.gpsimd.memset(M.V[:, :, :, :, 2 * HD:2 * HD + 1].rearrange("p a t h o -> p (a t h) o"), 1.0)
            nc.gpsimd.memset(M.pmax[:], LOWEST)
            for t in (M.On[:], M.OT[:], M.y[:, 0:TT]):
                nc.gpsimd.memset(t, 0.0)
            pool.wait_ge(S.w_hi, 1)
            nc.gpsimd.tensor_tensor(weights[0][:, 1, :], w32[:, 0, :], weights[0][:, 0, :], ALU.subtract)

        @blk.vector
        def _(dve):
            done = [0]

            def then(ins):
                done[0] += 1
                ins.then_inc(S.stats, 1)
                dve.wait_ge(S.stats, done[0])

            def variance(b):
                dve.wait_ge(S.x_load[b], 16)
                tiles = range(b * HT, (b + 1) * HT)
                for t in tiles:
                    last = nc.vector.bn_stats(bn[:, t, :], xs[:, t, :])
                then(last)
                for t in tiles:
                    last = nc.vector.bn_aggr(mv[:, t, :], bn[:, t, :])
                then(last)
                tiles = slice(b * HT, (b + 1) * HT)
                nc.vector.tensor_scalar(std[:, tiles], mv[:, tiles, 1], EPS, None, ALU.add).then_inc(S.var_ready[0], 1)

            def normal(b):
                tiles = slice(b * HT, (b + 1) * HT)
                dve.wait_ge(S.std_ready[0], b + 1)
                then(nc.vector.reciprocal(rstd[:, tiles], std[:, tiles]))
                for t in range(b * HT, (b + 1) * HT):
                    nc.vector.tensor_scalar(xn[:, t, :], xs[:, t, :], mv[:, t, 0:1], rstd[:, t:t + 1],
                                            ALU.subtract, ALU.mult).then_inc(S.norm_ready, 1)

            def low(b):
                for k in range(b * NB // 2, (b + 1) * NB // 2):
                    dve.wait_ge(S.split_hi, k + 1)
                    cols = slice(k * BANK, (k + 1) * BANK)
                    nc.vector.tensor_tensor(xT[:, 1, cols], psT[:, k % 2, :], xT[:, 0, cols],
                                            ALU.subtract).then_inc(S.split_lo, 1)

            for k in range(4):
                if k < 2:
                    variance(k)
                if 1 <= k <= 2:
                    normal(k - 1)
                if k >= 2:
                    low(k - 2)
            nc.vector.memset(M.K2[HD:HD + 1], MSCALE)
            for k in (1, 2):
                dve.wait_ge(S.w_hi, k + 1)
                nc.vector.tensor_tensor(weights[k][:, 1, :], w32[:, k, :], weights[k][:, 0, :], ALU.subtract)

        @blk.scalar
        def _(act):
            for k in range(2):
                tiles = slice(k * HT, (k + 1) * HT)
                act.wait_ge(S.var_ready[0], k + 1)
                nc.scalar.activation(std[:, tiles], std[:, tiles], ACT.Sqrt).then_inc(S.std_ready[0], 1)
            for n in range(NB):
                act.wait_ge(S.turned, n + 1)
                nc.scalar.copy(xT[:, 0, n * BANK:(n + 1) * BANK], psT[:, n % 2, :]).then_inc(S.split_hi, 1)
            for k in range(len(weights)):
                act.wait_ge(S.w_load[k], 16)
                nc.scalar.copy(weights[k][:, 0, :], w32[:, k, :]).then_inc(S.w_hi, 1)

        @blk.tensor
        def _(pe):
            pe.wait_ge(S.consts, 2)
            for k in range(NB):
                pe.wait_ge(S.norm_ready, TB * k + TB)
                if k >= 2:
                    pe.wait_ge(S.split_lo, k - 1)
                for i in range(TB):
                    mm = nc.tensor.transpose(psT[:, k % 2, i * P:(i + 1) * P], xn[:, TB * k + i, :], M.ident[:])
                mm.then_inc(S.turned, 1)
    block_end(nc, S)


def phase_attention(nc, I, M, S, sb, ps):
    with ExitStack() as stack:
        M.wkq = sb(stack, "wkq", [P, 2, 2, HEADS * HD], F16)
        M.wv = sb(stack, "wv", [P, 2, HEADS * HD], F16)
        M.wo = sb(stack, "wo", [P, HEADS * HD // P, D], F32)
        M.cos = sb(stack, "cos", [P, T], F32)
        M.sin = sb(stack, "sin", [P, T], F32)
        M.ident16 = sb(stack, "ident16", [P, P], BF16)
        M.maskT = sb(stack, "maskT", [P, P], BF16)
        M.maskN = sb(stack, "maskN", [P, BANK], BF16)
        M.x_tiles = I["x"].rearrange("b (t p) d -> p (b t) d", p=P)
        M.K2 = sb(stack, "K2", [P, 2, GH, T], F16)
        M.V = sb(stack, "V", [P, 2, TT, GH, VW], F16)
        M.pmax = sb(stack, "pmax", [P, 2, GH, TT], F32)
        M.xq = sb(stack, "xq", [P, 2, T], F16)
        M.xv = sb(stack, "xv", [P, 2, T], F16)
        M.On = sb(stack, "On", [P, TT, GH * HD], F32)
        M.OT = sb(stack, "OT", [P, CH, T], F32)
        with ExitStack() as temps:
            load_block(nc, I, M, S, temps, sb, ps)
        M.K1 = sb(stack, "K1", [P, 2, GH, T], F16)
        M.Q1 = sb(stack, "Q1", [P, 2, GH, T], F16)
        M.Q2 = sb(stack, "Q2", [P, 2, GH, T], F16)
        M.P32 = sb(stack, "P32", [P, NP_, BANK], F32)
        M.Phi = sb(stack, "Phi", [P, NP_, BANK], F16)
        M.Plo = sb(stack, "Plo", [P, NP_, BANK], F16)
        M.R4 = sb(stack, "R4", [P, 4, BANK], F32)
        M.R = sb(stack, "R", [P, 2, BANK], F32)
        M.HL = sb(stack, "HL", [P, 2, 4, T], F16)
        M.Olo = sb(stack, "Olo", [P, NO, 2, HD], F32)
        M.Osum = sb(stack, "Osum", [P, NO, 2, HD], F32)
        M.rsum = sb(stack, "rsum", [P, NO, 2, 1], F32)
        M.rmax = sb(stack, "rmax", [P, GH * TT], F32)
        M.mrow = sb(stack, "mrow", [GH * TT, P], F16)
        M.psS = ps(stack, "psS", [P, 2, BANK], F32)
        M.psO = ps(stack, "psO", [P, 3, BANK], F32)
        M.psX = ps(stack, "psX", [P, NAUX, BANK], F32)
        attention_block(nc, M, S, 0, [-2, -1], [-1], [-2, -1])
        block_end(nc, S)
        slots = list(range(GROUPS))
        with nc.Fori(0, B - 1) as b:
            attention_block(nc, M, S, b, slots, slots, slots)
            block_end(nc, S)
        attention_block(nc, M, S, B - 1, slots, slots[:-1], slots[:-2], flush=True)
        block_end(nc, S)


def norm_block(nc, I, M, S, stack, sb, ps):
    zn = sb(stack, "zn", [P, 2, NT, D], F32)
    bn = (M.bn, sb(stack, "bn3", [P, NT, 6], F32))
    mv = (M.mv, sb(stack, "mv3", [P, NT, 2], F32))
    std = (M.std, sb(stack, "std3", [P, NT], F32))
    rstd = (M.rstd, sb(stack, "rstd3", [P, NT], F32))
    shift = sb(stack, "shift3", [P, NT], F32)
    zT = sb(stack, "zT", [P, 2, BANK], F32)
    psT = ps(stack, "psT3", [P, 2, BANK], F32)
    psH = ps(stack, "psH3", [P, 2, BANK], F32)
    x_tiles = I["x"].rearrange("b (t p) d -> p (b t) d", p=P)
    TB = BANK // P
    NB = NT // TB
    CT = 2 * TB
    NCH = NT // CT
    with nc.Block() as blk:
        @blk.sync
        def _(sp):
            for c in range(NCH):
                tiles = slice(c * CT, (c + 1) * CT)
                sp.dma_start(M.x1[:, tiles], x_tiles[:, tiles]).then_inc(S.x_load[c], 16)
            sp.dma_start(M.wd[:, 0, :], I["lin0_w"]).then_inc(S.lin0_in, 16)
            sp.dma_start(M.bias[:, 0:1], I["lin0_b"].rearrange("(d o) -> d o", o=1)).then_inc(S.lin0_in, 16)
            for k, w in enumerate((I["swi1_w1"], I["swi1_w2"], I["lin1_w"], I["swi2_w1"], I["swi2_w2"])):
                sp.dma_start(M.wd[:, k + 1, :], w).then_inc(S.w_in, 16)
            for k, w in enumerate((I["swi1_b1"], I["swi1_b2"], I["lin1_b"], I["swi2_b1"], I["swi2_b2"])):
                sp.dma_start(M.bias[:, k + 1:k + 2], w.rearrange("(d o) -> d o", o=1)).then_inc(S.w_in, 16)
            sp.dma_start(M.gate[:], I["gate_w"]).then_inc(S.w_in, 16)
            sp.dma_start(M.we[:, 0, 0:E], I["exp_w1"].rearrange("e d h -> d e h")).then_inc(S.w_in, 16)
            sp.dma_start(M.we[:, 1, 0:E], I["exp_w3"].rearrange("e d h -> d e h")).then_inc(S.w_in, 16)
            sp.dma_start(M.we[:, 2, 0:E], I["exp_w2"].rearrange("e h d -> h e d")).then_inc(S.w_in, 16)
            sp.dma_start(M.we[:, 0, E:E + NC], I["sh_w1"].rearrange("d (c h) -> d c h", h=H)).then_inc(S.w_in, 16)
            sp.dma_start(M.we[:, 1, E:E + NC], I["sh_w3"].rearrange("d (c h) -> d c h", h=H)).then_inc(S.w_in, 16)
            sp.dma_start(M.we[:, 2, E:E + NC], I["sh_w2"].rearrange("(c h) d -> h c d", h=H)).then_inc(S.w_in, 16)
            sp.wait_ge(S.w_in, 16 * 17)

        @blk.vector
        def _(dve):
            done = [0]

            def then(ins):
                done[0] += 1
                ins.then_inc(S.stats, 1)
                dve.wait_ge(S.stats, done[0])

            def variance(i, c):
                if i == 1:
                    dve.wait_ge(S.x1_ready, CT * (c + 1))
                tiles = range(c * CT, (c + 1) * CT)
                src = (M.y[:, TT:], M.x1)[i]
                for t in tiles:
                    last = nc.vector.bn_stats(bn[i][:, t, :], src[:, t, :])
                then(last)
                for t in tiles:
                    last = nc.vector.bn_aggr(mv[i][:, t, :], bn[i][:, t, :])
                then(last)
                tiles = slice(c * CT, (c + 1) * CT)
                nc.vector.tensor_scalar(std[i][:, tiles], mv[i][:, tiles, 1], EPS, None,
                                        ALU.add).then_inc(S.var_ready[i], 1)

            def inverse(i, c):
                tiles = slice(c * CT, (c + 1) * CT)
                dve.wait_ge(S.std_ready[i], c + 1)
                then(nc.vector.reciprocal(rstd[i][:, tiles], std[i][:, tiles]))
                if i == 1:
                    for t in range(c * CT, (c + 1) * CT):
                        nc.vector.tensor_scalar(zn[:, 1, t, :], M.x1[:, t, :], mv[1][:, t, 0:1], rstd[1][:, t:t + 1],
                                                ALU.subtract, ALU.mult).then_inc(S.normal_ready[1], 1)
                    return
                nc.vector.scalar_tensor_tensor(out=shift[:, tiles], in0=mv[i][:, tiles, 0], scalar=-1.0,
                                               in1=rstd[i][:, tiles], op0=ALU.mult,
                                               op1=ALU.mult).then_inc(S.rstd_ready[0], 1)

            for k in range(NCH + 3):
                if k == NCH - 1:
                    variance(0, k)
                if 1 <= k <= NCH:
                    inverse(0, k - 1)
                if 2 <= k <= NCH + 1:
                    variance(1, k - 2)
                if k >= 3:
                    inverse(1, k - 3)
            nc.vector.memset(M.tri[:], 1.0)

        @blk.scalar
        def _(act):
            def root(i, c):
                tiles = slice(c * CT, (c + 1) * CT)
                if i == 1:
                    act.wait_ge(S.var_ready[1], c + 1)
                elif c == NCH - 1:
                    act.wait_ge(S.var_ready[0], 1)
                nc.scalar.activation(std[i][:, tiles], std[i][:, tiles], ACT.Sqrt).then_inc(S.std_ready[i], 1)

            def normal(c):
                act.wait_ge(S.rstd_ready[0], c + 1)
                for t in range(c * CT, (c + 1) * CT):
                    nc.scalar.activation(zn[:, 0, t, :], M.y[:, TT + t, :], ACT.Identity, scale=rstd[0][:, t:t + 1],
                                         bias=shift[:, t:t + 1]).then_inc(S.normal_ready[0], 1)

            def turned_out(k):
                act.wait_ge(S.turned, k + 1)
                if k >= 2:
                    act.wait_ge(S.lin0_mm, k - 1)
                nc.scalar.copy(zT[:, k % 2, :], psT[:, k % 2, :]).then_inc(S.turned_out, 1)

            def lin0_out(k):
                act.wait_ge(S.lin0_mm, k + 1)
                nc.scalar.activation(M.h0T[:, k * BANK:(k + 1) * BANK], psH[:, k % 2, :], ACT.Identity,
                                     bias=M.bias[:, 0:1]).then_inc(S.lin0_out, 1)

            for k in range(NCH + 3):
                if k < NCH:
                    root(0, k)
                if 1 <= k <= NCH:
                    normal(k - 1)
                if 2 <= k <= NCH + 1:
                    root(1, k - 2)
                if k >= 3:
                    if k == 3:
                        act.wait_ge(S.lin0_in, 32)
                    for n in range(2 * (k - 3), 2 * (k - 3) + 2):
                        turned_out(n)
                        if n >= 1:
                            lin0_out(n - 1)
            lin0_out(NB - 1)

        @blk.gpsimd
        def _(pool):
            for t in range(NT):
                if t % CT == 0:
                    pool.wait_ge(S.x_load[t // CT], 16)
                pool.wait_ge(S.normal_ready[0], t + 1)
                nc.gpsimd.tensor_tensor(M.x1[:, t, :], M.x1[:, t, :], zn[:, 0, t, :], ALU.add).then_inc(S.x1_ready, 1)

        @blk.tensor
        def _(pe):
            pe.wait_ge(S.lin0_in, 32)
            for k in range(NB + 1):
                if k < NB:
                    pe.wait_ge(S.normal_ready[1], TB * k + TB)
                    if k >= 2:
                        pe.wait_ge(S.turned_out, k - 1)
                    for i in range(TB):
                        mm = nc.tensor.transpose(psT[:, k % 2, i * P:(i + 1) * P], zn[:, 1, TB * k + i, :], M.ident[:])
                    mm.then_inc(S.turned, 1)
                if k >= 1:
                    i = k - 1
                    pe.wait_ge(S.turned_out, i + 1)
                    if i >= 2:
                        pe.wait_ge(S.lin0_out, i - 1)
                    nc.tensor.matmul(psH[:, i % 2, :], M.wd[:, 0, :], zT[:, i % 2, :],
                                     start=True, stop=True).then_inc(S.lin0_mm, 1)
    block_end(nc, S)


def front_block(nc, M, S, stack, sb, ps):
    sg = sb(stack, "sg", [P, 2, BANK], F32)
    psG = ps(stack, "psG", [P, 2, BANK], F32)
    psU = ps(stack, "psU", [P, 2, BANK], F32)
    psL = ps(stack, "psL", [P, NT, E], F32)
    NB = NT * P // BANK
    TB = BANK // P
    with nc.Block() as blk:
        @blk.tensor
        def _(pe):
            for k in range(NB + 2):
                if k < NB:
                    if k >= 2:
                        pe.wait_ge(S.h1_ready, k - 1)
                    x = M.h0T[:, k * BANK:(k + 1) * BANK]
                    nc.tensor.matmul(psG[:, k % 2, :], M.wd[:, 1, :], x, start=True, stop=True).then_inc(S.swi_mm, 1)
                    nc.tensor.matmul(psU[:, k % 2, :], M.wd[:, 2, :], x, start=True, stop=True).then_inc(S.swi_mm, 1)
                if k >= 2:
                    i = k - 2
                    pe.wait_ge(S.h1_ready, i + 1)
                    for t in range(TB * i, TB * i + TB):
                        mm = nc.tensor.matmul(psL[:, t, :], M.h1T[:, t * P:(t + 1) * P], M.gate[:],
                                              start=True, stop=True)
                    mm.then_inc(S.logits_mm, 1)

        @blk.scalar
        def _(act):
            for k in range(NB + 1):
                if k < NB:
                    act.wait_ge(S.swi_mm, 2 * k + 1)
                    if k >= 2:
                        act.wait_ge(S.h1_ready, k - 1)
                    nc.scalar.activation(sg[:, k % 2, :], psG[:, k % 2, :], ACT.Silu,
                                         bias=M.bias[:, 1:2]).then_inc(S.silu_done, 1)
                if k < 3:
                    nc.scalar.copy(M.ws[:, 0, k], M.we[:, k]).then_inc(S.split_hi, 1)
                if k >= 1:
                    i = k - 1
                    act.wait_ge(S.h1_ready, i + 1)
                    cols = slice(i * BANK, (i + 1) * BANK)
                    nc.scalar.copy(M.h1s[:, 0, cols], M.h1T[:, cols]).then_inc(S.h1_hi, 1)

        @blk.gpsimd
        def _(pool):
            nc.gpsimd.affine_select(out=M.tri[:], in_=M.tri[:], compare_op=ALU.is_ge, fill=0.0, base=-1,
                                    pattern=[[1, E], [-1, E]], channel_multiplier=0)
            for k in range(3):
                pool.wait_ge(S.split_hi, k + 1)
                nc.gpsimd.tensor_tensor(M.ws[:, 1, k], M.we[:, k], M.ws[:, 0, k], ALU.subtract)

        @blk.vector
        def _(dve):
            for k in range(NB + 1):
                if k < NB:
                    dve.wait_ge(S.silu_done, k + 1)
                    dve.wait_ge(S.swi_mm, 2 * k + 2)
                    nc.vector.scalar_tensor_tensor(out=M.h1T[:, k * BANK:(k + 1) * BANK], in0=psU[:, k % 2, :],
                                                   scalar=M.bias[:, 2:3], in1=sg[:, k % 2, :],
                                                   op0=ALU.add, op1=ALU.mult).then_inc(S.h1_ready, 1)
                if k >= 1:
                    dve.wait_ge(S.h1_hi, k)
                    cols = slice((k - 1) * BANK, k * BANK)
                    nc.vector.tensor_tensor(M.h1s[:, 1, cols], M.h1T[:, cols], M.h1s[:, 0, cols], ALU.subtract)
            dve.wait_ge(S.logits_mm, NB)
            nc.vector.tensor_copy(M.logit[:], psL[:])
    block_end(nc, S)


def routing_steps(nc, M, S, R, dve):
    logit, score, small, more, same, rank = M.logit, R.score, R.small, R.more, R.same, R.rank

    def wide(ap):
        return ap.to_broadcast([P, NT, E])

    done = 0

    def then(ins):
        nonlocal done
        done += 1
        ins.then_inc(S.route_step, 1)
        dve.wait_ge(S.route_step, done)

    then(nc.vector.tensor_reduce(small[:, 0, :, 0], logit[:], AX.X, ALU.max))
    nc.vector.tensor_tensor(logit[:], logit[:], wide(small[:, 0]), ALU.subtract).then_inc(S.route_shifted, 1)
    yield
    dve.wait_ge(S.route_exp, 1)
    then(nc.vector.tensor_reduce(small[:, 1, :, 0], score[:], AX.X, ALU.add))
    then(nc.vector.reciprocal(small[:, 2], small[:, 1]))
    then(nc.vector.tensor_tensor(score[:], score[:], wide(small[:, 2]), ALU.mult))
    yield
    own = score[:].unsqueeze(3).to_broadcast([P, NT, E, E])
    other = score[:].unsqueeze(2).to_broadcast([P, NT, E, E])
    tri = M.tri[:].unsqueeze(1).to_broadcast([P, NT, E, E])
    for h in (slice(0, NT // 2), slice(NT // 2, NT)):
        then(nc.vector.tensor_tensor(same[:, h], other[:, h], own[:, h], ALU.is_equal))
        yield
        then(nc.vector.tensor_tensor(same[:, h], same[:, h], tri[:, h], ALU.mult))
        yield
        then(nc.vector.tensor_tensor(more[:, h], other[:, h], own[:, h], ALU.is_gt))
        yield
        then(nc.vector.tensor_tensor(more[:, h], more[:, h], same[:, h], ALU.add))
        yield
        then(nc.vector.tensor_reduce(rank[:, h], more[:, h], AX.X, ALU.add))
        yield
    then(nc.vector.tensor_scalar(rank[:], rank[:], TOPK - 0.5, None, ALU.is_lt))
    then(nc.vector.tensor_tensor(rank[:], rank[:], score[:], ALU.mult))
    yield
    then(nc.vector.tensor_reduce(small[:, 3, :, 0], rank[:], AX.X, ALU.add))
    then(nc.vector.reciprocal(small[:, 0], small[:, 3]))
    then(nc.vector.tensor_tensor(M.comb[:], rank[:], wide(small[:, 0]), ALU.mult))
    yield


def expert_block(nc, M, S, R, base, work, per, routing):
    TB = BANK // P
    W = len(work)
    BACK = 2
    with nc.Block() as blk:
        @blk.tensor
        def _(pe):
            def hidden(n):
                k, c = work[n]
                if n >= 2:
                    pe.wait_ge(S.gated, n - 1)
                for j, bank in enumerate((R.psG, R.psU)):
                    for q, (wi, xi) in enumerate([(0, 0), (0, 1), (1, 0)]):
                        mm = nc.tensor.matmul(bank[:, n % 2, :], M.ws[:, wi, j, c, :],
                                              M.h1s[:, xi, bass.ds((base + k) * BANK, BANK)],
                                              start=q == 0, stop=q == 2)
                    mm.then_inc(S.hidden_mm, 1)

            def back(n):
                if n % per != per - 1:
                    return
                o = n // per
                chunks = range(n - per + 1, n + 1)
                pe.wait_ge(S.hid_lo, n + 1)
                if o >= 2:
                    pe.wait_ge(S.expert_added, o - 1)
                for t in range(TB):
                    for m in chunks:
                        for q, (hi, wi) in enumerate([(0, 0), (0, 1), (1, 0)]):
                            mm = nc.tensor.matmul(R.psY[:, o % 2, t * P:(t + 1) * P],
                                                  R.hid[:, m % 4, hi, t * P:(t + 1) * P], M.ws[:, wi, 2, work[m][1], :],
                                                  start=m == chunks[0] and q == 0, stop=m == n and q == 2)
                mm.then_inc(S.expert_out, 1)

            for n in range(W + BACK):
                if n < W:
                    hidden(n)
                if n >= BACK:
                    back(n - BACK)

        @blk.scalar
        def _(act):
            for n in range(W + 1):
                if n < W:
                    act.wait_ge(S.hidden_mm, 2 * n + 1)
                    if n >= 2:
                        act.wait_ge(S.gated, n - 1)
                    nc.scalar.activation(R.sg[:, n % 2, :], R.psG[:, n % 2, :], ACT.Silu).then_inc(S.silu_done, 1)
                if routing and n == 2:
                    act.wait_ge(S.route_shifted, 1)
                    nc.scalar.activation(R.score[:], M.logit[:], ACT.Exp).then_inc(S.route_exp, 1)
                if n >= 1:
                    m = n - 1
                    act.wait_ge(S.gated, m + 1)
                    if m >= 4:
                        act.wait_ge(S.expert_out, (m - 4) // per + 1)
                    nc.scalar.copy(R.hid[:, m % 4, 0, :], R.hid32[:, m % 3, :]).then_inc(S.hid_hi, 1)

        @blk.gpsimd
        def _(pool):
            for n in range(W):
                pool.wait_ge(S.hid_hi, n + 1)
                nc.gpsimd.tensor_tensor(R.hid[:, n % 4, 1, :], R.hid32[:, n % 3, :], R.hid[:, n % 4, 0, :],
                                        ALU.subtract).then_inc(S.hid_lo, 1)

        @blk.vector
        def _(dve):
            def gated(n):
                dve.wait_ge(S.silu_done, n + 1)
                dve.wait_ge(S.hidden_mm, 2 * n + 2)
                if n >= 3:
                    dve.wait_ge(S.hid_lo, n - 2)
                nc.vector.tensor_tensor(R.hid32[:, n % 3, :], R.psU[:, n % 2, :], R.sg[:, n % 2, :],
                                        ALU.mult).then_inc(S.gated, 1)

            def add(n):
                if n % per != per - 1:
                    return
                k, c = work[n]
                o = n // per
                dve.wait_ge(S.expert_out, o + 1)
                at = (base + k) * TB
                if routing:
                    nc.vector.tensor_copy(M.moe[:, at:at + TB, :].rearrange("p t d -> p (t d)"),
                                          R.psY[:, o % 2, :]).then_inc(S.expert_added, 1)
                    return
                if o >= 1:
                    dve.wait_ge(S.expert_added, o)
                for t in range(TB):
                    acc = M.moe[:, bass.ds(at + t, 1), :].rearrange("p t d -> p (t d)")
                    last = nc.vector.scalar_tensor_tensor(
                        out=acc, in0=R.psY[:, o % 2, t * P:(t + 1) * P],
                        scalar=R.comb[:, k * TB + t, c:c + 1], in1=acc, op0=ALU.mult, op1=ALU.add)
                last.then_inc(S.expert_added, 1)

            steps = routing_steps(nc, M, S, R, dve) if routing else iter(())
            if not routing:
                nc.vector.tensor_copy(R.comb[:].rearrange("p t e -> p (t e)"),
                                      M.comb[:, bass.ds(base * TB, KB * TB), :].rearrange("p t e -> p (t e)")
                                      ).then_inc(S.comb_here, 1)
            for n in range(W + BACK):
                if n < W:
                    gated(n)
                next(steps, None)
                if not routing and n == BACK:
                    dve.wait_ge(S.comb_here, 1)
                if n >= BACK:
                    add(n - BACK)
    block_end(nc, S)


def back_block(nc, M, S, stack, sb, ps, out):
    mT = sb(stack, "mT", [P, 2, BANK], F32)
    h3 = sb(stack, "h3", [P, 2, BANK], F32)
    sg = sb(stack, "sg5", [P, 2, BANK], F32)
    h4 = sb(stack, "h4", [P, 2, BANK], F32)
    hn = sb(stack, "hn", [P, NT, D], F32)
    bn = sb(stack, "bn5", [P, NT, 6], F32)
    mv = sb(stack, "mv5", [P, NT, 2], F32)
    std = sb(stack, "std5", [P, NT], F32)
    rstd = sb(stack, "rstd5", [P, NT], F32)
    psM = ps(stack, "psM", [P, 2, BANK], F32)
    psH = ps(stack, "psH5", [P, BANK], F32)
    psG = ps(stack, "psG5", [P, 2, BANK], F32)
    psU = ps(stack, "psU5", [P, 2, BANK], F32)
    psN = ps(stack, "psN", [P, BANK], F32)
    NB = NT * P // BANK
    TB = BANK // P
    CUTS = (0, NB - 5, NB - 3, NB - 1, NB)
    out_tiles = out.rearrange("b (t p) d -> p (b t) d", p=P)
    with nc.Block() as blk:
        @blk.tensor
        def _(pe):
            for k in range(NB + 3):
                if k < NB:
                    if k >= 2:
                        pe.wait_ge(S.turned_out, k - 1)
                    for t in range(TB):
                        mm = nc.tensor.transpose(psM[:, k % 2, t * P:(t + 1) * P], M.moe[:, TB * k + t, :], M.ident[:])
                    mm.then_inc(S.moe_turned, 1)
                if 1 <= k <= NB:
                    i = k - 1
                    pe.wait_ge(S.turned_out, i + 1)
                    if i >= 1:
                        pe.wait_ge(S.lin1_out, i)
                    nc.tensor.matmul(psH[:], M.wd[:, 3, :], mT[:, i % 2, :], start=True,
                                     stop=True).then_inc(S.lin1_mm, 1)
                if 2 <= k <= NB + 1:
                    i = k - 2
                    pe.wait_ge(S.lin1_out, i + 1)
                    if i >= 2:
                        pe.wait_ge(S.h4_ready, i - 1)
                    nc.tensor.matmul(psG[:, i % 2, :], M.wd[:, 4, :], h3[:, i % 2, :],
                                     start=True, stop=True).then_inc(S.swi_mm, 1)
                    nc.tensor.matmul(psU[:, i % 2, :], M.wd[:, 5, :], h3[:, i % 2, :],
                                     start=True, stop=True).then_inc(S.swi_mm, 1)
                if k >= 3:
                    i = k - 3
                    pe.wait_ge(S.h4_ready, i + 1)
                    if i >= 1:
                        pe.wait_ge(S.norm_ready, i)
                    for t in range(TB):
                        mm = nc.tensor.transpose(psN[:, t * P:(t + 1) * P], h4[:, i % 2, t * P:(t + 1) * P], M.ident[:])
                    mm.then_inc(S.h4_turned, 1)

        @blk.scalar
        def _(act):
            def root(j):
                tiles = slice(TB * CUTS[j], TB * CUTS[j + 1])
                act.wait_ge(S.var_ready[0], j + 1)
                nc.scalar.activation(std[:, tiles], std[:, tiles], ACT.Sqrt).then_inc(S.std_ready[0], 1)

            for k in range(NB + 2):
                if k < NB:
                    act.wait_ge(S.moe_turned, k + 1)
                    if k >= 2:
                        act.wait_ge(S.lin1_mm, k - 1)
                    nc.scalar.copy(mT[:, k % 2, :], psM[:, k % 2, :]).then_inc(S.turned_out, 1)
                if 1 <= k <= NB:
                    i = k - 1
                    act.wait_ge(S.lin1_mm, i + 1)
                    if i >= 2:
                        act.wait_ge(S.swi_mm, 2 * i - 2)
                    nc.scalar.activation(h3[:, i % 2, :], psH[:], ACT.Identity,
                                         bias=M.bias[:, 3:4]).then_inc(S.lin1_out, 1)
                if k >= 2:
                    i = k - 2
                    act.wait_ge(S.swi_mm, 2 * i + 1)
                    if i >= 2:
                        act.wait_ge(S.h4_ready, i - 1)
                    nc.scalar.activation(sg[:, i % 2, :], psG[:, i % 2, :], ACT.Silu,
                                         bias=M.bias[:, 4:5]).then_inc(S.silu_done, 1)
                if k - 3 in CUTS[1:]:
                    root(CUTS.index(k - 3) - 1)
            for j, cut in enumerate(CUTS[1:]):
                if cut + 3 >= NB + 2:
                    root(j)

        @blk.vector
        def _(dve):
            def variance(j):
                for t in range(TB * CUTS[j], TB * CUTS[j + 1]):
                    last = nc.vector.bn_aggr(mv[:, t, :], bn[:, t, :])
                last.then_inc(S.stats, 1)
                dve.wait_ge(S.stats, j + 1)
                tiles = slice(TB * CUTS[j], TB * CUTS[j + 1])
                nc.vector.tensor_scalar(std[:, tiles], mv[:, tiles, 1], EPS, None, ALU.add).then_inc(S.var_ready[0], 1)

            def normal(j):
                tiles = slice(TB * CUTS[j], TB * CUTS[j + 1])
                dve.wait_ge(S.std_ready[0], j + 1)
                nc.vector.reciprocal(rstd[:, tiles], std[:, tiles]).then_inc(S.rstd_ready[0], 1)
                dve.wait_ge(S.rstd_ready[0], j + 1)
                for t in range(TB * CUTS[j], TB * CUTS[j + 1]):
                    nc.vector.tensor_scalar(hn[:, t, :], hn[:, t, :], mv[:, t, 0:1], rstd[:, t:t + 1],
                                            ALU.subtract, ALU.mult).then_inc(S.split_hi, 1)

            for k in range(NB + 1):
                if k < NB:
                    dve.wait_ge(S.silu_done, k + 1)
                    dve.wait_ge(S.swi_mm, 2 * k + 2)
                    if k >= 2:
                        dve.wait_ge(S.h4_turned, k - 1)
                    nc.vector.scalar_tensor_tensor(out=h4[:, k % 2, :], in0=psU[:, k % 2, :],
                                                   scalar=M.bias[:, 5:6], in1=sg[:, k % 2, :],
                                                   op0=ALU.add, op1=ALU.mult).then_inc(S.h4_ready, 1)
                if k >= 1:
                    i = k - 1
                    dve.wait_ge(S.h4_turned, i + 1)
                    for t in range(TB):
                        nc.vector.bn_stats(bn[:, TB * i + t, :], psN[:, t * P:(t + 1) * P])
                    nc.vector.tensor_copy(hn[:, TB * i:TB * i + TB, :].rearrange("p t d -> p (t d)"),
                                          psN[:]).then_inc(S.norm_ready, 1)
                if k in CUTS[1:]:
                    dve.wait_ge(S.norm_ready, k)
                    variance(CUTS.index(k) - 1)
                if k - 2 in CUTS[1:]:
                    normal(CUTS.index(k - 2) - 1)
            for j, cut in enumerate(CUTS[1:]):
                if cut + 2 > NB:
                    normal(j)

        @blk.gpsimd
        def _(pool):
            for t in range(NT):
                pool.wait_ge(S.split_hi, t + 1)
                nc.gpsimd.tensor_tensor(M.x1[:, t, :], M.x1[:, t, :], hn[:, t, :], ALU.add).then_inc(S.split_lo, 1)

        @blk.sync
        def _(sp):
            for k in range(NB):
                sp.wait_ge(S.split_lo, TB * (k + 1))
                sp.dma_start(out_tiles[:, TB * k:TB * k + TB, :], M.x1[:, TB * k:TB * k + TB, :]).then_inc(S.stored, 16)
            sp.wait_ge(S.stored, 16 * NB)


def phase_ffn(nc, I, M, S, sb, ps, out):
    with ExitStack() as stack:
        M.x1 = sb(stack, "x1", [P, NT, D], F32)
        M.wd = sb(stack, "wd", [P, 6, D], F32)
        M.bias = sb(stack, "bias", [P, 6], F32)
        M.gate = sb(stack, "gate", [P, E], F32)
        M.ws = sb(stack, "ws", [P, 2, 3, E + NC, H], F16)
        M.h1s = sb(stack, "h1s", [P, 2, NT * P], F16)
        M.logit = sb(stack, "logit", [P, NT, E], F32)
        M.comb = sb(stack, "comb", [P, NT, E], F32)
        M.tri = sb(stack, "tri", [P, E, E], F32)
        with ExitStack() as early:
            M.h0T = sb(early, "h0T", [P, NT * P], F32)
            M.h1T = sb(early, "h1T", [P, NT * P], F32)
            M.we = sb(early, "we", [P, 3, E + NC, H], F32)
            with ExitStack() as temps:
                norm_block(nc, I, M, S, temps, sb, ps)
            with ExitStack() as temps:
                front_block(nc, M, S, temps, sb, ps)
        M.moe = sb(stack, "moe", [P, NT, D], F32)
        with ExitStack() as temps:
            R = Box()
            R.sg = sb(temps, "sg4", [P, 2, BANK], F32)
            R.hid32 = sb(temps, "hid32", [P, 3, BANK], F32)
            R.hid = sb(temps, "hid", [P, 4, 2, BANK], F16)
            R.comb = sb(temps, "comb4", [P, KB * BANK // P, E], F32)
            R.score = sb(temps, "score", [P, NT, E], F32)
            R.small = sb(temps, "small", [P, 4, NT, 1], F32)
            R.more = sb(temps, "more", [P, NT, E, E], F32)
            R.same = sb(temps, "same", [P, NT, E, E], F32)
            R.rank = sb(temps, "rank", [P, NT, E], F32)
            R.psG = ps(temps, "psG4", [P, 2, BANK], F32)
            R.psU = ps(temps, "psU4", [P, 2, BANK], F32)
            R.psY = ps(temps, "psY", [P, 2, BANK], F32)
            blocks = NT * P // BANK
            expert_block(nc, M, S, R, 0, [(k, E + c) for k in range(blocks) for c in range(NC)], NC, True)
            with nc.Fori(0, blocks // KB) as i:
                expert_block(nc, M, S, R, i * KB, [(k, c) for k in range(KB) for c in range(E)], 1, False)
        with ExitStack() as temps:
            back_block(nc, M, S, temps, sb, ps, out)


def build(nc, I, out):
    with ExitStack() as top:
        numbers = []

        def sem(name):
            x = top.enter_context(nc.semaphore(name))
            numbers.append(x.num)
            return x

        def sb(stack, name, shape, dt):
            return stack.enter_context(nc.sbuf_tensor(name, shape, dt))

        def ps(stack, name, shape, dt):
            return stack.enter_context(nc.psum_tensor(name, shape, dt))

        S = Box()
        S.scores_ready = sem("scores_ready")
        S.exp_done = sem("exp_done")
        S.lo_dve = sem("lo_dve")
        S.lo_pool = sem("lo_pool")
        S.weighted_done = sem("weighted_done")
        S.out_lo = sem("out_lo")
        S.out_added = sem("out_added")
        S.out_scaled = sem("out_scaled")
        S.aux_ready = sem("aux_ready")
        S.aux_free = [sem(f"aux_free{k}") for k in range(NAUX)]
        S.rope_sum = sem("rope_sum")
        S.rope_hi = sem("rope_hi")
        S.rope_lo = sem("rope_lo")
        S.v_hi = sem("v_hi")
        S.row_max = sem("row_max")
        S.k_out = sem("k_out")
        S.q_out = sem("q_out")
        S.near_in = [sem(f"near_in{i}") for i in range(2)]
        S.far_in = sem("far_in")
        S.row_max_in = sem("row_max_in")
        S.xq_in = sem("xq_in")
        S.xv_in = sem("xv_in")
        S.x_load = [sem(f"x_load{b}") for b in range(B)]
        S.w_in = sem("w_in")
        S.x_stored = [sem(f"x_stored{i}") for i in range(2)]
        S.w_load = [sem(f"w_load{k}") for k in range(3)]
        S.w_hi = sem("w_hi")
        S.c_in = sem("c_in")
        S.consts = sem("consts")
        S.stats = sem("stats")
        S.var_ready = [sem(f"var_ready{i}") for i in range(2)]
        S.std_ready = [sem(f"std_ready{i}") for i in range(2)]
        S.rstd_ready = [sem(f"rstd_ready{i}") for i in range(2)]
        S.normal_ready = [sem(f"normal_ready{i}") for i in range(2)]
        S.x1_ready = sem("x1_ready")
        S.lin0_in = sem("lin0_in")
        S.lin0_mm = sem("lin0_mm")
        S.lin0_out = sem("lin0_out")
        S.swi_mm = sem("swi_mm")
        S.silu_done = sem("silu_done")
        S.h1_ready = sem("h1_ready")
        S.h1_hi = sem("h1_hi")
        S.logits_mm = sem("logits_mm")
        S.hidden_mm = sem("hidden_mm")
        S.gated = sem("gated")
        S.hid_hi = sem("hid_hi")
        S.hid_lo = sem("hid_lo")
        S.expert_out = sem("expert_out")
        S.expert_added = sem("expert_added")
        S.comb_here = sem("comb_here")
        S.route_step = sem("route_step")
        S.route_shifted = sem("route_shifted")
        S.route_exp = sem("route_exp")
        S.norm_ready = sem("norm_ready")
        S.turned = sem("turned")
        S.turned_out = sem("turned_out")
        S.split_hi = sem("split_hi")
        S.split_lo = sem("split_lo")
        S.moe_turned = sem("moe_turned")
        S.lin1_mm = sem("lin1_mm")
        S.lin1_out = sem("lin1_out")
        S.h4_ready = sem("h4_ready")
        S.h4_turned = sem("h4_turned")
        S.stored = sem("stored")
        S.first, S.last = min(numbers), max(numbers)
        M = Box()
        M.ident = sb(top, "ident", [P, P], F32)
        M.bn = sb(top, "bn_xy", [P, NT, 6], F32)
        M.mv = sb(top, "mv_xy", [P, NT, 2], F32)
        M.std = sb(top, "std_xy", [P, NT], F32)
        M.rstd = sb(top, "rstd_xy", [P, NT], F32)
        M.y = sb(top, "y", [P, TT + NT, D], F32)
        M.x_way = nc.dram_tensor("x_way", (P, 2, NT * P), F16, kind="Internal").ap()
        M.k_way = nc.dram_tensor("k_way", (4, HALF, GH, T), F16, kind="Internal").ap()
        M.q_way = nc.dram_tensor("q_way", (4, HALF, GH, T), F16, kind="Internal").ap()
        phase_attention(nc, I, M, S, sb, ps)
        phase_ffn(nc, I, M, S, sb, ps, out)


def rotary_table():
    inv = np.float32(1.0) / np.float32(10000.0) ** (np.arange(0, HD, 2, dtype=np.float32) / np.float32(HD))
    angle = np.outer(np.arange(T, dtype=np.float32), inv.astype(np.float32)).astype(np.float32)
    cos, sin = np.cos(angle).astype(np.float32), np.sin(angle).astype(np.float32)
    return (np.ascontiguousarray(np.tile(cos.T, (GH, 1))), np.ascontiguousarray(np.tile(sin.T, (GH, 1))))


def by_halves(w):
    w = w.reshape(GROUPS, GH, 2, HALF, D).transpose(4, 0, 2, 1, 3)
    return np.ascontiguousarray(w.reshape(D, HEADS * HD))


def kernel(**inputs):
    import concourse.bacc as bacc
    from concourse.bass_utils import run_bass_kernel_spmd

    a = {name.removeprefix("L0_ffn_").removeprefix("L0_attn_"): np.asarray(v) for name, v in inputs.items()
         if name != "L0_attn_x"}
    laid = {name: np.ascontiguousarray(v) for name, v in a.items() if name not in ("wq", "wk", "wv", "wo", "gate_w")}
    laid["x"] = np.ascontiguousarray(np.asarray(inputs["L0_attn_x"]))
    laid["wq"], laid["wk"] = by_halves(a["wq"]), by_halves(a["wk"])
    laid["wv"] = np.ascontiguousarray(a["wv"].T)
    laid["wo"] = np.ascontiguousarray(a["wo"].T.reshape(HEADS * HD // P, P, D).transpose(1, 0, 2))
    laid["gate_w"] = np.ascontiguousarray(a["gate_w"].T)
    laid["cos"], laid["sin"] = rotary_table()

    nc = bacc.Bacc("TRN2", target_bir_lowering=False, num_devices=1)
    I = {name: nc.dram_tensor(f"in_{name}", v.shape, mybir.dt.from_np(v.dtype), kind="ExternalInput").ap()
         for name, v in laid.items()}
    out = nc.dram_tensor("out", (B, T, D), F32, kind="ExternalOutput").ap()
    build(nc, I, out)
    r = run_bass_kernel_spmd(nc, [{f"in_{name}": v for name, v in laid.items()}], core_ids=[0])
    return r.results[0]["out"]
```
